# Optimizing a Trainium2 kernel written in Bass

```python
import numpy as np
import jax
import jax.numpy as jnp

def _softmax(x, axis=-1):
    return jax.nn.softmax(x, axis=axis)

def _gelu(x):
    return jax.nn.gelu(x, approximate=True)

def _silu(x):
    return jax.nn.silu(x)

def _sigmoid(x):
    return jax.nn.sigmoid(x)

def _layernorm(x, axis=-1, eps=1e-05):
    m = jnp.mean(x, axis=axis, keepdims=True)
    v = jnp.var(x, axis=axis, keepdims=True)
    return (x - m) / jnp.sqrt(v + eps)

def _scatter_add(tgt, idx, src, axis=0):
    return tgt.at[idx].add(src)

def _segment_sum(src, seg, n):
    return jax.ops.segment_sum(src, seg, n)
kernel_name = 'mk_gnn_resnorm_d4_gnn_r64_6b2bac'

def setup_inputs(seed: int=0):
    np.random.seed(seed)
    _w = jnp.asarray

    def _rec_inputs():
        import jax
        import jax.numpy as jnp
        _gk = jax.random.key(seed)
        x = -0.0001538 + 1 * jax.random.normal(jax.random.fold_in(_gk, 1), (128, 768), jnp.float32)
        src = jax.random.randint(jax.random.fold_in(_gk, 2), (2048,), 0, 128, jnp.int32)
        dst = jax.random.randint(jax.random.fold_in(_gk, 3), (2048,), 0, 128, jnp.int32)
        _o = jnp.argsort(dst, stable=True)
        src = src[_o]
        dst = dst[_o]
        edge_attr_32 = 0.000376506 + 0.999991 * jax.random.normal(jax.random.fold_in(_gk, 11), (2048, 32), jnp.float32)
        edge_type_3 = jax.random.randint(jax.random.fold_in(_gk, 13), (2048,), 0, 3, jnp.int32)
        node_type_6 = jax.random.randint(jax.random.fold_in(_gk, 14), (128,), 0, 6, jnp.int32)
        return (x, src, dst, edge_attr_32, edge_type_3, node_type_6)
    x, src, dst, edge_attr_32, edge_type_3, node_type_6 = _rec_inputs()

    def _L0_gnn_setup():
        import jax, jax.numpy as jnp
        import numpy as np
        N_NODES = 128
        N_EDGES = 512
        D = 768
        H1 = 8
        NEG_SLOPE = 0.2

        def gat_conv(x, src, dst, W, a_src, a_dst, b, heads, out_ch):
            n = x.shape[0]
            h = (x @ W).reshape(n, heads, out_ch)
            alpha_src = jnp.einsum('nhc,hc->nh', h, a_src)
            alpha_dst = jnp.einsum('nhc,hc->nh', h, a_dst)
            e = jax.nn.leaky_relu(alpha_src[src] + alpha_dst[dst], NEG_SLOPE)
            m = jax.ops.segment_max(e, dst, num_segments=n)
            m = jnp.where(jnp.isfinite(m), m, 0.0)
            p = jnp.exp(e - m[dst])
            denom = jax.ops.segment_sum(p, dst, num_segments=n)
            alpha = p / denom[dst]
            msg = h[src] * alpha[:, :, None]
            out = jax.ops.segment_sum(msg, dst, num_segments=n)
            return out.reshape(n, heads * out_ch) + b
        key = jax.random.key(seed)
        ks = jax.random.split(key, 10)
        s = 0.02
        x = jax.random.normal(ks[0], (N_NODES, D), dtype=jnp.float32)
        edge_index = jax.random.randint(ks[1], (2, N_EDGES), 0, N_NODES, dtype=jnp.int64)
        W1 = jax.random.normal(ks[2], (D, H1 * D), dtype=jnp.float32) * s
        a_src1 = jax.random.normal(ks[3], (H1, D), dtype=jnp.float32) * s
        a_dst1 = jax.random.normal(ks[4], (H1, D), dtype=jnp.float32) * s
        b1 = jnp.zeros((H1 * D,), dtype=jnp.float32)
        W2 = jax.random.normal(ks[5], (H1 * D, D), dtype=jnp.float32) * s
        a_src2 = jax.random.normal(ks[6], (1, D), dtype=jnp.float32) * s
        a_dst2 = jax.random.normal(ks[7], (1, D), dtype=jnp.float32) * s
        b2 = jnp.zeros((D,), dtype=jnp.float32)
        return {'x': x, 'edge_index': edge_index, 'W1': W1, 'a_src1': a_src1, 'a_dst1': a_dst1, 'b1': b1, 'W2': W2, 'a_src2': a_src2, 'a_dst2': a_dst2, 'b2': b2}
    _L0_gnn_all = _L0_gnn_setup()
    _L0_gnn_in = {k: v for k, v in _L0_gnn_all.items() if k in ('W1', 'a_src1', 'a_dst1', 'b1', 'W2', 'a_src2', 'a_dst2', 'b2')}
    del _L0_gnn_all

    def _L1_gnn_setup():
        import jax, jax.numpy as jnp
        import numpy as np
        N, E, D, T, EA = (50000, 2048, 768, 6, 32)
        H4 = D // 4
        EPS = 1e-05
        key = jax.random.key(seed)
        ks = jax.random.split(key, 24)

        def init(k, shape, fan_in):
            return (jax.random.normal(k, shape, jnp.float32) / np.sqrt(fan_in)).astype(jnp.float32)
        inp = {'x': jax.random.normal(ks[0], (N, D), jnp.float32), 'edge_index': jax.random.randint(ks[1], (2, E), 0, N, jnp.int64), 'edge_attr': jax.random.normal(ks[2], (E, EA), jnp.float32), 'node_types': jax.random.randint(ks[3], (N,), 0, T, jnp.int64), 'W_type': init(ks[4], (T, D, D), D), 'b_type': jnp.zeros((T, D), jnp.float32), 'msg_W1': init(ks[5], (2 * D, D), 2 * D), 'msg_b1': jnp.zeros((D,), jnp.float32), 'msg_W2': init(ks[6], (D, D), D), 'msg_b2': jnp.zeros((D,), jnp.float32), 'edge_W1': init(ks[7], (EA, H4), EA), 'edge_b1': jnp.zeros((H4,), jnp.float32), 'edge_W2': init(ks[8], (H4, 1), H4), 'edge_b2': jnp.zeros((1,), jnp.float32), 'agg_W1': init(ks[9], (D, D), D), 'agg_b1': jnp.zeros((D,), jnp.float32), 'agg_W2': init(ks[10], (D, D), D), 'agg_b2': jnp.zeros((D,), jnp.float32), 'out_W': init(ks[11], (D, D), D), 'out_b': jnp.zeros((D,), jnp.float32), 'ln_g': jnp.ones((D,), jnp.float32), 'ln_b': jnp.zeros((D,), jnp.float32)}
        return inp
    _L1_gnn_all = _L1_gnn_setup()
    _L1_gnn_in = {k: v for k, v in _L1_gnn_all.items() if k in ('W_type', 'b_type', 'msg_W1', 'msg_b1', 'msg_W2', 'msg_b2', 'edge_W1', 'edge_b1', 'edge_W2', 'edge_b2', 'agg_W1', 'agg_b1', 'agg_W2', 'agg_b2', 'out_W', 'out_b', 'ln_g', 'ln_b')}
    del _L1_gnn_all

    def _L2_gnn_setup():
        import jax, jax.numpy as jnp
        import numpy as np
        N_NODES = 10000
        N_EDGES = 1250
        IN_DIM, HID, OUT_DIM, HEADS = (768, 512, 768, 4)
        NEG_SLOPE = 0.2

        def _gat_layer(x, src, dst, W, a_src, a_dst, b, heads, d_out, concat):
            N = x.shape[0]
            h = (x @ W).reshape(N, heads, d_out)
            as_n = jnp.einsum('nhd,hd->nh', h, a_src)
            ad_n = jnp.einsum('nhd,hd->nh', h, a_dst)
            e = jax.nn.leaky_relu(as_n[src] + ad_n[dst], NEG_SLOPE)
            e_max = jax.lax.stop_gradient(jax.ops.segment_max(e, dst, num_segments=N))
            ex = jnp.exp(e - e_max[dst])
            denom = jax.ops.segment_sum(ex, dst, num_segments=N)
            alpha = ex / (denom[dst] + 1e-16)
            msg = alpha[:, :, None] * h[src]
            out = jax.ops.segment_sum(msg, dst, num_segments=N)
            out = out.reshape(N, heads * d_out) if concat else out.mean(axis=1)
            return out + b
        key = jax.random.key(seed)
        ks = jax.random.split(key, 10)
        g = 0.05
        return {'x': jax.random.normal(ks[0], (N_NODES, IN_DIM), jnp.float32), 'edge_index': jax.random.randint(ks[1], (2, N_EDGES), 0, N_NODES, jnp.int64), 'W1': jax.random.normal(ks[2], (IN_DIM, HEADS * HID), jnp.float32) * g, 'a1_src': jax.random.normal(ks[3], (HEADS, HID), jnp.float32) * g, 'a1_dst': jax.random.normal(ks[4], (HEADS, HID), jnp.float32) * g, 'b1': jnp.zeros((HEADS * HID,), jnp.float32), 'W2': jax.random.normal(ks[5], (HEADS * HID, OUT_DIM), jnp.float32) * g, 'a2_src': jax.random.normal(ks[6], (1, OUT_DIM), jnp.float32) * g, 'a2_dst': jax.random.normal(ks[7], (1, OUT_DIM), jnp.float32) * g, 'b2': jnp.zeros((OUT_DIM,), jnp.float32)}
    _L2_gnn_all = _L2_gnn_setup()
    _L2_gnn_in = {k: v for k, v in _L2_gnn_all.items() if k in ('W1', 'a1_src', 'a1_dst', 'b1', 'W2', 'a2_src', 'a2_dst', 'b2')}
    del _L2_gnn_all

    def _L3_gnn_setup():
        import jax, jax.numpy as jnp
        import numpy as np
        NEG_SLOPE = 0.2
        EPS = 1e-16
        N_NODES = 512
        N_EDGES = 2500
        DIM = 768
        HEADS1 = 4
        OUT1 = DIM // HEADS1
        HEADS2 = 1
        OUT2 = DIM
        N_REL = 3

        def rgat_conv(x, W, q, k, b, src, dst, etype, heads, out_ch, n_nodes):
            xr = jnp.einsum('nd,rdf->rnf', x, W)
            oi = xr[etype, dst]
            oj = xr[etype, src]
            qi = oi @ q
            kj = oj @ k
            alpha = jax.nn.leaky_relu(qi + kj, NEG_SLOPE)
            m = jax.ops.segment_max(alpha, dst, num_segments=n_nodes)
            e = jnp.exp(alpha - m[dst])
            z = jax.ops.segment_sum(e, dst, num_segments=n_nodes)
            a = e / (z[dst] + EPS)
            msg = (a[:, :, None] * oj.reshape(-1, heads, out_ch)).reshape(-1, heads * out_ch)
            out = jax.ops.segment_sum(msg, dst, num_segments=n_nodes)
            return out + b
        key = jax.random.key(seed)
        ks = jax.random.split(key, 12)
        s = 0.02
        return {'x': jax.random.normal(ks[0], (N_NODES, DIM), dtype=jnp.float32), 'edge_index': jax.random.randint(ks[1], (2, N_EDGES), 0, N_NODES, dtype=jnp.int64), 'edge_type': jax.random.randint(ks[2], (N_EDGES,), 0, N_REL, dtype=jnp.int64), 'W1': jax.random.normal(ks[3], (N_REL, DIM, HEADS1 * OUT1), dtype=jnp.float32) * s, 'q1': jax.random.normal(ks[4], (HEADS1 * OUT1, HEADS1), dtype=jnp.float32) * s, 'k1': jax.random.normal(ks[5], (HEADS1 * OUT1, HEADS1), dtype=jnp.float32) * s, 'b1': jnp.zeros((HEADS1 * OUT1,), dtype=jnp.float32), 'W2': jax.random.normal(ks[6], (N_REL, DIM, HEADS2 * OUT2), dtype=jnp.float32) * s, 'q2': jax.random.normal(ks[7], (HEADS2 * OUT2, HEADS2), dtype=jnp.float32) * s, 'k2': jax.random.normal(ks[8], (HEADS2 * OUT2, HEADS2), dtype=jnp.float32) * s, 'b2': jnp.zeros((HEADS2 * OUT2,), dtype=jnp.float32)}
    _L3_gnn_all = _L3_gnn_setup()
    _L3_gnn_in = {k: v for k, v in _L3_gnn_all.items() if k in ('W1', 'q1', 'k1', 'b1', 'W2', 'q2', 'k2', 'b2')}
    del _L3_gnn_all
    return {'x': x, 'src': src, 'dst': dst, 'edge_attr_32': edge_attr_32, 'edge_type_3': edge_type_3, 'node_type_6': node_type_6, 'L0_gnn_W1': _L0_gnn_in['W1'], 'L0_gnn_a_src1': _L0_gnn_in['a_src1'], 'L0_gnn_a_dst1': _L0_gnn_in['a_dst1'], 'L0_gnn_b1': _L0_gnn_in['b1'], 'L0_gnn_W2': _L0_gnn_in['W2'], 'L0_gnn_a_src2': _L0_gnn_in['a_src2'], 'L0_gnn_a_dst2': _L0_gnn_in['a_dst2'], 'L0_gnn_b2': _L0_gnn_in['b2'], 'L1_gnn_W_type': _L1_gnn_in['W_type'], 'L1_gnn_b_type': _L1_gnn_in['b_type'], 'L1_gnn_msg_W1': _L1_gnn_in['msg_W1'], 'L1_gnn_msg_b1': _L1_gnn_in['msg_b1'], 'L1_gnn_msg_W2': _L1_gnn_in['msg_W2'], 'L1_gnn_msg_b2': _L1_gnn_in['msg_b2'], 'L1_gnn_edge_W1': _L1_gnn_in['edge_W1'], 'L1_gnn_edge_b1': _L1_gnn_in['edge_b1'], 'L1_gnn_edge_W2': _L1_gnn_in['edge_W2'], 'L1_gnn_edge_b2': _L1_gnn_in['edge_b2'], 'L1_gnn_agg_W1': _L1_gnn_in['agg_W1'], 'L1_gnn_agg_b1': _L1_gnn_in['agg_b1'], 'L1_gnn_agg_W2': _L1_gnn_in['agg_W2'], 'L1_gnn_agg_b2': _L1_gnn_in['agg_b2'], 'L1_gnn_out_W': _L1_gnn_in['out_W'], 'L1_gnn_out_b': _L1_gnn_in['out_b'], 'L1_gnn_ln_g': _L1_gnn_in['ln_g'], 'L1_gnn_ln_b': _L1_gnn_in['ln_b'], 'L2_gnn_W1': _L2_gnn_in['W1'], 'L2_gnn_a1_src': _L2_gnn_in['a1_src'], 'L2_gnn_a1_dst': _L2_gnn_in['a1_dst'], 'L2_gnn_b1': _L2_gnn_in['b1'], 'L2_gnn_W2': _L2_gnn_in['W2'], 'L2_gnn_a2_src': _L2_gnn_in['a2_src'], 'L2_gnn_a2_dst': _L2_gnn_in['a2_dst'], 'L2_gnn_b2': _L2_gnn_in['b2'], 'L3_gnn_W1': _L3_gnn_in['W1'], 'L3_gnn_q1': _L3_gnn_in['q1'], 'L3_gnn_k1': _L3_gnn_in['k1'], 'L3_gnn_b1': _L3_gnn_in['b1'], 'L3_gnn_W2': _L3_gnn_in['W2'], 'L3_gnn_q2': _L3_gnn_in['q2'], 'L3_gnn_k2': _L3_gnn_in['k2'], 'L3_gnn_b2': _L3_gnn_in['b2']}

def reference(x, src, dst, edge_attr_32, edge_type_3, node_type_6, L0_gnn_W1, L0_gnn_a_src1, L0_gnn_a_dst1, L0_gnn_b1, L0_gnn_W2, L0_gnn_a_src2, L0_gnn_a_dst2, L0_gnn_b2, L1_gnn_W_type, L1_gnn_b_type, L1_gnn_msg_W1, L1_gnn_msg_b1, L1_gnn_msg_W2, L1_gnn_msg_b2, L1_gnn_edge_W1, L1_gnn_edge_b1, L1_gnn_edge_W2, L1_gnn_edge_b2, L1_gnn_agg_W1, L1_gnn_agg_b1, L1_gnn_agg_W2, L1_gnn_agg_b2, L1_gnn_out_W, L1_gnn_out_b, L1_gnn_ln_g, L1_gnn_ln_b, L2_gnn_W1, L2_gnn_a1_src, L2_gnn_a1_dst, L2_gnn_b1, L2_gnn_W2, L2_gnn_a2_src, L2_gnn_a2_dst, L2_gnn_b2, L3_gnn_W1, L3_gnn_q1, L3_gnn_k1, L3_gnn_b1, L3_gnn_W2, L3_gnn_q2, L3_gnn_k2, L3_gnn_b2):
    import jax
    import jax.numpy as jnp

    def _L0_gnn_ref(x, edge_index, W1, a_src1, a_dst1, b1, W2, a_src2, a_dst2, b2):
        import jax, jax.numpy as jnp
        import numpy as np
        N_NODES = 128
        N_EDGES = 512
        D = 768
        H1 = 8
        NEG_SLOPE = 0.2

        def gat_conv(x, src, dst, W, a_src, a_dst, b, heads, out_ch):
            n = x.shape[0]
            h = (x @ W).reshape(n, heads, out_ch)
            alpha_src = jnp.einsum('nhc,hc->nh', h, a_src)
            alpha_dst = jnp.einsum('nhc,hc->nh', h, a_dst)
            e = jax.nn.leaky_relu(alpha_src[src] + alpha_dst[dst], NEG_SLOPE)
            m = jax.ops.segment_max(e, dst, num_segments=n)
            m = jnp.where(jnp.isfinite(m), m, 0.0)
            p = jnp.exp(e - m[dst])
            denom = jax.ops.segment_sum(p, dst, num_segments=n)
            alpha = p / denom[dst]
            msg = h[src] * alpha[:, :, None]
            out = jax.ops.segment_sum(msg, dst, num_segments=n)
            return out.reshape(n, heads * out_ch) + b
        n = x.shape[0]
        loops = jnp.arange(n, dtype=edge_index.dtype)
        src = jnp.concatenate([edge_index[0], loops])
        dst = jnp.concatenate([edge_index[1], loops])
        h = gat_conv(x, src, dst, W1, a_src1, a_dst1, b1, H1, D)
        h = jax.nn.elu(h)
        out = gat_conv(h, src, dst, W2, a_src2, a_dst2, b2, 1, D)
        return out

    def _L1_gnn_ref(x, edge_index, edge_attr, node_types, W_type, b_type, msg_W1, msg_b1, msg_W2, msg_b2, edge_W1, edge_b1, edge_W2, edge_b2, agg_W1, agg_b1, agg_W2, agg_b2, out_W, out_b, ln_g, ln_b):
        import jax, jax.numpy as jnp
        import numpy as np
        N, E, D, T, EA = (50000, 2048, 768, 6, 32)
        H4 = D // 4
        EPS = 1e-05
        n = x.shape[0]
        all_h = jnp.einsum('ni,tio->tno', x, W_type)
        h = jnp.take_along_axis(all_h, node_types[None, :, None], axis=0)[0]
        h = h + b_type[node_types]
        row, col = (edge_index[0], edge_index[1])
        m_in = jnp.concatenate([h[row], h[col]], axis=1)
        m = jax.nn.relu(m_in @ msg_W1 + msg_b1) @ msg_W2 + msg_b2
        ew = jax.nn.sigmoid(jax.nn.relu(edge_attr @ edge_W1 + edge_b1) @ edge_W2 + edge_b2)
        m = m * ew
        agg = jax.ops.segment_sum(m, col, num_segments=n)
        agg = jax.nn.relu(agg @ agg_W1 + agg_b1) @ agg_W2 + agg_b2
        h = h + agg
        h = h @ out_W + out_b
        h = h + x
        mu = jnp.mean(h, axis=-1, keepdims=True)
        var = jnp.mean(jnp.square(h - mu), axis=-1, keepdims=True)
        h = (h - mu) * jax.lax.rsqrt(var + EPS) * ln_g + ln_b
        return h

    def _L2_gnn_ref(x, edge_index, W1, a1_src, a1_dst, b1, W2, a2_src, a2_dst, b2):
        import jax, jax.numpy as jnp
        import numpy as np
        N_NODES = 10000
        N_EDGES = 1250
        IN_DIM, HID, OUT_DIM, HEADS = (768, 512, 768, 4)
        NEG_SLOPE = 0.2

        def _gat_layer(x, src, dst, W, a_src, a_dst, b, heads, d_out, concat):
            N = x.shape[0]
            h = (x @ W).reshape(N, heads, d_out)
            as_n = jnp.einsum('nhd,hd->nh', h, a_src)
            ad_n = jnp.einsum('nhd,hd->nh', h, a_dst)
            e = jax.nn.leaky_relu(as_n[src] + ad_n[dst], NEG_SLOPE)
            e_max = jax.lax.stop_gradient(jax.ops.segment_max(e, dst, num_segments=N))
            ex = jnp.exp(e - e_max[dst])
            denom = jax.ops.segment_sum(ex, dst, num_segments=N)
            alpha = ex / (denom[dst] + 1e-16)
            msg = alpha[:, :, None] * h[src]
            out = jax.ops.segment_sum(msg, dst, num_segments=N)
            out = out.reshape(N, heads * d_out) if concat else out.mean(axis=1)
            return out + b
        N = x.shape[0]
        loops = jnp.arange(N, dtype=edge_index.dtype)
        src = jnp.concatenate([edge_index[0], loops])
        dst = jnp.concatenate([edge_index[1], loops])
        h = _gat_layer(x, src, dst, W1, a1_src, a1_dst, b1, HEADS, HID, True)
        h = jax.nn.elu(h)
        out = _gat_layer(h, src, dst, W2, a2_src, a2_dst, b2, 1, OUT_DIM, False)
        return out

    def _L3_gnn_ref(x, edge_index, edge_type, W1, q1, k1, b1, W2, q2, k2, b2):
        import jax, jax.numpy as jnp
        import numpy as np
        NEG_SLOPE = 0.2
        EPS = 1e-16
        N_NODES = 512
        N_EDGES = 2500
        DIM = 768
        HEADS1 = 4
        OUT1 = DIM // HEADS1
        HEADS2 = 1
        OUT2 = DIM
        N_REL = 3

        def rgat_conv(x, W, q, k, b, src, dst, etype, heads, out_ch, n_nodes):
            xr = jnp.einsum('nd,rdf->rnf', x, W)
            oi = xr[etype, dst]
            oj = xr[etype, src]
            qi = oi @ q
            kj = oj @ k
            alpha = jax.nn.leaky_relu(qi + kj, NEG_SLOPE)
            m = jax.ops.segment_max(alpha, dst, num_segments=n_nodes)
            e = jnp.exp(alpha - m[dst])
            z = jax.ops.segment_sum(e, dst, num_segments=n_nodes)
            a = e / (z[dst] + EPS)
            msg = (a[:, :, None] * oj.reshape(-1, heads, out_ch)).reshape(-1, heads * out_ch)
            out = jax.ops.segment_sum(msg, dst, num_segments=n_nodes)
            return out + b
        src, dst = (edge_index[0], edge_index[1])
        n = x.shape[0]
        h = rgat_conv(x, W1, q1, k1, b1, src, dst, edge_type, HEADS1, OUT1, n)
        h = jax.nn.elu(h)
        out = rgat_conv(h, W2, q2, k2, b2, src, dst, edge_type, HEADS2, OUT2, n)
        return out
    edge_index = jnp.stack([src, dst])
    x = _layernorm(x + _L0_gnn_ref(x, edge_index, L0_gnn_W1, L0_gnn_a_src1, L0_gnn_a_dst1, L0_gnn_b1, L0_gnn_W2, L0_gnn_a_src2, L0_gnn_a_dst2, L0_gnn_b2), axis=-1)
    x = _layernorm(x + _L1_gnn_ref(x, edge_index, edge_attr_32, node_type_6, L1_gnn_W_type, L1_gnn_b_type, L1_gnn_msg_W1, L1_gnn_msg_b1, L1_gnn_msg_W2, L1_gnn_msg_b2, L1_gnn_edge_W1, L1_gnn_edge_b1, L1_gnn_edge_W2, L1_gnn_edge_b2, L1_gnn_agg_W1, L1_gnn_agg_b1, L1_gnn_agg_W2, L1_gnn_agg_b2, L1_gnn_out_W, L1_gnn_out_b, L1_gnn_ln_g, L1_gnn_ln_b), axis=-1)
    x = _layernorm(x + _L2_gnn_ref(x, edge_index, L2_gnn_W1, L2_gnn_a1_src, L2_gnn_a1_dst, L2_gnn_b1, L2_gnn_W2, L2_gnn_a2_src, L2_gnn_a2_dst, L2_gnn_b2), axis=-1)
    x = _layernorm(x + _L3_gnn_ref(x, edge_index, edge_type_3, L3_gnn_W1, L3_gnn_q1, L3_gnn_k1, L3_gnn_b1, L3_gnn_W2, L3_gnn_q2, L3_gnn_k2, L3_gnn_b2), axis=-1)
    return x

_drawn_inputs = setup_inputs


def setup_inputs(seed=0):
    import zlib

    import numpy as np

    out = dict(_drawn_inputs(seed))
    spreads = {'L0_gnn_b1': (0.0, 0.1),
     'L0_gnn_b2': (0.0, 0.1),
     'L1_gnn_b_type': (0.0, 0.1),
     'L1_gnn_msg_b1': (0.0, 0.1),
     'L1_gnn_msg_b2': (0.0, 0.1),
     'L1_gnn_edge_b1': (0.0, 2.0),
     'L1_gnn_agg_b1': (0.0, 0.44),
     'L1_gnn_agg_b2': (0.0, 0.284),
     'L1_gnn_out_b': (0.0, 0.285),
     'L1_gnn_ln_g': (1.0, 0.2),
     'L1_gnn_ln_b': (0.0, 0.1),
     'L2_gnn_b1': (0.0, 0.1),
     'L2_gnn_b2': (0.0, 0.1),
     'L3_gnn_b1': (0.0, 0.267),
     'L3_gnn_b2': (0.0, 0.1)}
    factors = {'L0_gnn_a_dst1': 58.37,
     'L0_gnn_a_src2': 8.0,
     'L0_gnn_a_dst2': 30.873,
     'L3_gnn_q1': 4.153,
     'L3_gnn_k1': 4.46,
     'L3_gnn_q2': 27.032,
     'L3_gnn_k2': 8.0,
     'edge_attr_32': 2.695,
     'L1_gnn_edge_W1': 2.931}
    for name, (base, spread) in spreads.items():
        noise = np.random.default_rng([zlib.crc32(name.encode()), seed]).standard_normal(out[name].shape)
        drawn = base * np.exp(spread * noise) if base else spread * noise
        out[name] = jnp.asarray(drawn.astype(out[name].dtype))
    for name, factor in factors.items():
        out[name] = (out[name] * factor).astype(out[name].dtype)
    return out
```

```python
from contextlib import ExitStack

import concourse.bass as bass
from concourse import mybir

F32 = mybir.dt.float32
F32R = mybir.dt.float32r
BF16 = mybir.dt.bfloat16
I32 = mybir.dt.int32
U32 = mybir.dt.uint32
ALU = mybir.AluOpType
ACT = mybir.ActivationFunctionType

P = 128
D = 768
KT = D // P
HALF = D // 2
E = 2048
ET = E // P
EA = 32
H4 = D // 4
TYPES = 6
REL = 3
H0 = 8
H2 = 4
C2 = 512
H3 = 4
C3 = D // H3
SLOPE = 0.2
EPS = 1e-5
TINY = 1e-16
BIG = 1e30
RAW = 4
SPLIT = 4
AHEAD = 3
CHUNK = 3 * D


def build(nc, io, out):
    ctx = ExitStack()
    with ctx:
        def sb(name, shape, dt=F32):
            return ctx.enter_context(nc.sbuf_tensor(name, shape, dt))

        def ps(name):
            return ctx.enter_context(nc.psum_tensor(name, [P, 2, 512], F32))

        def sem(name):
            return ctx.enter_context(nc.semaphore(name))

        chunks = []

        def tiles(w):
            return w.rearrange("(k p) n -> p k n", p=P)

        def add(view):
            chunks.append(view)
            return len(chunks) - 1

        w1, w2 = tiles(io["L0_gnn_W1"]), tiles(io["L0_gnn_W2"])
        L0W1, L0W2 = {}, {}
        for i in range(H0 + 2):
            if i < H0:
                for a in range(2):
                    L0W1[i, a] = add(w1[:, 3 * a:3 * a + 3, i * D:(i + 1) * D])
            if i >= 2:
                for a in range(2):
                    k = (i - 2) * KT + 3 * a
                    L0W2[i - 2, a] = add(w2[:, k:k + 3, :])
        L1T = {}
        for t in range(TYPES):
            wt = tiles(io["L1_gnn_W_type"][t])
            for a in range(2):
                L1T[t, a] = add(wt[:, 3 * a:3 * a + 3, :])
        L1M = [add(tiles(io["L1_gnn_msg_W1"])[:, 3 * a:3 * a + 3, :]) for a in range(4)]
        L1D = {}
        for name in ("msg_W2", "agg_W1", "agg_W2", "out_W"):
            for a in range(2):
                L1D[name, a] = add(tiles(io["L1_gnn_" + name])[:, 3 * a:3 * a + 3, :])
        w1, w2 = tiles(io["L2_gnn_W1"]), tiles(io["L2_gnn_W2"])
        L2W1, L2W2 = {}, {}
        for i in range(H2 + 2):
            if i < H2:
                for a in range(2):
                    L2W1[i, a] = add(w1[:, 3 * a:3 * a + 3, i * C2:(i + 1) * C2])
            if i >= 2:
                for a in range(2):
                    k = (i - 2) * (C2 // P) + 2 * a
                    L2W2[i - 2, a] = add(w2[:, k:k + 2, :])
        L3W = {}
        for layer in (1, 2):
            for r in range(REL):
                wr = tiles(io[f"L3_gnn_W{layer}"][r])
                for a in range(2):
                    L3W[layer, r, a] = add(wr[:, 3 * a:3 * a + 3, :])
        N = len(chunks)

        raw = sb("raw", [P, RAW, CHUNK])
        whi = sb("whi", [P, SPLIT, CHUNK], F32R)
        wlo = sb("wlo", [P, SPLIT, CHUNK], F32R)
        xT = sb("xT", [P, 2, D], F32R)
        el = sb("el", [P, 4, D], F32R)
        pq = sb("pq", [P, 4, D], F32R)
        oh = sb("oh", [P, 2, 2, P], F32R)
        ohe = sb("ohe", [P, 4, P], F32R)
        X = sb("X", [P, D])
        Hs = sb("Hs", [P, 2, D])
        tmp = sb("tmp", [P, 3, D])
        G = sb("G", [P, 6, D])
        bias = sb("bias", [P, 6, D])
        ident = sb("ident", [P, P])
        ones = sb("ones", [P, P])
        iota = sb("iota", [P, REL * P], I32)
        iotap = sb("iotap", [P, 1], I32)
        cnt3 = sb("cnt3", [P, REL, P])
        far3 = sb("far3", [P, REL, P])
        cnt = sb("cnt", [P, P])
        far = sb("far", [P, P])
        att = sb("att", [P, 4, P])
        biasT = sb("biasT", [P, 64])
        idx = sb("idx", [P, 3, ET], I32)
        nty = sb("nty", [P, 1], I32)
        idf = sb("idf", [P, 2, ET])
        typ = sb("typ", [P, TYPES], U32)
        tyo = sb("tyo", [TYPES, P])
        ew = sb("ew", [P, ET])
        ewhl = sb("ewhl", [P, ET, 2], F32R)
        sew = sb("sew", [P, 1])
        eb2 = sb("eb2", [P, 1])
        alph = sb("alph", [P, 2])
        red = sb("red", [P, 2])
        qk = sb("qk", [P, KT, 8])
        qkn = sb("qkn", [P, 10, REL])
        st = sb("st", [P, 2, 6])
        mv = sb("mv", [P, 4])
        neghalf = sb("neghalf", [P, 1])

        ohk = bias[:, 0:4, :].rearrange("p a b -> p (a b)").bitcast(BF16).rearrange("p (t n) -> p t n", t=ET)
        ohd = bias[:, 4:6, :].rearrange("p a b -> p (a b)")[:, 0:ET * P // 2].bitcast(BF16).rearrange("p (t n) -> p t n", t=ET)
        rows = G[:, :, :].rearrange("p a b -> p (a b)").bitcast(I32)
        rowT = [rows[:, j * E:(j + 1) * E].rearrange("p (m t) -> p t m", t=ET) for j in range(2)]
        ea = bias[:, 1, 0:ET * (EA + 1)].rearrange("p (t c) -> p t c", t=ET)
        eaT = bias[0:EA + 1, 2:5, :].rearrange("p a b -> p (a b)")[:, 0:E]
        ejunk = bias[:, 5, 0:H4]
        eW1 = bias[0:EA + 1, 5, D - 2 * H4:D - H4]
        eW2 = bias[:, 5, D - H4:D]
        bst = Hs[0:64, 1, P:2 * P]
        tyr = Hs[0:TYPES, 1, 0:P].bitcast(I32)
        bty = G[0:TYPES, 0, :]
        junk = tmp[:, 2, :]
        diag, sc, wt, wtT = (att[:, j, :] for j in range(4))

        HP, AC, TP, SB = (ps(name) for name in ("HP", "AC", "TP", "SB"))

        def two(pair):
            return pair[:, :, 0:HALF]

        def hidden_bank(n):
            return (AC, TP)[n // 2 % 2][:, n % 2, :]

        def cols(buf):
            return buf.rearrange("p (h n) -> p h n", h=2)

        def half(buf, h):
            return buf[:, h * HALF:(h + 1) * HALF]

        raw_landed = [sem(f"raw_landed{i}") for i in range(RAW)]
        hi_ready = sem("hi_ready")
        lo_dve = sem("lo_dve")
        lo_pool = sem("lo_pool")
        used = sem("used")
        made = {}

        def ev(name):
            if name not in made:
                made[name] = sem(name)
            return made[name]

        G0, G0F, G2, G2F = 0, H0, H0 + 1, H0 + 1 + H2
        NG = G2F + 1

        def width(g):
            return C2 if G2 <= g < G2F else D

        def inner(g):
            return g if g <= G0F else g - 1

        def arow(g):
            s = 0 if g < G0F else (2 if g % 2 == 0 else 4)
            return [G[:, s + j, 0:width(g)] for j in range(2)]

        def hbuf(g):
            return Hs[:, g % 2, 0:width(g)]

        def elbuf(g, j):
            return el[:, 2 * (g % 2) + j, 0:width(g)]

        def shape_of(n):
            _, k, c = chunks[n].shape
            return k, c

        def cut(n):
            k, c = shape_of(n)
            return k * c * 11 // 18 // 64 * 64

        def w_of(buf, n):
            k, c = shape_of(n)
            return buf[:, n % SPLIT, 0:k * c].rearrange("p (k c) -> p k c", k=k)

        block = ctx.enter_context(nc.Block())

        BIAS_SLOT = {"L0_gnn_b2": 0, "L1_gnn_msg_b1": 1, "L1_gnn_msg_b2": 2, "L1_gnn_agg_b1": 3,
                     "L1_gnn_agg_b2": 4, "L1_gnn_out_b": 5, "L1_gnn_ln_g": 2, "L1_gnn_ln_b": 0,
                     "L2_gnn_b2": 1, "L3_gnn_b2": 4, "L3_gnn_b1": 3}

        def bc(v):
            return v.partition_broadcast(P)

        @block.sync
        def _(sp):
            def chunk(n):
                if n >= RAW:
                    sp.wait_ge(lo_dve, n - RAW + 1)
                    sp.wait_ge(lo_pool, n - RAW + 1)
                k, c = shape_of(n)
                sp.dma_start(raw[:, n % RAW, 0:k * c].rearrange("p (k c) -> p k c", k=k), chunks[n])\
                  .then_inc(raw_landed[n % RAW], 16)

            def load_bias(name):
                sp.dma_start(bias[:, BIAS_SLOT[name], :], bc(io[name])).then_inc(ev("ld_" + name), 16)

            def load_arow(g, a, b):
                src, dst = arow(g)
                sp.dma_start(src, bc(a)).then_inc(ev(f"arow{g}"), 16)
                sp.dma_start(dst, bc(b)).then_inc(ev(f"arow{g}"), 16)

            sp.dma_start(X[:, :], io["x"]).then_inc(ev("ld_x"), 16)
            for n in range(N):
                chunk(n)
                if n == 0:
                    for j, name in enumerate(("L0_gnn_a_src1", "L0_gnn_a_dst1")):
                        for q in range(4):
                            sp.dma_start(G[32 * q:32 * q + 1, 2 + 2 * j:4 + 2 * j, :], io[name][2 * q:2 * q + 2, :])\
                               .then_inc(ev("ld_rows"), 16)
                if n == L0W1[1, 1]:
                    sp.dma_start(tyr, io["node_type_6"].partition_broadcast(TYPES)).then_inc(ev("ld_tyr"), 16)
                    sp.dma_start(eW1[0:EA, :], io["L1_gnn_edge_W1"]).then_inc(ev("ld_edge"), 16)
                    sp.dma_start(eW1[EA:EA + 1, :], io["L1_gnn_edge_b1"].rearrange("(a n) -> a n", a=1)).then_inc(ev("ld_edge"), 16)
                    sp.dma_start(eW2, bc(io["L1_gnn_edge_W2"].rearrange("n a -> (n a)"))).then_inc(ev("ld_edge"), 16)
                    sp.dma_start(eb2[:, :], bc(io["L1_gnn_edge_b2"])).then_inc(ev("ld_edge"), 16)
                    sp.dma_start(bst[0:H0 * KT, :], io["L0_gnn_b1"].rearrange("(a n) -> a n", n=P)).then_inc(ev("ld_edge"), 16)
                    sp.dma_start(bst[H0 * KT:64, :], io["L2_gnn_b1"].rearrange("(a n) -> a n", n=P)).then_inc(ev("ld_edge"), 16)
                    sp.dma_start(qk[:, :, 0:H3], tiles(io["L3_gnn_q1"])).then_inc(ev("ld_qk"), 16)
                    sp.dma_start(qk[:, :, H3:2 * H3], tiles(io["L3_gnn_k1"])).then_inc(ev("ld_qk"), 16)
                if n == L0W1[2, 1]:
                    sp.wait_ge(ev("counted"), 1)
                    sp.dma_start(ea[:, :, 0:EA], io["edge_attr_32"].rearrange("(p t) c -> p t c", t=ET)).then_inc(ev("ld_ea"), 16)
                    load_bias("L0_gnn_b2")
                if n == L0W2[6, 0]:
                    sp.wait_ge(ev("abc"), H0)
                    load_arow(G0F, io["L0_gnn_a_src2"][0], io["L0_gnn_a_dst2"][0])
                if n == L0W2[7, 1]:
                    sp.wait_ge(ev("dots"), H0)
                    sp.dma_start(bty, io["L1_gnn_b_type"]).then_inc(ev("ld_bty"), 16)
                    for name in ("msg_b1", "msg_b2", "agg_b1", "agg_b2", "out_b"):
                        load_bias("L1_gnn_" + name)
                    sp.wait_ge(ev("x_biased"), 1)
                    load_bias("L1_gnn_ln_b")
                if n == L1T[2, 0]:
                    sp.wait_ge(ev("dots"), G0F + 1)
                    sp.wait_ge(ev("type_bias"), 1)
                    sp.dma_start(rows[:, 0:E], bc(io["src"])).then_inc(ev("rows"), 16)
                    sp.dma_start(rows[:, E:2 * E], bc(io["dst"])).then_inc(ev("rows"), 16)
                if n == L1D["out_W", 0]:
                    sp.wait_ge(ev("ts_src"), 2 * 4)
                    load_bias("L1_gnn_ln_g")
                if n == L2W1[0, 0]:
                    sp.wait_ge(ev("oh_made"), ET)
                    for g in (G2, G2 + 1):
                        load_arow(g, io["L2_gnn_a1_src"][g - G2], io["L2_gnn_a1_dst"][g - G2])
                    sp.wait_ge(ev("ts_src"), 2 * 4)
                    load_bias("L2_gnn_b2")
                    load_bias("L3_gnn_b2")
                if n == L2W1[2, 1]:
                    sp.wait_ge(ev("dots"), G2 + 1)
                    g = G2 + 2
                    load_arow(g, io["L2_gnn_a1_src"][g - G2], io["L2_gnn_a1_dst"][g - G2])
                if n == L2W1[3, 1]:
                    sp.wait_ge(ev("dots"), G2 + 2)
                    g = G2 + 3
                    load_arow(g, io["L2_gnn_a1_src"][g - G2], io["L2_gnn_a1_dst"][g - G2])
                if n == L2W2[2, 0]:
                    sp.wait_ge(ev("dots"), G2 + 3)
                    load_arow(G2F, io["L2_gnn_a2_src"][0], io["L2_gnn_a2_dst"][0])
                    load_bias("L3_gnn_b1")
            sp.wait_ge(ev("dots"), NG)
            sp.dma_start(G[:, 4, :], bc(io["L3_gnn_q2"].rearrange("d a -> (d a)"))).then_inc(ev("qk2"), 16)
            sp.dma_start(G[:, 5, :], bc(io["L3_gnn_k2"].rearrange("d a -> (d a)"))).then_inc(ev("qk2"), 16)
            sp.wait_ge(ev("normed"), 2)
            sp.dma_start(out, X[:, :]).then_inc(ev("stored"), 16)
            sp.wait_ge(ev("stored"), 16)

        @block.tensor
        def _(pe):
            def wait_chunk(n):
                pe.wait_ge(hi_ready, n + 1)
                pe.wait_ge(lo_dve, n + 1)
                pe.wait_ge(lo_pool, n + 1)

            def dense(outs, left, n, kts, start, stop):
                wait_chunk(n)
                k, c = shape_of(n)
                hi, lo = w_of(whi, n), w_of(wlo, n)
                for o, (a, b) in outs:
                    for j, kt in enumerate(kts):
                        for m, (x, w) in enumerate(((left(0, kt), hi), (left(0, kt), lo), (left(1, kt), hi))):
                            last = pe.matmul(o, x, w[:, j, a:b], start=start and j == 0 and m == 0,
                                             stop=stop and j == k - 1 and m == 2)
                last.then_inc(used, 1)

            def left_x(i, kt):
                return xT[:, i, kt * P:(kt + 1) * P]

            def halves(pair):
                return [(pair[:, h, 0:HALF], (h * HALF, (h + 1) * HALF)) for h in range(2)]

            def product(pair, ns):
                for a, n in enumerate(ns):
                    dense(halves(pair), left_x, n, range(3 * a, 3 * a + 3), a == 0, a == 1)

            def transposes(k, src):
                for h in range(2):
                    if k == 0:
                        pe.wait_ge(ev("ld_x"), 16)
                    else:
                        pe.wait_ge(ev("ts_src"), 2 * (k - 1) + h + 1)
                    for j in range(3):
                        c = (3 * h + j) * P
                        last = pe.transpose(TP[:, h, j * P:(j + 1) * P], src[:, c:c + P], ident[:, :])
                    last.then_inc(ev("ts_out"), 1)

            def xt_ready(k):
                pe.wait_ge(ev("ts_hi"), 2 * k + 2)
                pe.wait_ge(ev("ts_lo"), 2 * k + 2)

            def w1(g, a, n):
                if a == 0 and g > 0:
                    pe.wait_ge(ev("h_out"), g)
                o = halves(HP) if width(g) == D else [(HP[:, 0, :], (0, C2))]
                dense(o, left_x, n, range(3 * a, 3 * a + 3), a == 0, a == 1)

            def spread(g):
                pe.wait_ge(ev("diag"), g + 1)
                pe.matmul(SB[:, 0, 0:P], ones[:, :], diag, start=True, stop=True).then_inc(ev("spread"), 1)

            def turn(g):
                pe.wait_ge(ev("weights"), g + 1)
                if g == 0:
                    pe.wait_ge(ev("biasT"), 1)
                pe.transpose(SB[:, 1, 0:P], wt, ident[:, :]).then_inc(ev("turned"), 1)

            def aggregate_T(g):
                pe.wait_ge(ev("turned_out"), g + 1)
                if inner(g) > 0:
                    pe.wait_ge(ev("z"), inner(g))
                for k in range(width(g) // P):
                    last = pe.matmul(TP[:, k // 3, (k % 3) * P:(k % 3 + 1) * P],
                                     hbuf(g)[:, k * P:(k + 1) * P], wtT, start=True, stop=True)
                last.then_inc(ev("summed"), 1)

            def w2(g, a, n, first, final):
                if a == 0 and g == 0:
                    pe.wait_ge(ev("ew_dot"), ET // 2)
                if a == 0:
                    pe.wait_ge(ev("el_hi"), inner(g) + 1)
                    pe.wait_ge(ev("el_lo"), inner(g) + 1)
                k, _ = shape_of(n)

                def left(i, kt):
                    return elbuf(g, i)[:, kt * P:(kt + 1) * P]
                dense(halves(AC), left, n, range(k * a, k * a + k), first and a == 0, final and a == 1)

            def gat(g0, heads, W1, W2):
                for i in range(heads + 2):
                    g = g0 + i
                    if i < heads:
                        w1(g, 0, W1[i, 0])
                    if 1 <= i <= heads:
                        turn(g - 1)
                    if i < heads:
                        w1(g, 1, W1[i, 1])
                    if 1 <= i <= heads:
                        aggregate_T(g - 1)
                    if g == 0:
                        pe.wait_ge(ev("ld_edge"), 16 * 6)
                        pe.transpose(SB[:, 1, 0:64], bst, ident[0:64, 0:64]).then_inc(ev("bst"), 1)
                        count_edges()
                    if g == 1:
                        spread(g)
                        edge_hidden()
                    if i >= 2:
                        w2(g - 2, 0, W2[i - 2, 0], i == 2, i == heads + 1)
                    if g != 1 and i < heads:
                        spread(g)
                    if i >= 2:
                        w2(g - 2, 1, W2[i - 2, 1], i == 2, i == heads + 1)
                g = g0 + heads
                spread(g)
                turn(g)
                pe.wait_ge(ev("turned_out"), g + 1)
                for h in range(2):
                    pe.matmul(HP[:, h, 0:HALF], wtT, half(hbuf(g), h), start=True, stop=True)\
                      .then_inc(ev("summed_h"), 1)

            def count_edges():
                pe.wait_ge(ev("onehots"), 3)
                for t in range(ET):
                    last = pe.matmul(AC[:, 0, 0:REL * P], ohd[:, t, :], ohk[:, t, :], start=t == 0, stop=t == ET - 1)
                last.then_inc(ev("counted"), 1)

            def edge_hidden():
                pe.wait_ge(ev("ea_ones"), 1)
                pe.wait_ge(ev("ld_ea"), 16)
                pe.wait_ge(ev("turned_out"), 1)
                pe.wait_ge(ev("scored"), 2)
                pe.wait_ge(ev("cnt_out"), 1)
                for q in range(2):
                    if q:
                        pe.wait_ge(ev("ea_out"), 1)
                    for j in range(8):
                        last = pe.transpose(SB[0:EA + 1, j // 4, (j % 4) * P:(j % 4 + 1) * P], ea[:, 8 * q + j, :], ident[:, :])
                    last.then_inc(ev("ea_T"), 1)
                pe.wait_ge(ev("z"), 1)
                for n in range(ET // 2):
                    if n == 4:
                        pe.wait_ge(ev("ea_out"), 2)
                    if n >= 4:
                        pe.wait_ge(ev("ew_dot"), n - 3)
                    for m in range(2):
                        last = pe.matmul(hidden_bank(n)[:, m * H4:(m + 1) * H4], eaT[:, (2 * n + m) * P:(2 * n + m + 1) * P],
                                         eW1, start=True, stop=True)
                    last.then_inc(ev("edge_hidden"), 1)

            pe.wait_ge(ev("consts"), 5)
            transposes(0, X)
            xt_ready(0)
            gat(G0, H0, L0W1, L0W2)
            pe.wait_ge(ev("ld_bty"), 16)
            pe.wait_ge(ev("tyo"), 1)
            for h in range(2):
                last = pe.matmul(AC[:, h, 0:HALF], tyo[:, :], half(bty, h), start=True, stop=True)
            last.then_inc(ev("type_bias"), 1)
            transposes(1, X)
            xt_ready(1)
            for t in range(TYPES):
                if t >= 2:
                    pe.wait_ge(ev("chosen"), t - 1)
                product((HP, SB)[t % 2], [L1T[t, a] for a in range(2)])
            transposes(2, Hs[:, 1, :])
            xt_ready(2)
            product(HP, L1M[0:2])
            product(SB, L1M[2:4])
            for t in range(ET + 2):
                if t < ET:
                    pair = (HP, SB)[t % 2]
                    pe.wait_ge(ev("oh_made"), t + 1)
                    if t == 0:
                        pe.wait_ge(ev("pq_hi"), 2)
                        pe.wait_ge(ev("pq_lo"), 2)
                    if t >= 2:
                        pe.wait_ge(ev("relu_out"), t - 1)
                    for h in range(2):
                        for m in range(4):
                            last = pe.matmul(pair[:, h, 0:HALF], oh[:, t % 2, m // 2, :],
                                             half(pq[:, m, :], h), start=m == 0, stop=m == 3)
                    last.then_inc(ev("gathered"), 1)
                if t >= 2:
                    s = t - 2
                    pe.wait_ge(ev("r_hi"), s + 1)
                    pe.wait_ge(ev("r_lo"), s + 1)
                    for h in range(2):
                        for m in range(2):
                            last = pe.matmul(AC[:, h, 0:HALF], ohe[:, s % 4, :], half(el[:, 2 * (s % 2) + m, :], h),
                                             start=s == 0 and m == 0, stop=s == ET - 1 and m == 1)
                    last = pe.matmul(TP[:, 0, HALF:HALF + 2], ohe[:, s % 4, :], ewhl[:, s, :],
                                     start=s == 0, stop=s == ET - 1)
                    last.then_inc(ev("scattered"), 1)
            for j, name in enumerate(("msg_W2", "agg_W1", "agg_W2", "out_W")):
                transposes(3 + j, tmp[:, j % 2, :])
                xt_ready(3 + j)
                product(HP, [L1D[name, a] for a in range(2)])
            transposes(7, X)
            xt_ready(7)
            gat(G2, H2, L2W1, L2W2)
            transposes(8, X)
            xt_ready(8)
            pe.wait_ge(ev("ld_qk"), 32)
            for layer in (1, 2):
                if layer == 2:
                    transposes(9, tmp[:, 0, :])
                    xt_ready(9)
                for r in range(REL):
                    if r == 2:
                        pe.wait_ge(ev("xr_out"), REL * (layer - 1) + 1)
                    product((HP, SB)[r % 2], [L3W[layer, r, a] for a in range(2)])
                    if layer == 1:
                        pe.wait_ge(ev("xr_out"), r + 1)
                        for k in range(KT):
                            last = pe.transpose(TP[:, k // 3, (k % 3) * P:(k % 3 + 1) * P],
                                                G[:, r, k * P:(k + 1) * P], ident[:, :])
                        last.then_inc(ev("xrT"), 1)
                        pe.wait_ge(ev("xrT_out"), r + 1)
                        for k in range(KT):
                            last = pe.matmul(AC[:, 0, r * 8:(r + 1) * 8], G[:, 3, k * P:(k + 1) * P], qk[:, k, :],
                                             start=k == 0, stop=k == KT - 1)
                        last.then_inc(ev("qk_dot"), 1)
                for hd in range(H3 if layer == 1 else 1):
                    v = hd if layer == 1 else H3
                    pe.wait_ge(ev("diag3"), v + 1)
                    pe.matmul(SB[:, 0, 0:REL * P], ones[:, :], tmp[:, 1, 0:REL * P], start=True, stop=True)\
                      .then_inc(ev("spread3"), 1)
                    pe.wait_ge(ev("weights3"), v + 1)
                    for r in range(REL):
                        last = pe.transpose(SB[:, 1, r * P:(r + 1) * P], tmp[:, 2, r * P:(r + 1) * P], ident[:, :])
                    last.then_inc(ev("turned3"), 1)
                    pe.wait_ge(ev("turned3_out"), v + 1)
                    if layer == 1:
                        h, c = hd // 2, (hd % 2) * C3
                        for r in range(REL):
                            last = pe.matmul(HP[:, h, c:c + C3], Hs[:, 0, r * P:(r + 1) * P],
                                             G[:, r, hd * C3:(hd + 1) * C3], start=r == 0, stop=r == REL - 1)
                        last.then_inc(ev("summed3"), 1)
                    else:
                        for h in range(2):
                            for r in range(REL):
                                last = pe.matmul(HP[:, h, 0:HALF], Hs[:, 0, r * P:(r + 1) * P],
                                                 half(G[:, r, :], h), start=r == 0, stop=r == REL - 1)
                            last.then_inc(ev("summed_h"), 1)

        @block.scalar
        def _(act):
            at = [0]

            def split_to(n):
                while at[0] <= min(n, N - 1):
                    m = at[0]
                    act.wait_ge(raw_landed[m % RAW], 16 * (m // RAW + 1))
                    if m >= SPLIT:
                        act.wait_ge(used, m - SPLIT + 1)
                    k, c = shape_of(m)
                    act.activation(whi[:, m % SPLIT, 0:k * c], raw[:, m % RAW, 0:k * c], ACT.Copy).then_inc(hi_ready, 1)
                    at[0] += 1

            def ts_hi(k, func=ACT.Copy):
                for h in range(2):
                    act.wait_ge(ev("ts_out"), 2 * k + h + 1)
                    act.activation(half(xT[:, 0, :], h), TP[:, h, 0:HALF], func).then_inc(ev("ts_hi"), 1)

            def expo(g):
                act.wait_ge(ev("lowest"), g + 1)
                act.activation(wt, sc, ACT.Exp, bias=red[:, 0:1], scale=-1.0).then_inc(ev("exped"), 1)

            def turned_out(g):
                act.wait_ge(ev("turned"), g + 1)
                act.activation(wtT, SB[:, 1, 0:P], ACT.Copy).then_inc(ev("turned_out"), 1)

            def h_out(g, n):
                act.wait_ge(used, n + 1)
                if g == 1:
                    act.wait_ge(ev("tyo"), 1)
                if inner(g) >= 2:
                    act.wait_ge(ev("summed"), inner(g) - 1)
                src = AC if g in (G0F, G2F) else HP
                o, i = (cols(hbuf(g)), two(src)) if width(g) == D else (hbuf(g), src[:, 0, :])
                act.activation(o, i, ACT.Copy).then_inc(ev("h_out"), 1)

            def elu_exp(g):
                act.wait_ge(ev("zmin"), inner(g) + 1)
                c = width(g)
                act.activation(tmp[:, 1, 0:c], tmp[:, 1, 0:c], ACT.Exp).then_inc(ev("elu_exp"), 1)

            def el_hi(g):
                act.wait_ge(ev("elu"), inner(g) + 1)
                act.activation(elbuf(g, 0), tmp[:, 0, 0:width(g)], ACT.Copy).then_inc(ev("el_hi"), 1)

            def gat(g0, heads, W1, W2):
                n = W1[0, 0]
                for i in range(heads + 2):
                    g = g0 + i
                    if i < heads:
                        n = W1[i, 0]
                        split_to(n + AHEAD)
                    if 1 <= i <= heads:
                        turned_out(g - 1)
                    if i < heads:
                        n = W1[i, 1]
                        split_to(n + AHEAD)
                        h_out(g, n)
                    if g == 0:
                        act.wait_ge(ev("bst"), 1)
                        act.activation(biasT[:, :], SB[:, 1, 0:64], ACT.Copy).then_inc(ev("biasT"), 1)
                    if i >= 2:
                        n = W2[i - 2, 0]
                        split_to(n + AHEAD)
                    if 1 <= i <= heads:
                        elu_exp(g - 1)
                    if i < heads:
                        expo(g)
                    if i >= 2:
                        n = W2[i - 2, 1]
                        split_to(n + AHEAD)
                    if 1 <= i <= heads:
                        el_hi(g - 1)
                    if g == 1:
                        edge_weights()
                g = g0 + heads
                h_out(g, n)
                expo(g)
                turned_out(g)
                split_to(n + 1 + AHEAD)

            for j, name in enumerate(("dst", "src", "edge_type_3")):
                act.dma_start(idx[:, j, :], io[name].rearrange("(p t) -> p t", t=ET)).then_inc(ev("ld_idx"), 16)
            act.dma_start(nty[:, :], io["node_type_6"].rearrange("(p a) -> p a", a=1)).then_inc(ev("ld_idx"), 16)
            def edge_weights():
                for q in range(2):
                    act.wait_ge(ev("ea_T"), q + 1)
                    act.activation(eaT[:, q * 8 * P:(q + 1) * 8 * P].rearrange("p (a n) -> p a n", a=2), SB[0:EA + 1, :, :], ACT.Copy).then_inc(ev("ea_out"), 1)
                act.wait_ge(ev("ew_dot"), ET // 2)
                act.wait_ge(ev("eb2_neg"), 1)
                act.activation(ew[:, :], ew[:, :], ACT.Exp, bias=eb2[:, 0:1], scale=-1.0).then_inc(ev("ew_exp"), 1)

            ts_hi(0)
            gat(G0, H0, L0W1, L0W2)
            ts_hi(1)
            for t in range(TYPES):
                for a in range(2):
                    split_to(L1T[t, a] + AHEAD)
                if t == 0:
                    act.wait_ge(ev("ew_done"), 1)
                    act.activation(ewhl[:, :, 0], ew[:, :], ACT.Copy).then_inc(ev("ew_hi"), 1)
            ts_hi(2)
            for a in range(2):
                split_to(L1M[a] + AHEAD)
            act.wait_ge(used, L1M[1] + 1)
            act.activation(cols(pq[:, 0, :]), two(HP), ACT.Copy).then_inc(ev("pq_hi"), 1)
            for a in range(2, 4):
                split_to(L1M[a] + AHEAD)
            act.wait_ge(ev("q_sum"), 1)
            act.activation(pq[:, 2, :], tmp[:, 2, :], ACT.Copy).then_inc(ev("pq_hi"), 1)
            for t in range(ET):
                act.wait_ge(ev("gathered"), t + 1)
                if t >= 2:
                    act.wait_ge(ev("r_lo"), t - 1)
                act.activation(cols(tmp[:, t % 2, :]), two((HP, SB)[t % 2]), ACT.Relu, scale=ew[:, t:t + 1])\
                   .then_inc(ev("relu_out"), 1)
                act.wait_ge(ev("relu_out"), t + 1)
                if t >= 2:
                    act.wait_ge(ev("scattered"), t - 1)
                act.activation(el[:, 2 * (t % 2), :], tmp[:, t % 2, :], ACT.Copy).then_inc(ev("r_hi"), 1)
                if t % 4 == 3:
                    split_to(L1M[3] + 1 + min(t // 4, AHEAD))
            split_to(L1M[3] + 1 + AHEAD)
            for j, name in enumerate(("msg_W2", "agg_W1", "agg_W2", "out_W")):
                ts_hi(3 + j, ACT.Relu if j == 2 else ACT.Copy)
                for a in range(2):
                    split_to(L1D[name, a] + AHEAD)
            split_to(L1D["out_W", 1] + 1 + AHEAD)
            ts_hi(7)
            gat(G2, H2, L2W1, L2W2)
            ts_hi(8)
            for layer in (1, 2):
                if layer == 2:
                    act.wait_ge(ev("zmin"), inner(NG))
                    act.activation(tmp[:, 1, :], tmp[:, 1, :], ACT.Exp).then_inc(ev("elu_exp"), 1)
                    ts_hi(9)
                for r in range(REL):
                    for a in range(2):
                        split_to(L3W[layer, r, a] + AHEAD)
                    act.wait_ge(used, L3W[layer, r, 1] + 1)
                    if layer == 1 and r == 0:
                        act.wait_ge(ev("dots"), NG)
                    act.activation(cols(G[:, r, :]), two((HP, SB)[r % 2]), ACT.Copy).then_inc(ev("xr_out"), 1)
                    if layer == 1:
                        act.wait_ge(ev("xrT"), r + 1)
                        if r:
                            act.wait_ge(ev("qk_dot"), r)
                        act.activation(cols(G[:, 3, :]), two(TP), ACT.Copy).then_inc(ev("xrT_out"), 1)
                for hd in range(H3 if layer == 1 else 1):
                    v = hd if layer == 1 else H3
                    act.wait_ge(ev("lowest3"), v + 1)
                    act.activation(tmp[:, 2, 0:REL * P], Hs[:, 1, 0:REL * P], ACT.Exp, bias=red[:, 0:1], scale=-1.0)\
                       .then_inc(ev("exped3"), 1)
                    act.wait_ge(ev("turned3"), v + 1)
                    if hd:
                        act.wait_ge(ev("summed3"), hd)
                    act.activation(Hs[:, 0, 0:REL * P], SB[:, 1, 0:REL * P], ACT.Copy).then_inc(ev("turned3_out"), 1)

        @block.vector
        def _(dve):
            at = [0]
            count = {}

            def done(ins, name, by=1):
                count[name] = count.get(name, 0) + by
                ins.then_inc(ev(name), by)
                dve.wait_ge(ev(name), count[name])

            def step(ins):
                done(ins, "vector_step")

            def split_to(n):
                while at[0] <= min(n, N - 1):
                    m = at[0]
                    dve.wait_ge(hi_ready, m + 1)
                    c = cut(m)
                    dve.tensor_tensor(wlo[:, m % SPLIT, 0:c], raw[:, m % RAW, 0:c],
                                      whi[:, m % SPLIT, 0:c].bitcast(F32), ALU.subtract).then_inc(lo_dve, 1)
                    at[0] += 1

            def ts_lo(k, relu=False):
                for h in range(2):
                    dve.wait_ge(ev("ts_hi"), 2 * k + h + 1)
                    hi = half(xT[:, 0, :], h).bitcast(F32)
                    if relu:
                        ins = dve.scalar_tensor_tensor(half(xT[:, 1, :], h), TP[:, h, 0:HALF], 0.0, hi, ALU.max, ALU.subtract)
                    else:
                        ins = dve.tensor_tensor(half(xT[:, 1, :], h), TP[:, h, 0:HALF], hi, ALU.subtract)
                    ins.then_inc(ev("ts_lo"), 1)

            def dots(g):
                dve.wait_ge(ev("h_out"), g + 1)
                if g < G0F:
                    dve.wait_ge(ev("abc"), g + 1)
                else:
                    dve.wait_ge(ev(f"arow{g}"), 32)
                c = width(g)
                for j in range(2):
                    ins = dve.tensor_tensor_reduce(junk[:, 0:c], hbuf(g), arow(g)[j], 1.0, 0.0, ALU.mult, ALU.add,
                                                   alph[:, j:j + 1])
                    if j:
                        done(ins, "dots")
                    else:
                        step(ins)
                if g:
                    dve.wait_ge(ev("spread"), g)
                dve.tensor_scalar(diag, ident[:, :], alph[:, 0:1], None, ALU.mult).then_inc(ev("diag"), 1)

            def scores(g):
                dve.wait_ge(ev("spread"), g + 1)
                done(dve.tensor_scalar(sc, SB[:, 0, 0:P], -1.0, alph[:, 1:2], ALU.mult, ALU.subtract), "scored")
                step(dve.scalar_tensor_tensor(sc, sc, SLOPE, sc, ALU.mult, ALU.min))
                done(dve.tensor_tensor_reduce(sc, sc, far[:, :], 1.0, 3e38, ALU.add, ALU.min, red[:, 0:1]), "lowest")

            def weights(g):
                dve.wait_ge(ev("exped"), g + 1)
                step(dve.tensor_tensor_reduce(wt, wt, cnt[:, :], 1.0, 0.0, ALU.mult, ALU.add, red[:, 1:2]))
                if g >= G2:
                    step(dve.tensor_scalar(red[:, 1:2], red[:, 1:2], TINY, None, ALU.add))
                step(dve.reciprocal(red[:, 1:2], red[:, 1:2]))
                done(dve.tensor_scalar(wt, wt, red[:, 1:2], None, ALU.mult), "weights")

            def elu_in(g):
                dve.wait_ge(ev("summed"), inner(g) + 1)
                if g == 0:
                    dve.wait_ge(ev("biasT"), 1)
                c = width(g)
                for b in range(2):
                    k0, k1 = 3 * b, min(3 * b + 3, c // P)
                    first = (g * KT if g < G0F else H0 * KT + (g - G2) * (C2 // P)) + k0
                    m = k1 - k0
                    ins = dve.tensor_tensor(tmp[:, 0, k0 * P:k1 * P].rearrange("p (k n) -> p k n", k=m),
                                            TP[:, b, 0:m * P].rearrange("p (k n) -> p k n", k=m),
                                            biasT[:, first:first + m].unsqueeze(2).broadcast_to((P, m, P)), ALU.add)
                    if b:
                        done(ins, "z")
                    else:
                        step(ins)
                done(dve.tensor_scalar(tmp[:, 1, 0:c], tmp[:, 0, 0:c], 0.0, None, ALU.min), "zmin")

            def elu_end(g):
                dve.wait_ge(ev("elu_exp"), inner(g) + 1)
                c = width(g)
                done(dve.scalar_tensor_tensor(tmp[:, 0, 0:c], tmp[:, 1, 0:c], -1.0, tmp[:, 0, 0:c], ALU.add, ALU.max), "elu")

            def el_low(g):
                c = width(g)
                dve.wait_ge(ev("el_hi"), inner(g) + 1)
                done(dve.tensor_tensor(elbuf(g, 1), tmp[:, 0, 0:c], elbuf(g, 0).bitcast(F32), ALU.subtract), "el_lo")

            def stats(k, src):
                for h in range(2):
                    step(dve.bn_stats(st[:, h, :], half(src, h)))
                step(dve.bn_aggr(mv[:, 0:2], st[:, :, :].rearrange("p a b -> p (a b)")))
                done(dve.tensor_scalar(mv[:, 2:3], mv[:, 1:2], EPS, None, ALU.add), "variance")
                dve.wait_ge(ev("rstd"), k + 1)

            def norm_x(k, last=False):
                stats(k, X[:, :])
                for h in range(2):
                    ins = dve.tensor_scalar(half(X[:, :], h), half(X[:, :], h), mv[:, 0:1], mv[:, 3:4], ALU.subtract, ALU.mult)
                    if last:
                        done(ins, "normed")
                    else:
                        done(ins, "ts_src")

            def gat(g0, heads, W1, W2, b2, ts, f):
                n = W1[0, 0]
                for i in range(heads + 2):
                    g = g0 + i
                    for k in range(2):
                        if i < heads:
                            n = W1[i, k]
                            split_to(n + AHEAD)
                    if g == 0:
                        edge_counts()
                    if i < heads:
                        dots(g)
                    if 1 <= i <= heads:
                        elu_in(g - 1)
                    if i < heads:
                        scores(g)
                    if i >= 2:
                        n = W2[i - 2, 0]
                        split_to(n + AHEAD)
                    if 1 <= i <= heads:
                        elu_end(g - 1)
                    if i < heads:
                        weights(g)
                    if i >= 2:
                        n = W2[i - 2, 1]
                        split_to(n + AHEAD)
                    if 1 <= i <= heads:
                        el_low(g - 1)
                    if g == 1:
                        edge_weights()
                    if i == 2:
                        add_bias(b2, ts)
                g = g0 + heads
                dots(g)
                scores(g)
                weights(g)
                split_to(n + 1 + AHEAD)
                residual(f)

            def add_bias(name, ts):
                dve.wait_ge(ev("ld_" + name), 16)
                dve.wait_ge(ev("ts_out"), 2 * ts + 2)
                done(dve.tensor_tensor(X[:, :], X[:, :], bias[:, BIAS_SLOT[name], :], ALU.add), "x_biased")

            def residual(f):
                for h in range(2):
                    dve.wait_ge(ev("summed_h"), 2 * f + h + 1)
                    step(dve.tensor_tensor(half(X[:, :], h), HP[:, h, 0:HALF], half(X[:, :], h), ALU.add))

            def edge_counts():
                dve.wait_ge(ev("counted"), 1)
                dve.memset(ea[:, :, EA], 1.0).then_inc(ev("ea_ones"), 1)
                done(dve.tensor_copy(cnt3[:, :, :].rearrange("p r n -> p (r n)"), AC[:, 0, 0:REL * P]), "cnt_out")
                step(dve.tensor_scalar(far3[:, :, :], cnt3[:, :, :], 0.5, BIG, ALU.is_lt, ALU.mult))
                step(dve.tensor_tensor(cnt[:, :], ident[:, :], cnt3[:, 0, :], ALU.add))
                for r in range(1, REL):
                    step(dve.tensor_tensor(cnt[:, :], cnt[:, :], cnt3[:, r, :], ALU.add))
                step(dve.tensor_scalar(far[:, :], cnt[:, :], 0.5, BIG, ALU.is_lt, ALU.mult))

            def edge_weights():
                for n in range(ET // 2):
                    dve.wait_ge(ev("edge_hidden"), n + 1)
                    for m in range(2):
                        ins = dve.scalar_tensor_tensor(ejunk, hidden_bank(n)[:, m * H4:(m + 1) * H4], 0.0, eW2,
                                                       ALU.max, ALU.mult, accum_out=ew[:, 2 * n + m:2 * n + m + 1])
                        if m:
                            done(ins, "ew_dot")
                        else:
                            step(ins)
                dve.wait_ge(ev("ew_exp"), 1)
                step(dve.tensor_scalar(ew[:, :], ew[:, :], 1.0, None, ALU.add))
                done(dve.reciprocal(ew[:, :], ew[:, :]), "ew_done")

            dve.wait_ge(ev("consts"), 5)
            dve.wait_ge(ev("ld_idx"), 16 * 4)
            step(dve.tensor_copy(idf[:, 0, :], idx[:, 0, :]))
            step(dve.scalar_tensor_tensor(idf[:, 1, :], idx[:, 2, :], float(P), idx[:, 1, :], ALU.mult, ALU.add))

            def onehots(o, m, j, t0, t1):
                n = t1 - t0
                dve.tensor_tensor(o[:, t0:t1, :], iota[:, 0:m].unsqueeze(1).broadcast_to((P, n, m)),
                                  idf[:, j, t0:t1].unsqueeze(2).broadcast_to((P, n, m)), ALU.is_equal).then_inc(ev("onehots"), 1)

            onehots(ohd, P, 0, 0, ET)
            ts_lo(0)
            split_to(0)
            onehots(ohk, REL * P, 1, 0, ET // 2)
            split_to(1)
            onehots(ohk, REL * P, 1, ET // 2, ET)
            step(dve.tensor_scalar(typ[:, :], iota[:, 0:TYPES], nty[:, 0:1], None, ALU.is_equal))
            dve.wait_ge(ev("ld_tyr"), 16)
            done(dve.tensor_scalar(tyo[:, :], tyr, iotap[0:TYPES, 0:1], None, ALU.is_equal), "tyo")
            dve.wait_ge(ev("ld_edge"), 16 * 6)
            done(dve.tensor_scalar(eb2[:, :], eb2[:, :], -1.0, None, ALU.mult), "eb2_neg")
            gat(G0, H0, L0W1, L0W2, "L0_gnn_b2", 0, 0)
            norm_x(0)
            ts_lo(1)
            for name in ("out_b", "ln_b"):
                b = bias[:, BIAS_SLOT["L1_gnn_" + name], :]
                dve.wait_ge(ev("ld_L1_gnn_" + name), 16)
                step(dve.tensor_tensor(b, b, X[:, :], ALU.add))
            for t in range(TYPES):
                for a in range(2):
                    split_to(L1T[t, a] + AHEAD)
                if t == 1:
                    dve.wait_ge(ev("ew_hi"), 1)
                    step(dve.tensor_tensor(ewhl[:, :, 1], ew[:, :], ewhl[:, :, 0].bitcast(F32), ALU.subtract))
                dve.wait_ge(used, L1T[t, 1] + 1)
                done(dve.copy_predicated(cols(Hs[:, 1, :]), typ[:, t:t + 1].unsqueeze(2).broadcast_to((P, 2, HALF)),
                                         two((HP, SB)[t % 2])), "chosen")
            dve.wait_ge(ev("type_bias"), 1)
            for h in range(2):
                done(dve.tensor_tensor(half(Hs[:, 1, :], h), half(Hs[:, 1, :], h), AC[:, h, 0:HALF], ALU.add), "ts_src")
            ts_lo(2)
            for a in range(2):
                split_to(L1M[a] + AHEAD)
            dve.wait_ge(ev("pq_hi"), 1)
            dve.tensor_tensor(cols(pq[:, 1, :]), two(HP), cols(pq[:, 0, :].bitcast(F32)), ALU.subtract).then_inc(ev("pq_lo"), 1)
            dve.wait_ge(ev("ts_out"), 6)
            dve.wait_ge(ev("ld_L1_gnn_agg_b2"), 16)
            step(dve.tensor_tensor(Hs[:, 1, :], Hs[:, 1, :], bias[:, BIAS_SLOT["L1_gnn_agg_b2"], :], ALU.add))
            for a in range(2, 4):
                split_to(L1M[a] + AHEAD)
            dve.wait_ge(used, L1M[3] + 1)
            dve.wait_ge(ev("ld_L1_gnn_msg_b1"), 16)
            done(dve.tensor_tensor(cols(tmp[:, 2, :]), two(SB), cols(bias[:, BIAS_SLOT["L1_gnn_msg_b1"], :]), ALU.add), "q_sum")
            dve.wait_ge(ev("pq_hi"), 2)
            dve.tensor_tensor(pq[:, 3, :], tmp[:, 2, :], pq[:, 2, :].bitcast(F32), ALU.subtract).then_inc(ev("pq_lo"), 1)

            def edge_onehots(t):
                if t >= 2:
                    dve.wait_ge(ev("gathered"), t - 1)
                if t >= 4:
                    dve.wait_ge(ev("scattered"), t - 3)
                for j, row in enumerate((rowT[0], rowT[1])):
                    dve.tensor_scalar(oh[:, t % 2, j, :], row[:, t, :], iotap[:, 0:1], None, ALU.is_equal)
                dve.tensor_scalar(ohe[:, t % 4, :], iota[:, 0:P], idf[:, 0, t:t + 1], None, ALU.is_equal).then_inc(ev("oh_made"), 1)

            for j in range(2):
                dve.wait_ge(ev("rows"), 32)
            edge_onehots(0)
            edge_onehots(1)
            for t in range(ET):
                dve.wait_ge(ev("r_hi"), t + 1)
                dve.tensor_tensor(el[:, 2 * (t % 2) + 1, :], tmp[:, t % 2, :], el[:, 2 * (t % 2), :].bitcast(F32), ALU.subtract)\
                   .then_inc(ev("r_lo"), 1)
                if t + 2 < ET:
                    edge_onehots(t + 2)
                if t % 4 == 3:
                    split_to(L1M[3] + 1 + min(t // 4, AHEAD))
            dve.wait_ge(ev("scattered"), ET)
            dve.wait_ge(ev("r_lo"), ET)
            step(dve.tensor_reduce(sew[:, :], TP[:, 0, HALF:HALF + 2], mybir.AxisListType.X, ALU.add))
            for h in range(2):
                done(dve.tensor_copy(half(tmp[:, 0, :], h), AC[:, h, 0:HALF]), "ts_src")
            ts_lo(3)
            for j, name in enumerate(("msg_W2", "agg_W1", "agg_W2", "out_W")):
                for a in range(2):
                    split_to(L1D[name, a] + AHEAD)
                b = bias[:, BIAS_SLOT["L1_gnn_" + ("msg_b2", "agg_b1", "agg_b2", "out_b")[j]], :]
                if j < 2:
                    dve.wait_ge(ev("ld_L1_gnn_" + ("msg_b2", "agg_b1")[j]), 16)
                if j == 2:
                    b = Hs[:, 1, :]
                dve.wait_ge(used, L1D[name, 1] + 1)
                for h in range(2):
                    o = half(tmp[:, (j + 1) % 2, :], h)
                    if j == 0:
                        ins = dve.scalar_tensor_tensor(o, half(b, h), sew[:, 0:1], HP[:, h, 0:HALF], ALU.mult, ALU.add)
                    else:
                        ins = dve.tensor_tensor(o, HP[:, h, 0:HALF], half(b, h), ALU.add)
                    if j < 3:
                        done(ins, "ts_src")
                    else:
                        step(ins)
                if j < 3:
                    ts_lo(4 + j, relu=j == 1)
            y = tmp[:, 0, :]
            stats(1, y)
            step(dve.tensor_scalar(y, y, mv[:, 0:1], mv[:, 3:4], ALU.subtract, ALU.mult))
            dve.wait_ge(ev("ld_L1_gnn_ln_g"), 16)
            step(dve.tensor_tensor(y, y, bias[:, BIAS_SLOT["L1_gnn_ln_g"], :], ALU.mult))
            step(dve.tensor_tensor(X[:, :], y, bias[:, BIAS_SLOT["L1_gnn_ln_b"], :], ALU.add))
            norm_x(2)
            ts_lo(7)
            split_to(L1D["out_W", 1] + 1 + AHEAD)
            gat(G2, H2, L2W1, L2W2, "L2_gnn_b2", 7, 1)
            norm_x(3)
            ts_lo(8)
            add_bias("L3_gnn_b2", 8)
            for layer in (1, 2):
                for r in range(REL):
                    for a in range(2):
                        split_to(L3W[layer, r, a] + AHEAD)
                    if layer == 2:
                        dve.wait_ge(ev("xr_out"), REL + r + 1)
                        dve.wait_ge(ev("qk2"), 32)
                        for j in range(2):
                            step(dve.tensor_tensor_reduce(Hs[:, 1, :], G[:, r, :], G[:, 4 + j, :], 1.0, 0.0, ALU.mult, ALU.add,
                                                          qkn[:, 8 + j, r:r + 1]))
                if layer == 1:
                    dve.wait_ge(ev("qk_dot"), REL)
                    step(dve.tensor_copy(qkn[:, 0:8, :], AC[:, 0, 0:REL * 8].rearrange("p (r c) -> p c r", r=REL)))
                for hd in range(H3 if layer == 1 else 1):
                    v, q, k = (hd, hd, H3 + hd) if layer == 1 else (H3, 8, 9)

                    def by_rel(buf):
                        return buf.rearrange("p (r n) -> p r n", r=REL)

                    def spread_rel(c):
                        return qkn[:, c, :].unsqueeze(2).broadcast_to((P, REL, P))
                    if v:
                        dve.wait_ge(ev("spread3"), v)
                    dve.tensor_tensor(by_rel(tmp[:, 1, 0:REL * P]), ident[:, :].unsqueeze(1).broadcast_to((P, REL, P)),
                                      spread_rel(k), ALU.mult).then_inc(ev("diag3"), 1)
                    dve.wait_ge(ev("spread3"), v + 1)
                    s3, w3 = Hs[:, 1, 0:REL * P], tmp[:, 2, 0:REL * P]
                    step(dve.scalar_tensor_tensor(by_rel(s3), by_rel(SB[:, 0, 0:REL * P]), -1.0, spread_rel(q), ALU.mult, ALU.subtract))
                    step(dve.scalar_tensor_tensor(s3, s3, SLOPE, s3, ALU.mult, ALU.min))
                    done(dve.tensor_tensor_reduce(s3, s3, far3[:, :, :].rearrange("p r n -> p (r n)"), 1.0, 3e38, ALU.add, ALU.min,
                                                  red[:, 0:1]), "lowest3")
                    dve.wait_ge(ev("exped3"), v + 1)
                    step(dve.tensor_tensor_reduce(w3, w3, cnt3[:, :, :].rearrange("p r n -> p (r n)"), 1.0, 0.0, ALU.mult, ALU.add,
                                                  red[:, 1:2]))
                    step(dve.tensor_scalar(red[:, 1:2], red[:, 1:2], TINY, None, ALU.add))
                    step(dve.reciprocal(red[:, 1:2], red[:, 1:2]))
                    done(dve.tensor_scalar(w3, w3, red[:, 1:2], None, ALU.mult), "weights3")
                if layer == 1:
                    dve.wait_ge(ev("summed3"), H3)
                    dve.wait_ge(ev("ld_L3_gnn_b1"), 16)
                    step(dve.tensor_tensor(cols(tmp[:, 0, :]), two(HP), cols(bias[:, BIAS_SLOT["L3_gnn_b1"], :]), ALU.add))
                    done(dve.tensor_scalar(tmp[:, 1, :], tmp[:, 0, :], 0.0, None, ALU.min), "zmin")
                    dve.wait_ge(ev("elu_exp"), inner(NG))
                    for h in range(2):
                        done(dve.scalar_tensor_tensor(half(tmp[:, 0, :], h), half(tmp[:, 1, :], h), -1.0, half(tmp[:, 0, :], h),
                                                      ALU.add, ALU.max), "ts_src")
                    ts_lo(9)
            residual(2)
            norm_x(4, last=True)

        @block.gpsimd
        def _(pool):
            at = [0]

            def split_to(n):
                while at[0] <= min(n, N - 1):
                    m = at[0]
                    pool.wait_ge(hi_ready, m + 1)
                    k, c = shape_of(m)
                    a = cut(m)
                    pool.tensor_tensor(wlo[:, m % SPLIT, a:k * c], raw[:, m % RAW, a:k * c],
                                       whi[:, m % SPLIT, a:k * c].bitcast(F32), ALU.subtract).then_inc(lo_pool, 1)
                    at[0] += 1

            def spread_vectors(g):
                if g == 0:
                    pool.wait_ge(ev("ld_rows"), 16 * 8)
                else:
                    pool.wait_ge(ev("dots"), g)
                    pool.wait_ge(lo_pool, at[0])
                q = 32 * (g // 2)
                for j in range(2):
                    ins = pool.partition_broadcast(arow(g)[j], G[q:q + 1, 2 + 2 * j + g % 2, :])
                ins.then_inc(ev("abc"), 1)
                pool.wait_ge(ev("abc"), g + 1)

            def power(k):
                pool.wait_ge(ev("variance"), k + 1)
                pool.tensor_tensor(mv[:, 3:4], mv[:, 2:3], neghalf[:, :], ALU.pow).then_inc(ev("rstd"), 1)

            def gat(g0, heads, W1, W2):
                n = W1[0, 0]
                for i in range(heads + 2):
                    for k in range(2):
                        if i < heads:
                            n = W1[i, k]
                            split_to(n + AHEAD)
                    for k in range(2):
                        if i >= 2:
                            n = W2[i - 2, k]
                            split_to(n + AHEAD)
                    if g0 == G0 and i + 1 < heads:
                        spread_vectors(i + 1)

            pool.memset(ident[:, :], 0.0).then_inc(ev("pool_step"), 1)
            pool.memset(ones[:, :], 1.0).then_inc(ev("consts"), 1)
            pool.iota(iota[:, :], pattern=[[1, REL * P]], base=0, channel_multiplier=0).then_inc(ev("consts"), 1)
            pool.iota(iotap[:, :], pattern=[[0, 1]], base=0, channel_multiplier=1).then_inc(ev("consts"), 1)
            pool.memset(neghalf[:, :], -0.5).then_inc(ev("consts"), 1)
            pool.wait_ge(ev("pool_step"), 1)
            pool.affine_select(out=ident[:, :], in_=ident[:, :], compare_op=ALU.not_equal, fill=1.0, base=0,
                               pattern=[[-1, P]], channel_multiplier=1).then_inc(ev("consts"), 1)
            spread_vectors(0)
            gat(G0, H0, L0W1, L0W2)
            power(0)
            for t in range(TYPES):
                for a in range(2):
                    split_to(L1T[t, a] + AHEAD)
            split_to(L1M[3] + 1 + AHEAD)
            for name in ("msg_W2", "agg_W1", "agg_W2", "out_W"):
                for a in range(2):
                    split_to(L1D[name, a] + AHEAD)
            power(1)
            power(2)
            gat(G2, H2, L2W1, L2W2)
            power(3)
            split_to(N - 1)
            power(4)


INPUTS = ["x", "src", "dst", "edge_attr_32", "edge_type_3", "node_type_6",
          "L0_gnn_W1", "L0_gnn_a_src1", "L0_gnn_a_dst1", "L0_gnn_b1", "L0_gnn_W2", "L0_gnn_a_src2", "L0_gnn_a_dst2", "L0_gnn_b2",
          "L1_gnn_W_type", "L1_gnn_b_type", "L1_gnn_msg_W1", "L1_gnn_msg_b1", "L1_gnn_msg_W2", "L1_gnn_msg_b2",
          "L1_gnn_edge_W1", "L1_gnn_edge_b1", "L1_gnn_edge_W2", "L1_gnn_edge_b2", "L1_gnn_agg_W1", "L1_gnn_agg_b1",
          "L1_gnn_agg_W2", "L1_gnn_agg_b2", "L1_gnn_out_W", "L1_gnn_out_b", "L1_gnn_ln_g", "L1_gnn_ln_b",
          "L2_gnn_W1", "L2_gnn_a1_src", "L2_gnn_a1_dst", "L2_gnn_b1", "L2_gnn_W2", "L2_gnn_a2_src", "L2_gnn_a2_dst", "L2_gnn_b2",
          "L3_gnn_W1", "L3_gnn_q1", "L3_gnn_k1", "L3_gnn_b1", "L3_gnn_W2", "L3_gnn_q2", "L3_gnn_k2", "L3_gnn_b2"]


def kernel(**inputs):
    import numpy as np
    import concourse.bacc as bacc
    from concourse.bass_utils import run_bass_kernel_spmd

    nc = bacc.Bacc("TRN2", target_bir_lowering=False, num_devices=1)
    arrays, io = {}, {}
    for name in INPUTS:
        a = np.ascontiguousarray(inputs[name])
        arrays[name + "_dram"] = a
        io[name] = nc.dram_tensor(name + "_dram", a.shape, mybir.dt.from_np(a.dtype), kind="ExternalInput").ap()
    out = nc.dram_tensor("out_dram", (P, D), F32, kind="ExternalOutput").ap()
    build(nc, io, out)
    r = run_bass_kernel_spmd(nc, [arrays], core_ids=[0])
    return r.results[0]["out_dram"]
```

```python
from contextlib import ExitStack

import concourse.bass as bass
from concourse import mybir

F32 = mybir.dt.float32
F32R = mybir.dt.float32r
BF16 = mybir.dt.bfloat16
I32 = mybir.dt.int32
U32 = mybir.dt.uint32
ALU = mybir.AluOpType
ACT = mybir.ActivationFunctionType

P = 128
D = 768
KT = D // P
HALF = D // 2
E = 2048
ET = E // P
EA = 32
H4 = D // 4
TYPES = 6
REL = 3
H0 = 8
H2 = 4
C2 = 512
H3 = 4
C3 = D // H3
SLOPE = 0.2
EPS = 1e-5
TINY = 1e-16
BIG = 1e30
RAW = 4
SPLIT = 4
AHEAD = 3
CHUNK = 3 * D


def build(nc, io, out):
    ctx = ExitStack()
    with ctx:
        def sb(name, shape, dt=F32):
            return ctx.enter_context(nc.sbuf_tensor(name, shape, dt))

        def ps(name):
            return ctx.enter_context(nc.psum_tensor(name, [P, 2, 512], F32))

        def sem(name):
            return ctx.enter_context(nc.semaphore(name))

        chunks = []

        def tiles(w):
            return w.rearrange("(k p) n -> p k n", p=P)

        def add(view):
            chunks.append(view)
            return len(chunks) - 1

        w1, w2 = tiles(io["L0_gnn_W1"]), tiles(io["L0_gnn_W2"])
        L0W1, L0W2 = {}, {}
        for i in range(H0 + 2):
            if i < H0:
                for a in range(2):
                    L0W1[i, a] = add(w1[:, 3 * a:3 * a + 3, i * D:(i + 1) * D])
            if i >= 2:
                for a in range(2):
                    k = (i - 2) * KT + 3 * a
                    L0W2[i - 2, a] = add(w2[:, k:k + 3, :])
        L1T = {}
        for t in range(TYPES):
            wt = tiles(io["L1_gnn_W_type"][t])
            for a in range(2):
                L1T[t, a] = add(wt[:, 3 * a:3 * a + 3, :])
        L1M = [add(tiles(io["L1_gnn_msg_W1"])[:, 3 * a:3 * a + 3, :]) for a in range(4)]
        L1D = {}
        for name in ("msg_W2", "agg_W1", "agg_W2", "out_W"):
            for a in range(2):
                L1D[name, a] = add(tiles(io["L1_gnn_" + name])[:, 3 * a:3 * a + 3, :])
        w1, w2 = tiles(io["L2_gnn_W1"]), tiles(io["L2_gnn_W2"])
        L2W1, L2W2 = {}, {}
        for i in range(H2 + 2):
            if i < H2:
                for a in range(2):
                    L2W1[i, a] = add(w1[:, 3 * a:3 * a + 3, i * C2:(i + 1) * C2])
            if i >= 2:
                for a in range(2):
                    k = (i - 2) * (C2 // P) + 2 * a
                    L2W2[i - 2, a] = add(w2[:, k:k + 2, :])
        L3W = {}
        for layer in (1, 2):
            for r in range(REL):
                wr = tiles(io[f"L3_gnn_W{layer}"][r])
                for a in range(2):
                    L3W[layer, r, a] = add(wr[:, 3 * a:3 * a + 3, :])
        N = len(chunks)
        HALVES = [L0W2[H0 - 1, 1], L1T[TYPES - 1, 1], L1M[3]] + \
                 [L1D[name, 1] for name in ("msg_W2", "agg_W1", "agg_W2", "out_W")] + \
                 [L2W2[H2 - 1, 1], L3W[1, REL - 1, 1], L3W[2, REL - 1, 1]]

        def wait_half(engine, n, h):
            if h == 0:
                engine.wait_ge(ev("first_half"), HALVES.index(n) + 1)
            else:
                engine.wait_ge(used, n + 1)

        raw = sb("raw", [P, RAW, CHUNK])
        whi = sb("whi", [P, SPLIT, CHUNK], F32R)
        wlo = sb("wlo", [P, SPLIT, CHUNK], F32R)
        xT = sb("xT", [P, 2, D], F32R)
        el = sb("el", [P, 4, D], F32R)
        pq = sb("pq", [P, 4, D], F32R)
        oh = sb("oh", [P, 2, 2, P], F32R)
        ohe = sb("ohe", [P, 4, P], F32R)
        X = sb("X", [P, D])
        Hs = sb("Hs", [P, 2, D])
        tmp = sb("tmp", [P, 3, D])
        G = sb("G", [P, 6, D])
        bias = sb("bias", [P, 6, D])
        ident = sb("ident", [P, P])
        ones = sb("ones", [P, P])
        iota = sb("iota", [P, REL * P], I32)
        iotap = sb("iotap", [P, 1], I32)
        cnt3 = sb("cnt3", [P, REL, P])
        far3 = sb("far3", [P, REL, P])
        cnt = sb("cnt", [P, P])
        far = sb("far", [P, P])
        att = sb("att", [P, 4, P])
        biasT = sb("biasT", [P, 64])
        idx = sb("idx", [P, 3, ET], I32)
        nty = sb("nty", [P, 1], I32)
        idf = sb("idf", [P, 2, ET])
        typ = sb("typ", [P, TYPES], U32)
        tyo = sb("tyo", [TYPES, P])
        ew = sb("ew", [P, ET])
        ewhl = sb("ewhl", [P, ET, 2], F32R)
        sew = sb("sew", [P, 1])
        eb2 = sb("eb2", [P, 1])
        alph = sb("alph", [P, 4])
        red = sb("red", [P, 2])
        low3 = sb("low3", [P, 2])
        inv3 = sb("inv3", [P, H3 + 1])
        qk = sb("qk", [P, KT, 8])
        qkn = sb("qkn", [P, 10, REL])
        st = sb("st", [P, 2, 6])
        mv = sb("mv", [P, 4])
        neghalf = sb("neghalf", [P, 1])

        ohk = bias[:, 0:4, :].rearrange("p a b -> p (a b)").bitcast(BF16).rearrange("p (t n) -> p t n", t=ET)
        ohd = bias[:, 4:6, :].rearrange("p a b -> p (a b)")[:, 0:ET * P // 2].bitcast(BF16).rearrange("p (t n) -> p t n", t=ET)
        rows = G[:, :, :].rearrange("p a b -> p (a b)").bitcast(I32)
        rowT = [rows[:, j * E:(j + 1) * E].rearrange("p (m t) -> p t m", t=ET) for j in range(2)]
        ea = bias[:, 1, 0:ET * (EA + 1)].rearrange("p (t c) -> p t c", t=ET)
        eaT = bias[0:EA + 1, 2:5, :].rearrange("p a b -> p (a b)")[:, 0:E]
        ejunk = bias[:, 5, 0:H4]
        eW1 = bias[0:EA + 1, 5, D - 2 * H4:D - H4]
        eW2 = bias[:, 5, D - H4:D]
        bst = Hs[0:64, 1, P:2 * P]
        tyr = Hs[0:TYPES, 1, 0:P].bitcast(I32)
        bty = G[0:TYPES, 0, :]
        junk = tmp[:, 2, :]
        diag, sc, wt, wtT = (att[:, j, :] for j in range(4))

        HP, AC, TP, SB = (ps(name) for name in ("HP", "AC", "TP", "SB"))

        def two(pair):
            return pair[:, :, 0:HALF]

        def hidden_bank(n):
            return (AC, TP)[n // 2 % 2][:, n % 2, :]

        def cols(buf):
            return buf.rearrange("p (h n) -> p h n", h=2)

        def half(buf, h):
            return buf[:, h * HALF:(h + 1) * HALF]

        raw_landed = [sem(f"raw_landed{i}") for i in range(RAW)]
        hi_ready = sem("hi_ready")
        lo_dve = sem("lo_dve")
        lo_pool = sem("lo_pool")
        used = sem("used")
        made = {}

        def ev(name):
            if name not in made:
                made[name] = sem(name)
            return made[name]

        RN = REL * P

        def by_parity(buf, v):
            return buf[:, v % 2 * RN:(v % 2 + 1) * RN]

        def diag3(v):
            return by_parity(tmp[:, 1, :], v)

        def score3(v):
            return by_parity(Hs[:, 1, :], v)

        def weight3(v):
            return by_parity(tmp[:, 2, :], v)

        def weight3_T(v):
            return by_parity(Hs[:, 0, :], v)

        def bank3(v, j):
            return (SB, AC)[v % 2][:, j, 0:RN]

        G0, G0F, G2, G2F = 0, H0, H0 + 1, H0 + 1 + H2
        NG = G2F + 1

        def width(g):
            return C2 if G2 <= g < G2F else D

        def inner(g):
            return g if g <= G0F else g - 1

        def arow(g):
            s = 0 if g < G0F else (2 if g % 2 == 0 else 4)
            return [G[:, s + j, 0:width(g)] for j in range(2)]

        def hbuf(g):
            return Hs[:, g % 2, 0:width(g)]

        def elbuf(g, j):
            return el[:, 2 * (g % 2) + j, 0:width(g)]

        def shape_of(n):
            _, k, c = chunks[n].shape
            return k, c

        def cut(n):
            k, c = shape_of(n)
            return k * c * 11 // 18 // 64 * 64

        def w_of(buf, n):
            k, c = shape_of(n)
            return buf[:, n % SPLIT, 0:k * c].rearrange("p (k c) -> p k c", k=k)

        block = ctx.enter_context(nc.Block())

        BIAS_SLOT = {"L0_gnn_b2": 0, "L1_gnn_msg_b1": 1, "L1_gnn_msg_b2": 2, "L1_gnn_agg_b1": 3,
                     "L1_gnn_agg_b2": 4, "L1_gnn_out_b": 5, "L1_gnn_ln_g": 2, "L1_gnn_ln_b": 0,
                     "L2_gnn_b2": 1, "L3_gnn_b2": 4, "L3_gnn_b1": 3}

        def bc(v):
            return v.partition_broadcast(P)

        @block.sync
        def _(sp):
            def chunk(n):
                if n >= RAW:
                    sp.wait_ge(lo_dve, n - RAW + 1)
                    sp.wait_ge(lo_pool, n - RAW + 1)
                k, c = shape_of(n)
                sp.dma_start(raw[:, n % RAW, 0:k * c].rearrange("p (k c) -> p k c", k=k), chunks[n])\
                  .then_inc(raw_landed[n % RAW], 16)

            def load_bias(name):
                sp.dma_start(bias[:, BIAS_SLOT[name], :], bc(io[name])).then_inc(ev("ld_" + name), 16)

            def load_arow(g, a, b):
                src, dst = arow(g)
                sp.dma_start(src, bc(a)).then_inc(ev(f"arow{g}"), 16)
                sp.dma_start(dst, bc(b)).then_inc(ev(f"arow{g}"), 16)

            sp.dma_start(X[:, :], io["x"]).then_inc(ev("ld_x"), 16)
            for n in range(N):
                chunk(n)
                if n == 0:
                    for j, name in enumerate(("L0_gnn_a_src1", "L0_gnn_a_dst1")):
                        for q in range(4):
                            sp.dma_start(G[32 * q:32 * q + 1, 2 + 2 * j:4 + 2 * j, :], io[name][2 * q:2 * q + 2, :])\
                               .then_inc(ev("ld_rows"), 16)
                if n == L0W1[1, 1]:
                    sp.dma_start(tyr, io["node_type_6"].partition_broadcast(TYPES)).then_inc(ev("ld_tyr"), 16)
                    sp.dma_start(eW1[0:EA, :], io["L1_gnn_edge_W1"]).then_inc(ev("ld_edge"), 16)
                    sp.dma_start(eW1[EA:EA + 1, :], io["L1_gnn_edge_b1"].rearrange("(a n) -> a n", a=1)).then_inc(ev("ld_edge"), 16)
                    sp.dma_start(eW2, bc(io["L1_gnn_edge_W2"].rearrange("n a -> (n a)"))).then_inc(ev("ld_edge"), 16)
                    sp.dma_start(eb2[:, :], bc(io["L1_gnn_edge_b2"])).then_inc(ev("ld_edge"), 16)
                    sp.dma_start(bst[0:H0 * KT, :], io["L0_gnn_b1"].rearrange("(a n) -> a n", n=P)).then_inc(ev("ld_edge"), 16)
                    sp.dma_start(bst[H0 * KT:64, :], io["L2_gnn_b1"].rearrange("(a n) -> a n", n=P)).then_inc(ev("ld_edge"), 16)
                    sp.dma_start(qk[:, :, 0:H3], tiles(io["L3_gnn_q1"])).then_inc(ev("ld_qk"), 16)
                    sp.dma_start(qk[:, :, H3:2 * H3], tiles(io["L3_gnn_k1"])).then_inc(ev("ld_qk"), 16)
                if n == L0W1[2, 1]:
                    sp.wait_ge(ev("counted"), 1)
                    sp.dma_start(ea[:, :, 0:EA], io["edge_attr_32"].rearrange("(p t) c -> p t c", t=ET)).then_inc(ev("ld_ea"), 16)
                    load_bias("L0_gnn_b2")
                if n == L0W2[7, 0]:
                    sp.wait_ge(ev("abc"), H0)
                    load_arow(G0F, io["L0_gnn_a_src2"][0], io["L0_gnn_a_dst2"][0])
                if n == L1T[0, 0]:
                    sp.wait_ge(ev("dots"), H0)
                    sp.dma_start(bty, io["L1_gnn_b_type"]).then_inc(ev("ld_bty"), 16)
                    load_bias("L1_gnn_msg_b1")
                if n == L1T[0, 1]:
                    load_bias("L1_gnn_out_b")
                    sp.wait_ge(ev("x_biased"), 1)
                    load_bias("L1_gnn_ln_b")
                if n == L1T[3, 0]:
                    load_bias("L1_gnn_agg_b2")
                if n == L1T[4, 0]:
                    load_bias("L1_gnn_msg_b2")
                if n == L1T[5, 0]:
                    load_bias("L1_gnn_agg_b1")
                if n == L1T[5, 1]:
                    sp.wait_ge(ev("dots"), G0F + 1)
                    sp.wait_ge(ev("type_bias"), 1)
                    sp.dma_start(rows[:, 0:E], bc(io["src"])).then_inc(ev("rows"), 16)
                    sp.dma_start(rows[:, E:2 * E], bc(io["dst"])).then_inc(ev("rows"), 16)
                if n == L1D["out_W", 0]:
                    sp.wait_ge(ev("ts_src"), 2 * 4)
                    load_bias("L1_gnn_ln_g")
                if n == L2W1[0, 0]:
                    sp.wait_ge(ev("oh_made"), ET)
                    for g in (G2, G2 + 1):
                        load_arow(g, io["L2_gnn_a1_src"][g - G2], io["L2_gnn_a1_dst"][g - G2])
                    sp.wait_ge(ev("ts_src"), 2 * 4)
                    load_bias("L2_gnn_b2")
                    load_bias("L3_gnn_b2")
                if n == L2W1[2, 1]:
                    sp.wait_ge(ev("dots"), G2 + 1)
                    g = G2 + 2
                    load_arow(g, io["L2_gnn_a1_src"][g - G2], io["L2_gnn_a1_dst"][g - G2])
                if n == L2W1[3, 1]:
                    sp.wait_ge(ev("dots"), G2 + 2)
                    g = G2 + 3
                    load_arow(g, io["L2_gnn_a1_src"][g - G2], io["L2_gnn_a1_dst"][g - G2])
                if n == L2W2[2, 0]:
                    sp.wait_ge(ev("dots"), G2 + 3)
                    load_arow(G2F, io["L2_gnn_a2_src"][0], io["L2_gnn_a2_dst"][0])
                    load_bias("L3_gnn_b1")
            sp.wait_ge(ev("dots"), NG)
            sp.dma_start(G[:, 4, :], bc(io["L3_gnn_q2"].rearrange("d a -> (d a)"))).then_inc(ev("qk2"), 16)
            sp.dma_start(G[:, 5, :], bc(io["L3_gnn_k2"].rearrange("d a -> (d a)"))).then_inc(ev("qk2"), 16)
            sp.wait_ge(ev("normed"), 2)
            sp.dma_start(out, X[:, :]).then_inc(ev("stored"), 16)
            sp.wait_ge(ev("stored"), 16)

        @block.tensor
        def _(pe):
            def wait_chunk(n):
                pe.wait_ge(hi_ready, n + 1)
                pe.wait_ge(lo_dve, n + 1)
                pe.wait_ge(lo_pool, n + 1)

            def dense(outs, left, n, kts, start, stop):
                wait_chunk(n)
                k, c = shape_of(n)
                hi, lo = w_of(whi, n), w_of(wlo, n)
                for i, (o, (a, b)) in enumerate(outs):
                    if i == 1 and n in HALVES:
                        last.then_inc(ev("first_half"), 1)
                    for j, kt in enumerate(kts):
                        for m, (x, w) in enumerate(((left(0, kt), hi), (left(0, kt), lo), (left(1, kt), hi))):
                            last = pe.matmul(o, x, w[:, j, a:b], start=start and j == 0 and m == 0,
                                             stop=stop and j == k - 1 and m == 2)
                last.then_inc(used, 1)

            def left_x(i, kt):
                return xT[:, i, kt * P:(kt + 1) * P]

            def halves(pair):
                return [(pair[:, h, 0:HALF], (h * HALF, (h + 1) * HALF)) for h in range(2)]

            def product(pair, ns, k=None):
                for a, n in enumerate(ns):
                    if k is not None:
                        xt_ready(k, a)
                    dense(halves(pair), left_x, n, range(3 * a, 3 * a + 3), a == 0, a == 1)

            def transposes(k, src):
                for h in range(2):
                    if k == 0:
                        pe.wait_ge(ev("ld_x"), 16)
                    else:
                        pe.wait_ge(ev("ts_src"), 2 * (k - 1) + h + 1)
                    for j in range(3):
                        c = (3 * h + j) * P
                        last = pe.transpose(TP[:, h, j * P:(j + 1) * P], src[:, c:c + P], ident[:, :])
                    last.then_inc(ev("ts_out"), 1)

            def xt_ready(k, h):
                pe.wait_ge(ev("ts_hi"), 2 * k + h + 1)
                pe.wait_ge(ev("ts_lo"), 2 * k + h + 1)

            def w1(g, a, n):
                if a == 0 and g > 0:
                    pe.wait_ge(ev("h_out"), inner(g))
                if g in (G0, G2):
                    xt_ready(0 if g == G0 else 7, a)
                o = halves(HP) if width(g) == D else [(HP[:, 0, :], (0, C2))]
                dense(o, left_x, n, range(3 * a, 3 * a + 3), a == 0, a == 1)

            def spread(g):
                pe.wait_ge(ev("diag"), g + 1)
                pe.matmul(SB[:, 0, 0:P], ones[:, :], diag, start=True, stop=True).then_inc(ev("spread"), 1)

            def turn(g):
                pe.wait_ge(ev("weights"), g + 1)
                if g == 0:
                    pe.wait_ge(ev("biasT"), 1)
                pe.transpose(SB[:, 1, 0:P], wt, ident[:, :]).then_inc(ev("turned"), 1)

            def aggregate_T(g):
                pe.wait_ge(ev("turned_out"), g + 1)
                if inner(g) > 0:
                    pe.wait_ge(ev("z"), inner(g))
                for k in range(width(g) // P):
                    last = pe.matmul(TP[:, k // 3, (k % 3) * P:(k % 3 + 1) * P],
                                     hbuf(g)[:, k * P:(k + 1) * P], wtT, start=True, stop=True)
                last.then_inc(ev("summed"), 1)

            def w2(g, a, n, first, final):
                if a == 0 and g == 0:
                    pe.wait_ge(ev("ew_dot"), ET // 2)
                if a == 0:
                    pe.wait_ge(ev("el_hi"), inner(g) + 1)
                    pe.wait_ge(ev("el_lo"), inner(g) + 1)
                k, _ = shape_of(n)

                def left(i, kt):
                    return elbuf(g, i)[:, kt * P:(kt + 1) * P]
                dense(halves(AC), left, n, range(k * a, k * a + k), first and a == 0, final and a == 1)

            def gat(g0, heads, W1, W2):
                for i in range(heads + 2):
                    g = g0 + i
                    if i == heads:
                        turn(g - 1)
                        w2(g - 2, 0, W2[i - 2, 0], False, False)
                        aggregate_T(g - 1)
                        w2(g - 2, 1, W2[i - 2, 1], False, False)
                        continue
                    if i < heads:
                        w1(g, 0, W1[i, 0])
                    if 1 <= i <= heads:
                        turn(g - 1)
                    if i < heads:
                        w1(g, 1, W1[i, 1])
                    if 1 <= i <= heads:
                        aggregate_T(g - 1)
                    if g == 0:
                        pe.wait_ge(ev("ld_edge"), 16 * 6)
                        pe.transpose(SB[:, 1, 0:64], bst, ident[0:64, 0:64]).then_inc(ev("bst"), 1)
                        count_edges()
                    if g == 1:
                        spread(g)
                        edge_hidden()
                    if i >= 2:
                        w2(g - 2, 0, W2[i - 2, 0], i == 2, i == heads + 1)
                    if g != 1 and i < heads:
                        spread(g)
                    if i >= 2:
                        w2(g - 2, 1, W2[i - 2, 1], i == 2, i == heads + 1)
                g = g0 + heads
                spread(g)
                turn(g)
                pe.wait_ge(ev("turned_out"), g + 1)
                pe.wait_ge(ev("final_out"), 2 if g == G0F else 4)
                for h in range(2):
                    pe.matmul(HP[:, h, 0:HALF], wtT, half(hbuf(g), h), start=True, stop=True)\
                      .then_inc(ev("summed_h"), 1)

            def count_edges():
                pe.wait_ge(ev("onehots"), 3)
                for t in range(ET):
                    last = pe.matmul(AC[:, 0, 0:REL * P], ohd[:, t, :], ohk[:, t, :], start=t == 0, stop=t == ET - 1)
                last.then_inc(ev("counted"), 1)

            def edge_hidden():
                pe.wait_ge(ev("ea_ones"), 1)
                pe.wait_ge(ev("ld_ea"), 16)
                pe.wait_ge(ev("turned_out"), 1)
                pe.wait_ge(ev("scored"), 2)
                pe.wait_ge(ev("cnt_out"), 1)
                for q in range(2):
                    if q:
                        pe.wait_ge(ev("ea_out"), 1)
                    for j in range(8):
                        last = pe.transpose(SB[0:EA + 1, j // 4, (j % 4) * P:(j % 4 + 1) * P], ea[:, 8 * q + j, :], ident[:, :])
                    last.then_inc(ev("ea_T"), 1)
                pe.wait_ge(ev("z"), 1)
                for n in range(ET // 2):
                    if n == 4:
                        pe.wait_ge(ev("ea_out"), 2)
                    if n >= 4:
                        pe.wait_ge(ev("ew_dot"), n - 3)
                    for m in range(2):
                        last = pe.matmul(hidden_bank(n)[:, m * H4:(m + 1) * H4], eaT[:, (2 * n + m) * P:(2 * n + m + 1) * P],
                                         eW1, start=True, stop=True)
                    last.then_inc(ev("edge_hidden"), 1)

            def xr_T(r):
                pe.wait_ge(ev("xr_out"), r + 1)
                for k in range(KT):
                    last = pe.transpose(TP[:, k // 3, (k % 3) * P:(k % 3 + 1) * P], G[:, r, k * P:(k + 1) * P], ident[:, :])
                last.then_inc(ev("xrT"), 1)

            def xr_scores(r):
                pe.wait_ge(ev("xrT_out"), r + 1)
                for k in range(KT):
                    last = pe.matmul(AC[:, 0, r * 8:(r + 1) * 8], G[:, 3, k * P:(k + 1) * P], qk[:, k, :],
                                     start=k == 0, stop=k == KT - 1)
                last.then_inc(ev("qk_dot"), 1)

            def spread3(v):
                pe.wait_ge(ev("diag3"), v + 1)
                if v >= 2:
                    pe.wait_ge(ev("scored3"), v - 1)
                pe.matmul(bank3(v, 0), ones[:, :], diag3(v), start=True, stop=True).then_inc(ev("spread3"), 1)

            def turn3(v):
                pe.wait_ge(ev("weights3"), v + 1)
                for r in range(REL):
                    last = pe.transpose(bank3(v, 1)[:, r * P:(r + 1) * P], weight3(v)[:, r * P:(r + 1) * P], ident[:, :])
                last.then_inc(ev("turned3"), 1)

            def sum3(v):
                pe.wait_ge(ev("turned3_out"), v + 1)
                h, c = v // 2, (v % 2) * C3
                for r in range(REL):
                    last = pe.matmul(HP[:, h, c:c + C3], weight3_T(v)[:, r * P:(r + 1) * P],
                                     G[:, r, v * C3:(v + 1) * C3], start=r == 0, stop=r == REL - 1)
                last.then_inc(ev("summed3"), 1)

            pe.wait_ge(ev("consts"), 5)
            transposes(0, X)
            gat(G0, H0, L0W1, L0W2)
            transposes(1, X)
            for t in range(TYPES):
                if t >= 2:
                    pe.wait_ge(ev("chosen"), t - 1)
                if t == 2:
                    pe.wait_ge(ev("ld_bty"), 16)
                    pe.wait_ge(ev("tyo"), 1)
                    for h in range(2):
                        last = pe.matmul(AC[:, h, 0:HALF], tyo[:, :], half(bty, h), start=True, stop=True)
                    last.then_inc(ev("type_bias"), 1)
                product((HP, SB)[t % 2], [L1T[t, a] for a in range(2)], 1 if t == 0 else None)
            transposes(2, Hs[:, 1, :])
            pe.wait_ge(ev("chosen"), TYPES - 1)
            product(HP, L1M[0:2], 2)
            product(SB, L1M[2:4])
            for t in range(ET + 2):
                if t < ET:
                    pair = (HP, SB)[t % 2]
                    pe.wait_ge(ev("oh_made"), t + 1)
                    if t >= 2:
                        pe.wait_ge(ev("relu_out"), t - 1)
                    for h in range(2):
                        if t == 0:
                            pe.wait_ge(ev("pq_hi"), 2 + h)
                            pe.wait_ge(ev("pq_lo"), 2 + h)
                        for m in range(4):
                            last = pe.matmul(pair[:, h, 0:HALF], oh[:, t % 2, m // 2, :],
                                             half(pq[:, m, :], h), start=m == 0, stop=m == 3)
                    last.then_inc(ev("gathered"), 1)
                if t >= 2:
                    s = t - 2
                    pe.wait_ge(ev("r_hi"), s + 1)
                    pe.wait_ge(ev("r_lo"), s + 1)
                    for h in range(2):
                        for m in range(2):
                            last = pe.matmul(AC[:, h, 0:HALF], ohe[:, s % 4, :], half(el[:, 2 * (s % 2) + m, :], h),
                                             start=s == 0 and m == 0, stop=s == ET - 1 and m == 1)
                    last = pe.matmul(TP[:, 0, HALF:HALF + 2], ohe[:, s % 4, :], ewhl[:, s, :],
                                     start=s == 0, stop=s == ET - 1)
                    last.then_inc(ev("scattered"), 1)
            for j, name in enumerate(("msg_W2", "agg_W1", "agg_W2", "out_W")):
                transposes(3 + j, tmp[:, j % 2, :])
                product(HP, [L1D[name, a] for a in range(2)], 3 + j)
            transposes(7, X)
            gat(G2, H2, L2W1, L2W2)
            transposes(8, X)
            pe.wait_ge(ev("ld_qk"), 32)
            for r in range(REL):
                if r == 2:
                    pe.wait_ge(ev("xr_out"), 1)
                product((HP, SB)[r % 2], [L3W[1, r, a] for a in range(2)], 8 if r == 0 else None)
                if r >= 1:
                    if r == 2:
                        xr_scores(0)
                    xr_T(r - 1)
            xr_scores(1)
            xr_T(2)
            xr_scores(2)
            spread3(0)
            spread3(1)
            for v in range(H3):
                turn3(v)
                if v + 2 < H3:
                    spread3(v + 2)
                sum3(v)
            transposes(9, tmp[:, 0, :])
            for r in range(REL):
                if r == 2:
                    pe.wait_ge(ev("xr_out"), REL + 1)
                product((HP, SB)[r % 2], [L3W[2, r, a] for a in range(2)], 9 if r == 0 else None)
            spread3(H3)
            turn3(H3)
            pe.wait_ge(ev("turned3_out"), H3 + 1)
            for h in range(2):
                for r in range(REL):
                    last = pe.matmul(HP[:, h, 0:HALF], weight3_T(H3)[:, r * P:(r + 1) * P],
                                     half(G[:, r, :], h), start=r == 0, stop=r == REL - 1)
                last.then_inc(ev("summed_h"), 1)

        @block.scalar
        def _(act):
            at = [0]

            def split_to(n):
                while at[0] <= min(n, N - 1):
                    m = at[0]
                    act.wait_ge(raw_landed[m % RAW], 16 * (m // RAW + 1))
                    if m >= SPLIT:
                        act.wait_ge(used, m - SPLIT + 1)
                    k, c = shape_of(m)
                    act.activation(whi[:, m % SPLIT, 0:k * c], raw[:, m % RAW, 0:k * c], ACT.Copy).then_inc(hi_ready, 1)
                    at[0] += 1

            def ts_hi(k, func=ACT.Copy):
                for h in range(2):
                    act.wait_ge(ev("ts_out"), 2 * k + h + 1)
                    act.activation(half(xT[:, 0, :], h), TP[:, h, 0:HALF], func).then_inc(ev("ts_hi"), 1)

            def expo(g):
                act.wait_ge(ev("lowest"), g + 1)
                act.activation(wt, sc, ACT.Exp, bias=red[:, 0:1], scale=-1.0).then_inc(ev("exped"), 1)

            def turned_out(g):
                act.wait_ge(ev("turned"), g + 1)
                act.activation(wtT, SB[:, 1, 0:P], ACT.Copy).then_inc(ev("turned_out"), 1)

            def h_out(g, n):
                if g not in (G0F, G2F):
                    act.wait_ge(used, n + 1)
                if g == 1:
                    act.wait_ge(ev("tyo"), 1)
                if inner(g) >= 2:
                    act.wait_ge(ev("summed"), inner(g) - 1)
                if g in (G0F, G2F):
                    for h in range(2):
                        wait_half(act, n, h)
                        act.activation(half(hbuf(g), h), AC[:, h, 0:HALF], ACT.Copy).then_inc(ev("final_out"), 1)
                    return
                o, i = (cols(hbuf(g)), two(HP)) if width(g) == D else (hbuf(g), HP[:, 0, :])
                act.activation(o, i, ACT.Copy).then_inc(ev("h_out"), 1)

            def elu_exp(g):
                act.wait_ge(ev("zmin"), inner(g) + 1)
                c = width(g)
                act.activation(tmp[:, 1, 0:c], tmp[:, 1, 0:c], ACT.Exp).then_inc(ev("elu_exp"), 1)

            def el_hi(g):
                act.wait_ge(ev("elu"), inner(g) + 1)
                act.activation(elbuf(g, 0), tmp[:, 0, 0:width(g)], ACT.Copy).then_inc(ev("el_hi"), 1)

            def gat(g0, heads, W1, W2):
                n = W1[0, 0]
                for i in range(heads + 2):
                    g = g0 + i
                    if i == heads:
                        turned_out(g - 1)
                        split_to(W2[i - 2, 0] + AHEAD)
                        elu_exp(g - 1)
                        el_hi(g - 1)
                        split_to(W2[i - 2, 1] + AHEAD)
                        continue
                    if i < heads:
                        n = W1[i, 0]
                        split_to(n + AHEAD)
                    if 1 <= i <= heads:
                        turned_out(g - 1)
                    if i < heads:
                        n = W1[i, 1]
                        split_to(n + AHEAD)
                        h_out(g, n)
                    if g == 0:
                        act.wait_ge(ev("bst"), 1)
                        act.activation(biasT[:, :], SB[:, 1, 0:64], ACT.Copy).then_inc(ev("biasT"), 1)
                    if i >= 2:
                        n = W2[i - 2, 0]
                        split_to(n + AHEAD)
                    if 1 <= i <= heads:
                        elu_exp(g - 1)
                    if i < heads:
                        expo(g)
                    if i == heads - 1:
                        el_hi(g - 1)
                    if i >= 2:
                        n = W2[i - 2, 1]
                        split_to(n + AHEAD)
                    if 1 <= i < heads - 1:
                        el_hi(g - 1)
                    if g == 1:
                        edge_weights()
                g = g0 + heads
                h_out(g, n)
                expo(g)
                turned_out(g)
                split_to(n + 1 + AHEAD)

            def xrT_out(r):
                act.wait_ge(ev("xrT"), r + 1)
                if r:
                    act.wait_ge(ev("qk_dot"), r)
                act.activation(cols(G[:, 3, :]), two(TP), ACT.Copy).then_inc(ev("xrT_out"), 1)

            def exp3(v):
                act.wait_ge(ev("lowest3"), v + 1)
                if v >= 2:
                    act.wait_ge(ev("turned3"), v - 1)
                act.activation(weight3(v), score3(v), ACT.Exp, bias=low3[:, v % 2:v % 2 + 1], scale=-1.0).then_inc(ev("exped3"), 1)

            def turned3_out(v):
                act.wait_ge(ev("turned3"), v + 1)
                if v >= 2:
                    act.wait_ge(ev("summed3"), v - 1)
                act.activation(weight3_T(v), bank3(v, 1), ACT.Copy).then_inc(ev("turned3_out"), 1)

            for j, name in enumerate(("dst", "src", "edge_type_3")):
                act.dma_start(idx[:, j, :], io[name].rearrange("(p t) -> p t", t=ET)).then_inc(ev("ld_idx"), 16)
            act.dma_start(nty[:, :], io["node_type_6"].rearrange("(p a) -> p a", a=1)).then_inc(ev("ld_idx"), 16)
            def edge_weights():
                for q in range(2):
                    act.wait_ge(ev("ea_T"), q + 1)
                    act.activation(eaT[:, q * 8 * P:(q + 1) * 8 * P].rearrange("p (a n) -> p a n", a=2), SB[0:EA + 1, :, :], ACT.Copy).then_inc(ev("ea_out"), 1)
                act.wait_ge(ev("ew_dot"), ET // 2)
                act.wait_ge(ev("eb2_neg"), 1)
                act.activation(ew[:, :], ew[:, :], ACT.Exp, bias=eb2[:, 0:1], scale=-1.0).then_inc(ev("ew_exp"), 1)

            ts_hi(0)
            gat(G0, H0, L0W1, L0W2)
            ts_hi(1)
            for t in range(TYPES):
                for a in range(2):
                    split_to(L1T[t, a] + AHEAD)
                if t == 0:
                    act.wait_ge(ev("ew_done"), 1)
                    act.activation(ewhl[:, :, 0], ew[:, :], ACT.Copy).then_inc(ev("ew_hi"), 1)
            ts_hi(2)
            for a in range(2):
                split_to(L1M[a] + AHEAD)
            act.wait_ge(used, L1M[1] + 1)
            act.activation(cols(pq[:, 0, :]), two(HP), ACT.Copy).then_inc(ev("pq_hi"), 1)
            for a in range(2, 4):
                split_to(L1M[a] + AHEAD)
            for h in range(2):
                act.wait_ge(ev("q_sum"), h + 1)
                act.activation(half(pq[:, 2, :], h), half(tmp[:, 2, :], h), ACT.Copy).then_inc(ev("pq_hi"), 1)
            for t in range(ET):
                act.wait_ge(ev("gathered"), t + 1)
                if t >= 2:
                    act.wait_ge(ev("r_lo"), t - 1)
                act.activation(cols(tmp[:, t % 2, :]), two((HP, SB)[t % 2]), ACT.Relu, scale=ew[:, t:t + 1])\
                   .then_inc(ev("relu_out"), 1)
                act.wait_ge(ev("relu_out"), t + 1)
                if t >= 2:
                    act.wait_ge(ev("scattered"), t - 1)
                act.activation(el[:, 2 * (t % 2), :], tmp[:, t % 2, :], ACT.Copy).then_inc(ev("r_hi"), 1)
                if t % 4 == 3:
                    split_to(L1M[3] + 1 + min(t // 4, AHEAD))
            split_to(L1M[3] + 1 + AHEAD)
            for j, name in enumerate(("msg_W2", "agg_W1", "agg_W2", "out_W")):
                ts_hi(3 + j, ACT.Relu if j == 2 else ACT.Copy)
                for a in range(2):
                    split_to(L1D[name, a] + AHEAD)
            split_to(L1D["out_W", 1] + 1 + AHEAD)
            ts_hi(7)
            gat(G2, H2, L2W1, L2W2)
            ts_hi(8)
            for r in range(REL):
                for a in range(2):
                    split_to(L3W[1, r, a] + AHEAD)
                act.wait_ge(used, L3W[1, r, 1] + 1)
                if r == 0:
                    act.wait_ge(ev("dots"), NG)
                act.activation(cols(G[:, r, :]), two((HP, SB)[r % 2]), ACT.Copy).then_inc(ev("xr_out"), 1)
                if r >= 1:
                    xrT_out(r - 1)
            xrT_out(2)
            split_to(L3W[1, 2, 1] + AHEAD + 1)
            exp3(0)
            exp3(1)
            for v in range(H3):
                turned3_out(v)
                if v + 2 < H3:
                    exp3(v + 2)
            for h in range(2):
                act.wait_ge(ev("zmin3"), h + 1)
                act.activation(half(tmp[:, 1, :], h), half(tmp[:, 1, :], h), ACT.Exp).then_inc(ev("elu_exp3"), 1)
            ts_hi(9)
            for r in range(REL):
                for a in range(2):
                    split_to(L3W[2, r, a] + AHEAD)
                act.wait_ge(used, L3W[2, r, 1] + 1)
                act.activation(cols(G[:, r, :]), two((HP, SB)[r % 2]), ACT.Copy).then_inc(ev("xr_out"), 1)
            exp3(H3)
            turned3_out(H3)

        @block.vector
        def _(dve):
            at = [0]
            count = {}

            def done(ins, name, by=1):
                count[name] = count.get(name, 0) + by
                ins.then_inc(ev(name), by)
                dve.wait_ge(ev(name), count[name])

            def step(ins):
                done(ins, "vector_step")

            def split_to(n):
                while at[0] <= min(n, N - 1):
                    m = at[0]
                    dve.wait_ge(hi_ready, m + 1)
                    c = cut(m)
                    dve.tensor_tensor(wlo[:, m % SPLIT, 0:c], raw[:, m % RAW, 0:c],
                                      whi[:, m % SPLIT, 0:c].bitcast(F32), ALU.subtract).then_inc(lo_dve, 1)
                    at[0] += 1

            def ts_lo(k, relu=False):
                for h in range(2):
                    dve.wait_ge(ev("ts_hi"), 2 * k + h + 1)
                    hi = half(xT[:, 0, :], h).bitcast(F32)
                    if relu:
                        ins = dve.scalar_tensor_tensor(half(xT[:, 1, :], h), TP[:, h, 0:HALF], 0.0, hi, ALU.max, ALU.subtract)
                    else:
                        ins = dve.tensor_tensor(half(xT[:, 1, :], h), TP[:, h, 0:HALF], hi, ALU.subtract)
                    ins.then_inc(ev("ts_lo"), 1)

            def dots(g):
                if g < G0F:
                    dve.wait_ge(ev("abc"), g + 1)
                else:
                    dve.wait_ge(ev(f"arow{g}"), 32)
                c = width(g)
                if g in (G0F, G2F):
                    for h in range(2):
                        dve.wait_ge(ev("final_out"), (2 if g == G2F else 0) + h + 1)
                        for j in range(2):
                            step(dve.tensor_tensor_reduce(half(junk, h), half(hbuf(g), h), half(arow(g)[j], h), 1.0, 0.0,
                                                          ALU.mult, ALU.add, alph[:, 2 * h + j:2 * h + j + 1]))
                    done(dve.tensor_tensor(alph[:, 0:2], alph[:, 0:2], alph[:, 2:4], ALU.add), "dots")
                    dve.wait_ge(ev("spread"), g)
                    dve.tensor_scalar(diag, ident[:, :], alph[:, 0:1], None, ALU.mult).then_inc(ev("diag"), 1)
                    return
                dve.wait_ge(ev("h_out"), inner(g) + 1)
                for j in range(2):
                    ins = dve.tensor_tensor_reduce(junk[:, 0:c], hbuf(g), arow(g)[j], 1.0, 0.0, ALU.mult, ALU.add,
                                                   alph[:, j:j + 1])
                    if j:
                        done(ins, "dots")
                    else:
                        step(ins)
                if g:
                    dve.wait_ge(ev("spread"), g)
                dve.tensor_scalar(diag, ident[:, :], alph[:, 0:1], None, ALU.mult).then_inc(ev("diag"), 1)

            def scores(g):
                dve.wait_ge(ev("spread"), g + 1)
                done(dve.tensor_scalar(sc, SB[:, 0, 0:P], -1.0, alph[:, 1:2], ALU.mult, ALU.subtract), "scored")
                step(dve.scalar_tensor_tensor(sc, sc, SLOPE, sc, ALU.mult, ALU.min))
                done(dve.tensor_tensor_reduce(sc, sc, far[:, :], 1.0, 3e38, ALU.add, ALU.min, red[:, 0:1]), "lowest")

            def weights(g):
                dve.wait_ge(ev("exped"), g + 1)
                total = dve.tensor_tensor_reduce(wt, wt, cnt[:, :], 1.0, 0.0, ALU.mult, ALU.add, red[:, 1:2])
                if g in (G0F, G2F):
                    done(total, "weights")
                else:
                    step(total)
                if g >= G2:
                    step(dve.tensor_scalar(red[:, 1:2], red[:, 1:2], TINY, None, ALU.add))
                step(dve.reciprocal(red[:, 1:2], red[:, 1:2]))
                if g not in (G0F, G2F):
                    done(dve.tensor_scalar(wt, wt, red[:, 1:2], None, ALU.mult), "weights")

            def elu_in(g):
                dve.wait_ge(ev("summed"), inner(g) + 1)
                if g == 0:
                    dve.wait_ge(ev("biasT"), 1)
                c = width(g)
                for b in range(2):
                    k0, k1 = 3 * b, min(3 * b + 3, c // P)
                    first = (g * KT if g < G0F else H0 * KT + (g - G2) * (C2 // P)) + k0
                    m = k1 - k0
                    ins = dve.tensor_tensor(tmp[:, 0, k0 * P:k1 * P].rearrange("p (k n) -> p k n", k=m),
                                            TP[:, b, 0:m * P].rearrange("p (k n) -> p k n", k=m),
                                            biasT[:, first:first + m].unsqueeze(2).broadcast_to((P, m, P)), ALU.add)
                    if b:
                        done(ins, "z")
                    else:
                        step(ins)
                done(dve.tensor_scalar(tmp[:, 1, 0:c], tmp[:, 0, 0:c], 0.0, None, ALU.min), "zmin")

            def elu_end(g):
                dve.wait_ge(ev("elu_exp"), inner(g) + 1)
                c = width(g)
                done(dve.scalar_tensor_tensor(tmp[:, 0, 0:c], tmp[:, 1, 0:c], -1.0, tmp[:, 0, 0:c], ALU.add, ALU.max), "elu")

            def el_low(g):
                c = width(g)
                dve.wait_ge(ev("el_hi"), inner(g) + 1)
                done(dve.tensor_tensor(elbuf(g, 1), tmp[:, 0, 0:c], elbuf(g, 0).bitcast(F32), ALU.subtract), "el_lo")

            def stats_half(h, src):
                dve.bn_stats(st[:, h, :], half(src, h)).then_inc(ev("vector_step"), 1)
                count["vector_step"] += 1

            def stats_end(k):
                dve.wait_ge(ev("vector_step"), count["vector_step"])
                step(dve.bn_aggr(mv[:, 0:2], st[:, :, :].rearrange("p a b -> p (a b)")))
                done(dve.tensor_scalar(mv[:, 2:3], mv[:, 1:2], EPS, None, ALU.add), "variance")
                dve.wait_ge(ev("rstd"), k + 1)

            def norm_x(k, last=False):
                stats_end(k)
                for h in range(2):
                    ins = dve.tensor_scalar(half(X[:, :], h), half(X[:, :], h), mv[:, 0:1], mv[:, 3:4], ALU.subtract, ALU.mult)
                    if last:
                        done(ins, "normed")
                    else:
                        done(ins, "ts_src")

            def gat(g0, heads, W1, W2, b2, ts, f):
                n = W1[0, 0]
                for i in range(heads + 2):
                    g = g0 + i
                    if i == heads:
                        split_to(W2[i - 2, 0] + AHEAD)
                        elu_in(g - 1)
                        elu_end(g - 1)
                        el_low(g - 1)
                        split_to(W2[i - 2, 1] + AHEAD)
                        continue
                    for k in range(2):
                        if i < heads:
                            n = W1[i, k]
                            split_to(n + AHEAD)
                    if g == 0:
                        edge_counts()
                    if i < heads:
                        dots(g)
                    if 1 <= i <= heads:
                        elu_in(g - 1)
                    if i < heads:
                        scores(g)
                    if i >= 2:
                        n = W2[i - 2, 0]
                        split_to(n + AHEAD)
                    if 1 <= i <= heads:
                        elu_end(g - 1)
                    if i < heads:
                        weights(g)
                    if i == heads - 1:
                        el_low(g - 1)
                    if i >= 2:
                        n = W2[i - 2, 1]
                        split_to(n + AHEAD)
                    if 1 <= i < heads - 1:
                        el_low(g - 1)
                    if g == 1:
                        edge_weights()
                    if i == 2:
                        add_bias(b2, ts)
                g = g0 + heads
                dots(g)
                scores(g)
                weights(g)
                split_to(n + 1 + AHEAD)
                residual(f, red[:, 1:2])

            def add_bias(name, ts):
                dve.wait_ge(ev("ld_" + name), 16)
                dve.wait_ge(ev("ts_out"), 2 * ts + 2)
                done(dve.tensor_tensor(X[:, :], X[:, :], bias[:, BIAS_SLOT[name], :], ALU.add), "x_biased")

            def residual(f, inv):
                for h in range(2):
                    dve.wait_ge(ev("summed_h"), 2 * f + h + 1)
                    step(dve.scalar_tensor_tensor(half(X[:, :], h), HP[:, h, 0:HALF], inv, half(X[:, :], h), ALU.mult, ALU.add))
                    stats_half(h, X[:, :])

            def edge_counts():
                dve.wait_ge(ev("counted"), 1)
                dve.memset(ea[:, :, EA], 1.0).then_inc(ev("ea_ones"), 1)
                done(dve.tensor_copy(cnt3[:, :, :].rearrange("p r n -> p (r n)"), AC[:, 0, 0:REL * P]), "cnt_out")
                step(dve.tensor_scalar(far3[:, :, :], cnt3[:, :, :], 0.5, BIG, ALU.is_lt, ALU.mult))
                step(dve.tensor_tensor(cnt[:, :], ident[:, :], cnt3[:, 0, :], ALU.add))
                for r in range(1, REL):
                    step(dve.tensor_tensor(cnt[:, :], cnt[:, :], cnt3[:, r, :], ALU.add))
                step(dve.tensor_scalar(far[:, :], cnt[:, :], 0.5, BIG, ALU.is_lt, ALU.mult))

            def edge_weights():
                for n in range(ET // 2):
                    dve.wait_ge(ev("edge_hidden"), n + 1)
                    for m in range(2):
                        ins = dve.scalar_tensor_tensor(ejunk, hidden_bank(n)[:, m * H4:(m + 1) * H4], 0.0, eW2,
                                                       ALU.max, ALU.mult, accum_out=ew[:, 2 * n + m:2 * n + m + 1])
                        if m:
                            done(ins, "ew_dot")
                        else:
                            step(ins)
                dve.wait_ge(ev("ew_exp"), 1)
                step(dve.tensor_scalar(ew[:, :], ew[:, :], 1.0, None, ALU.add))
                done(dve.reciprocal(ew[:, :], ew[:, :]), "ew_done")

            def by_rel(buf):
                return buf.rearrange("p (r n) -> p r n", r=REL)

            def scores3(v):
                dve.wait_ge(ev("spread3"), v + 1)
                s, q = score3(v), v if v < H3 else 8
                done(dve.scalar_tensor_tensor(by_rel(s), by_rel(bank3(v, 0)), -1.0,
                                              qkn[:, q, :].unsqueeze(2).broadcast_to((P, REL, P)), ALU.mult, ALU.subtract), "scored3")
                step(dve.scalar_tensor_tensor(s, s, SLOPE, s, ALU.mult, ALU.min))
                done(dve.tensor_tensor_reduce(s, s, far3[:, :, :].rearrange("p r n -> p (r n)"), 1.0, 3e38, ALU.add, ALU.min,
                                              low3[:, v % 2:v % 2 + 1]), "lowest3")

            def weights3(v):
                dve.wait_ge(ev("exped3"), v + 1)
                w, total = weight3(v), inv3[:, v:v + 1]
                done(dve.tensor_tensor_reduce(w, w, cnt3[:, :, :].rearrange("p r n -> p (r n)"), 1.0, 0.0, ALU.mult, ALU.add,
                                              total), "weights3")
                step(dve.tensor_scalar(total, total, TINY, None, ALU.add))
                step(dve.reciprocal(total, total))

            dve.wait_ge(ev("consts"), 5)
            dve.wait_ge(ev("ld_idx"), 16 * 4)
            step(dve.tensor_copy(idf[:, 0, :], idx[:, 0, :]))
            step(dve.scalar_tensor_tensor(idf[:, 1, :], idx[:, 2, :], float(P), idx[:, 1, :], ALU.mult, ALU.add))

            def onehots(o, m, j, t0, t1):
                n = t1 - t0
                dve.tensor_tensor(o[:, t0:t1, :], iota[:, 0:m].unsqueeze(1).broadcast_to((P, n, m)),
                                  idf[:, j, t0:t1].unsqueeze(2).broadcast_to((P, n, m)), ALU.is_equal).then_inc(ev("onehots"), 1)

            onehots(ohd, P, 0, 0, ET)
            ts_lo(0)
            split_to(0)
            onehots(ohk, REL * P, 1, 0, ET // 2)
            split_to(1)
            onehots(ohk, REL * P, 1, ET // 2, ET)
            step(dve.tensor_scalar(typ[:, :], iota[:, 0:TYPES], nty[:, 0:1], None, ALU.is_equal))
            dve.wait_ge(ev("ld_tyr"), 16)
            done(dve.tensor_scalar(tyo[:, :], tyr, iotap[0:TYPES, 0:1], None, ALU.is_equal), "tyo")
            dve.wait_ge(ev("ld_edge"), 16 * 6)
            done(dve.tensor_scalar(eb2[:, :], eb2[:, :], -1.0, None, ALU.mult), "eb2_neg")
            gat(G0, H0, L0W1, L0W2, "L0_gnn_b2", 0, 0)
            norm_x(0)
            ts_lo(1)
            for t in range(TYPES):
                for a in range(2):
                    split_to(L1T[t, a] + AHEAD)
                if t == 1:
                    dve.wait_ge(ev("ew_hi"), 1)
                    step(dve.tensor_tensor(ewhl[:, :, 1], ew[:, :], ewhl[:, :, 0].bitcast(F32), ALU.subtract))
                if t in (2, 3):
                    b = bias[:, BIAS_SLOT[("L1_gnn_out_b", "L1_gnn_ln_b")[t - 2]], :]
                    dve.wait_ge(ev(("ld_L1_gnn_out_b", "ld_L1_gnn_ln_b")[t - 2]), 16)
                    step(dve.tensor_tensor(b, b, X[:, :], ALU.add))
                if t < TYPES - 1:
                    dve.wait_ge(used, L1T[t, 1] + 1)
                    done(dve.copy_predicated(cols(Hs[:, 1, :]), typ[:, t:t + 1].unsqueeze(2).broadcast_to((P, 2, HALF)),
                                             two((HP, SB)[t % 2])), "chosen")
            dve.wait_ge(ev("type_bias"), 1)
            for h in range(2):
                wait_half(dve, L1T[t, 1], h)
                done(dve.copy_predicated(half(Hs[:, 1, :], h), typ[:, t:t + 1].broadcast_to((P, HALF)),
                                         (HP, SB)[t % 2][:, h, 0:HALF]), "chosen_last")
                done(dve.tensor_tensor(half(Hs[:, 1, :], h), half(Hs[:, 1, :], h), AC[:, h, 0:HALF], ALU.add), "ts_src")
            ts_lo(2)
            for a in range(2):
                split_to(L1M[a] + AHEAD)
            dve.wait_ge(ev("pq_hi"), 1)
            dve.tensor_tensor(cols(pq[:, 1, :]), two(HP), cols(pq[:, 0, :].bitcast(F32)), ALU.subtract).then_inc(ev("pq_lo"), 1)
            dve.wait_ge(ev("ts_out"), 6)
            dve.wait_ge(ev("ld_L1_gnn_agg_b2"), 16)
            step(dve.tensor_tensor(Hs[:, 1, :], Hs[:, 1, :], bias[:, BIAS_SLOT["L1_gnn_agg_b2"], :], ALU.add))
            for a in range(2, 4):
                split_to(L1M[a] + AHEAD)
            dve.wait_ge(ev("ld_L1_gnn_msg_b1"), 16)
            for h in range(2):
                wait_half(dve, L1M[3], h)
                done(dve.tensor_tensor(half(tmp[:, 2, :], h), SB[:, h, 0:HALF], half(bias[:, BIAS_SLOT["L1_gnn_msg_b1"], :], h),
                                       ALU.add), "q_sum")
            for h in range(2):
                dve.wait_ge(ev("pq_hi"), 2 + h)
                dve.tensor_tensor(half(pq[:, 3, :], h), half(tmp[:, 2, :], h), half(pq[:, 2, :], h).bitcast(F32), ALU.subtract)\
                   .then_inc(ev("pq_lo"), 1)

            def edge_onehots(t):
                if t >= 2:
                    dve.wait_ge(ev("gathered"), t - 1)
                if t >= 4:
                    dve.wait_ge(ev("scattered"), t - 3)
                for j, row in enumerate((rowT[0], rowT[1])):
                    dve.tensor_scalar(oh[:, t % 2, j, :], row[:, t, :], iotap[:, 0:1], None, ALU.is_equal)
                dve.tensor_scalar(ohe[:, t % 4, :], iota[:, 0:P], idf[:, 0, t:t + 1], None, ALU.is_equal).then_inc(ev("oh_made"), 1)

            for j in range(2):
                dve.wait_ge(ev("rows"), 32)
            edge_onehots(0)
            edge_onehots(1)
            for t in range(ET):
                if t + 2 < ET:
                    edge_onehots(t + 2)
                dve.wait_ge(ev("r_hi"), t + 1)
                dve.tensor_tensor(el[:, 2 * (t % 2) + 1, :], tmp[:, t % 2, :], el[:, 2 * (t % 2), :].bitcast(F32), ALU.subtract)\
                   .then_inc(ev("r_lo"), 1)
                if t % 4 == 3:
                    split_to(L1M[3] + 1 + min(t // 4, AHEAD))
            dve.wait_ge(ev("scattered"), ET)
            dve.wait_ge(ev("r_lo"), ET)
            step(dve.tensor_reduce(sew[:, :], TP[:, 0, HALF:HALF + 2], mybir.AxisListType.X, ALU.add))
            for h in range(2):
                done(dve.tensor_copy(half(tmp[:, 0, :], h), AC[:, h, 0:HALF]), "ts_src")
            ts_lo(3)
            for j, name in enumerate(("msg_W2", "agg_W1", "agg_W2", "out_W")):
                for a in range(2):
                    split_to(L1D[name, a] + AHEAD)
                b = bias[:, BIAS_SLOT["L1_gnn_" + ("msg_b2", "agg_b1", "agg_b2", "out_b")[j]], :]
                if j < 2:
                    dve.wait_ge(ev("ld_L1_gnn_" + ("msg_b2", "agg_b1")[j]), 16)
                if j == 2:
                    b = Hs[:, 1, :]
                for h in range(2):
                    wait_half(dve, L1D[name, 1], h)
                    o = half(tmp[:, (j + 1) % 2, :], h)
                    if j == 0:
                        ins = dve.scalar_tensor_tensor(o, half(b, h), sew[:, 0:1], HP[:, h, 0:HALF], ALU.mult, ALU.add)
                    else:
                        ins = dve.tensor_tensor(o, HP[:, h, 0:HALF], half(b, h), ALU.add)
                    if j < 3:
                        done(ins, "ts_src")
                    else:
                        step(ins)
                        stats_half(h, tmp[:, 0, :])
                if j < 3:
                    ts_lo(4 + j, relu=j == 1)
            stats_end(1)
            y = tmp[:, 0, :]
            dve.wait_ge(ev("ld_L1_gnn_ln_g"), 16)
            step(dve.scalar_tensor_tensor(y, y, mv[:, 0:1], bias[:, BIAS_SLOT["L1_gnn_ln_g"], :], ALU.subtract, ALU.mult))
            for h in range(2):
                step(dve.scalar_tensor_tensor(half(X[:, :], h), half(y, h), mv[:, 3:4], half(bias[:, BIAS_SLOT["L1_gnn_ln_b"], :], h),
                                              ALU.mult, ALU.add))
                stats_half(h, X[:, :])
            norm_x(2)
            ts_lo(7)
            split_to(L1D["out_W", 1] + 1 + AHEAD)
            gat(G2, H2, L2W1, L2W2, "L2_gnn_b2", 7, 1)
            norm_x(3)
            ts_lo(8)
            add_bias("L3_gnn_b2", 8)
            for r in range(REL):
                for a in range(2):
                    split_to(L3W[1, r, a] + AHEAD)
            dve.wait_ge(ev("qk_dot"), REL)
            done(dve.tensor_copy(qkn[:, 0:8, :], AC[:, 0, 0:REL * 8].rearrange("p (r c) -> p c r", r=REL)), "qk_out")
            split_to(L3W[1, 2, 1] + AHEAD + 1)
            scores3(0)
            for v in range(H3):
                if v + 1 < H3:
                    scores3(v + 1)
                weights3(v)
            dve.wait_ge(ev("ld_L3_gnn_b1"), 16)
            for h in range(2):
                for v in (2 * h, 2 * h + 1):
                    dve.wait_ge(ev("summed3"), 2 * h + 2)
                    c = v % 2 * C3
                    step(dve.scalar_tensor_tensor(tmp[:, 0, v * C3:(v + 1) * C3], HP[:, h, c:c + C3], inv3[:, v:v + 1],
                                                  bias[:, BIAS_SLOT["L3_gnn_b1"], v * C3:(v + 1) * C3], ALU.mult, ALU.add))
                done(dve.tensor_scalar(half(tmp[:, 1, :], h), half(tmp[:, 0, :], h), 0.0, None, ALU.min), "zmin3")
            for h in range(2):
                dve.wait_ge(ev("elu_exp3"), h + 1)
                done(dve.scalar_tensor_tensor(half(tmp[:, 0, :], h), half(tmp[:, 1, :], h), -1.0, half(tmp[:, 0, :], h),
                                              ALU.add, ALU.max), "ts_src")
            ts_lo(9)
            dve.wait_ge(ev("qk2"), 32)
            for r in range(REL):
                for a in range(2):
                    split_to(L3W[2, r, a] + AHEAD)
                dve.wait_ge(ev("xr_out"), REL + r + 1)
                for j in range(2):
                    ins = dve.tensor_tensor_reduce(Hs[:, 1, :], G[:, r, :], G[:, 4 + j, :], 1.0, 0.0, ALU.mult, ALU.add,
                                                   qkn[:, 8 + j, r:r + 1])
                    if r == REL - 1 and j == 1:
                        done(ins, "qk_out")
                    else:
                        step(ins)
            scores3(H3)
            weights3(H3)
            residual(2, inv3[:, H3:H3 + 1])
            norm_x(4, last=True)

        @block.gpsimd
        def _(pool):
            at = [0]

            def split_to(n):
                while at[0] <= min(n, N - 1):
                    m = at[0]
                    pool.wait_ge(hi_ready, m + 1)
                    k, c = shape_of(m)
                    a = cut(m)
                    pool.tensor_tensor(wlo[:, m % SPLIT, a:k * c], raw[:, m % RAW, a:k * c],
                                       whi[:, m % SPLIT, a:k * c].bitcast(F32), ALU.subtract).then_inc(lo_pool, 1)
                    at[0] += 1

            def spread_vectors(g):
                if g == 0:
                    pool.wait_ge(ev("ld_rows"), 16 * 8)
                else:
                    pool.wait_ge(ev("dots"), g)
                    pool.wait_ge(lo_pool, at[0])
                q = 32 * (g // 2)
                for j in range(2):
                    ins = pool.partition_broadcast(arow(g)[j], G[q:q + 1, 2 + 2 * j + g % 2, :])
                ins.then_inc(ev("abc"), 1)
                pool.wait_ge(ev("abc"), g + 1)

            def diagonals(v):
                pool.wait_ge(ev("qk_out"), 1 if v < H3 else 2)
                if v >= 2:
                    pool.wait_ge(ev("spread3"), v - 1)
                k = H3 + v if v < H3 else 9
                pool.tensor_tensor(diag3(v).rearrange("p (r n) -> p r n", r=REL),
                                   ident[:, :].unsqueeze(1).broadcast_to((P, REL, P)),
                                   qkn[:, k, :].unsqueeze(2).broadcast_to((P, REL, P)), ALU.mult).then_inc(ev("diag3"), 1)

            def power(k):
                pool.wait_ge(ev("variance"), k + 1)
                pool.tensor_tensor(mv[:, 3:4], mv[:, 2:3], neghalf[:, :], ALU.pow).then_inc(ev("rstd"), 1)

            def gat(g0, heads, W1, W2):
                n = W1[0, 0]
                for i in range(heads + 2):
                    for k in range(2):
                        if i < heads:
                            n = W1[i, k]
                            split_to(n + AHEAD)
                    for k in range(2):
                        if i >= 2:
                            n = W2[i - 2, k]
                            split_to(n + AHEAD)
                    if g0 == G0 and i + 1 < heads:
                        spread_vectors(i + 1)

            pool.memset(ident[:, :], 0.0).then_inc(ev("pool_step"), 1)
            pool.memset(ones[:, :], 1.0).then_inc(ev("consts"), 1)
            pool.iota(iota[:, :], pattern=[[1, REL * P]], base=0, channel_multiplier=0).then_inc(ev("consts"), 1)
            pool.iota(iotap[:, :], pattern=[[0, 1]], base=0, channel_multiplier=1).then_inc(ev("consts"), 1)
            pool.memset(neghalf[:, :], -0.5).then_inc(ev("consts"), 1)
            pool.wait_ge(ev("pool_step"), 1)
            pool.affine_select(out=ident[:, :], in_=ident[:, :], compare_op=ALU.not_equal, fill=1.0, base=0,
                               pattern=[[-1, P]], channel_multiplier=1).then_inc(ev("consts"), 1)
            spread_vectors(0)
            gat(G0, H0, L0W1, L0W2)
            power(0)
            for t in range(TYPES):
                for a in range(2):
                    split_to(L1T[t, a] + AHEAD)
            split_to(L1M[3] + 1 + AHEAD)
            for name in ("msg_W2", "agg_W1", "agg_W2", "out_W"):
                for a in range(2):
                    split_to(L1D[name, a] + AHEAD)
            power(1)
            power(2)
            gat(G2, H2, L2W1, L2W2)
            power(3)
            split_to(L3W[1, 2, 1] + AHEAD)
            for v in range(H3):
                diagonals(v)
            split_to(N - 1)
            diagonals(H3)
            power(4)


INPUTS = ["x", "src", "dst", "edge_attr_32", "edge_type_3", "node_type_6",
          "L0_gnn_W1", "L0_gnn_a_src1", "L0_gnn_a_dst1", "L0_gnn_b1", "L0_gnn_W2", "L0_gnn_a_src2", "L0_gnn_a_dst2", "L0_gnn_b2",
          "L1_gnn_W_type", "L1_gnn_b_type", "L1_gnn_msg_W1", "L1_gnn_msg_b1", "L1_gnn_msg_W2", "L1_gnn_msg_b2",
          "L1_gnn_edge_W1", "L1_gnn_edge_b1", "L1_gnn_edge_W2", "L1_gnn_edge_b2", "L1_gnn_agg_W1", "L1_gnn_agg_b1",
          "L1_gnn_agg_W2", "L1_gnn_agg_b2", "L1_gnn_out_W", "L1_gnn_out_b", "L1_gnn_ln_g", "L1_gnn_ln_b",
          "L2_gnn_W1", "L2_gnn_a1_src", "L2_gnn_a1_dst", "L2_gnn_b1", "L2_gnn_W2", "L2_gnn_a2_src", "L2_gnn_a2_dst", "L2_gnn_b2",
          "L3_gnn_W1", "L3_gnn_q1", "L3_gnn_k1", "L3_gnn_b1", "L3_gnn_W2", "L3_gnn_q2", "L3_gnn_k2", "L3_gnn_b2"]


def kernel(**inputs):
    import numpy as np
    import concourse.bacc as bacc
    from concourse.bass_utils import run_bass_kernel_spmd

    nc = bacc.Bacc("TRN2", target_bir_lowering=False, num_devices=1)
    arrays, io = {}, {}
    for name in INPUTS:
        a = np.ascontiguousarray(inputs[name])
        arrays[name + "_dram"] = a
        io[name] = nc.dram_tensor(name + "_dram", a.shape, mybir.dt.from_np(a.dtype), kind="ExternalInput").ap()
    out = nc.dram_tensor("out_dram", (P, D), F32, kind="ExternalOutput").ap()
    build(nc, io, out)
    r = run_bass_kernel_spmd(nc, [arrays], core_ids=[0])
    return r.results[0]["out_dram"]
```

```python
from contextlib import ExitStack

import concourse.bass as bass
from concourse import mybir

F32 = mybir.dt.float32
F32R = mybir.dt.float32r
BF16 = mybir.dt.bfloat16
F16 = mybir.dt.float16
I32 = mybir.dt.int32
U32 = mybir.dt.uint32
ALU = mybir.AluOpType
ACT = mybir.ActivationFunctionType

P = 128
D = 768
KT = D // P
HALF = D // 2
E = 2048
ET = E // P
EA = 32
H4 = D // 4
TYPES = 6
REL = 3
H0 = 8
H2 = 4
C2 = 512
H3 = 4
C3 = D // H3
SLOPE = 0.2
EPS = 1e-5
TINY = 1e-16
BIG = 1e30
RAW = 4
SPLIT = 4
AHEAD = 3
CHUNK = 3 * D


def build(nc, io, out):
    ctx = ExitStack()
    with ctx:
        def sb(name, shape, dt=F32):
            return ctx.enter_context(nc.sbuf_tensor(name, shape, dt))

        def ps(name):
            return ctx.enter_context(nc.psum_tensor(name, [P, 2, 512], F32))

        def sem(name):
            return ctx.enter_context(nc.semaphore(name))

        chunks = []

        def tiles(w):
            return w.rearrange("(k p) n -> p k n", p=P)

        def add(view):
            chunks.append(view)
            return len(chunks) - 1

        w1, w2 = tiles(io["L0_gnn_W1"]), tiles(io["L0_gnn_W2"])
        L0W1, L0W2 = {}, {}
        for i in range(H0 + 2):
            if i < H0:
                for a in range(2):
                    L0W1[i, a] = add(w1[:, 3 * a:3 * a + 3, i * D:(i + 1) * D])
            if i >= 2:
                for a in range(2):
                    k = (i - 2) * KT + 3 * a
                    L0W2[i - 2, a] = add(w2[:, k:k + 3, :])
        L1T = {}
        for t in range(TYPES):
            wt = tiles(io["L1_gnn_W_type"][t])
            for a in range(2):
                L1T[t, a] = add(wt[:, 3 * a:3 * a + 3, :])
        L1M = [add(tiles(io["L1_gnn_msg_W1"])[:, 3 * a:3 * a + 3, :]) for a in range(4)]
        L1D = {}
        for name in ("msg_W2", "agg_W1", "agg_W2", "out_W"):
            for a in range(2):
                L1D[name, a] = add(tiles(io["L1_gnn_" + name])[:, 3 * a:3 * a + 3, :])
        w1, w2 = tiles(io["L2_gnn_W1"]), tiles(io["L2_gnn_W2"])
        L2W1, L2W2 = {}, {}
        for i in range(H2 + 2):
            if i < H2:
                for a in range(2):
                    L2W1[i, a] = add(w1[:, 3 * a:3 * a + 3, i * C2:(i + 1) * C2])
            if i >= 2:
                for a in range(2):
                    k = (i - 2) * (C2 // P) + 2 * a
                    L2W2[i - 2, a] = add(w2[:, k:k + 2, :])
        L3W = {}
        for layer in (1, 2):
            for r in range(REL):
                wr = tiles(io[f"L3_gnn_W{layer}"][r])
                for a in range(2):
                    L3W[layer, r, a] = add(wr[:, 3 * a:3 * a + 3, :])
        N = len(chunks)
        HALVES = [L0W2[H0 - 1, 1], L1T[TYPES - 1, 1], L1M[3]] + \
                 [L1D[name, 1] for name in ("msg_W2", "agg_W1", "agg_W2", "out_W")] + \
                 [L2W2[H2 - 1, 1], L3W[1, REL - 1, 1], L3W[2, REL - 1, 1]]

        def wait_half(engine, n, h):
            if h == 0:
                engine.wait_ge(ev("first_half"), HALVES.index(n) + 1)
            else:
                engine.wait_ge(used, n + 1)

        raw = sb("raw", [P, RAW, CHUNK])
        whi = sb("whi", [P, SPLIT, CHUNK], F32R)
        wlo = sb("wlo", [P, SPLIT, CHUNK], F32R)
        xT = sb("xT", [P, 2, D], F32R)
        el = sb("el", [P, 4, D], F32R)
        pq = sb("pq", [P, 4, D], F32R)
        oh = sb("oh", [P, 2, 2, P], F32R)
        ohe = sb("ohe", [P, 4, P], F32R)
        X = sb("X", [P, D])
        Hs = sb("Hs", [P, 2, D])
        tmp = sb("tmp", [P, 3, D])
        G = sb("G", [P, 6, D])
        bias = sb("bias", [P, 6, D])
        ident = sb("ident", [P, P])
        ones = sb("ones", [P, P])
        iota = sb("iota", [P, REL * P], I32)
        iotap = sb("iotap", [P, 1], I32)
        cnt3 = sb("cnt3", [P, REL, P])
        far3 = sb("far3", [P, REL, P])
        cnt = sb("cnt", [P, P])
        far = sb("far", [P, P])
        att = sb("att", [P, 4, P])
        biasT = sb("biasT", [P, 64])
        idx = sb("idx", [P, 3, ET], I32)
        nty = sb("nty", [P, 1], I32)
        idf = sb("idf", [P, 2, ET])
        typ = sb("typ", [P, TYPES], U32)
        tyo = sb("tyo", [TYPES, P])
        ew = sb("ew", [P, ET])
        ewhl = sb("ewhl", [P, ET, 2], F32R)
        sew = sb("sew", [P, 1])
        eb2 = sb("eb2", [P, 1])
        alph = sb("alph", [P, 4])
        red = sb("red", [P, 2])
        low3 = sb("low3", [P, 2])
        inv3 = sb("inv3", [P, H3 + 1])
        qk = sb("qk", [P, KT, 8])
        qkn = sb("qkn", [P, 10, REL])
        st = sb("st", [P, 2, 6])
        mv = sb("mv", [P, 4])
        neghalf = sb("neghalf", [P, 1])

        ohk = bias[:, 0:4, :].rearrange("p a b -> p (a b)").bitcast(BF16).rearrange("p (t n) -> p t n", t=ET)
        ohd = bias[:, 4:6, :].rearrange("p a b -> p (a b)")[:, 0:ET * P // 2].bitcast(BF16).rearrange("p (t n) -> p t n", t=ET)
        rows = G[:, :, :].rearrange("p a b -> p (a b)").bitcast(I32)
        rowT = [rows[:, j * E:(j + 1) * E].rearrange("p (m t) -> p t m", t=ET) for j in range(2)]
        row1 = [bias[0:1, 2:5, :].rearrange("p a b -> p (a b)")[:, 0:E].bitcast(I32),
                tmp[0:1, :, :].rearrange("p a b -> p (a b)")[:, 0:E].bitcast(I32)]
        ea = bias[:, 1, 0:ET * (EA + 1)].rearrange("p (t c) -> p t c", t=ET)
        eaT = bias[0:EA + 1, 2:5, :].rearrange("p a b -> p (a b)")[:, 0:E]
        ejunk = bias[:, 5, 0:H4]
        eW1 = bias[0:EA + 1, 5, D - 2 * H4:D - H4]
        eW2 = bias[:, 5, D - H4:D]
        bst = Hs[0:64, 1, P:2 * P]
        tyr = Hs[0:TYPES, 1, 0:P].bitcast(I32)
        bty = G[0:TYPES, 0, :]
        iota16 = Hs[:, 1, 2 * P:2 * P + REL * P // 2].bitcast(F16)
        junk = tmp[:, 2, :]
        diag, sc, wt, wtT = (att[:, j, :] for j in range(4))

        HP, AC, TP, SB = (ps(name) for name in ("HP", "AC", "TP", "SB"))

        def two(pair):
            return pair[:, :, 0:HALF]

        def hidden_bank(n):
            return (AC, TP)[n // 2 % 2][:, n % 2, :]

        def cols(buf):
            return buf.rearrange("p (h n) -> p h n", h=2)

        def half(buf, h):
            return buf[:, h * HALF:(h + 1) * HALF]

        raw_landed = [sem(f"raw_landed{i}") for i in range(RAW)]
        hi_ready = sem("hi_ready")
        lo_dve = sem("lo_dve")
        lo_pool = sem("lo_pool")
        used = sem("used")
        made = {}

        def ev(name):
            if name not in made:
                made[name] = sem(name)
            return made[name]

        RN = REL * P

        def by_parity(buf, v):
            return buf[:, v % 2 * RN:(v % 2 + 1) * RN]

        def diag3(v):
            return by_parity(tmp[:, 1, :], v)

        def score3(v):
            return by_parity(Hs[:, 1, :], v)

        def weight3(v):
            return by_parity(tmp[:, 2, :], v)

        def weight3_T(v):
            return by_parity(Hs[:, 0, :], v)

        def bank3(v, j):
            return (SB, AC)[v % 2][:, j, 0:RN]

        G0, G0F, G2, G2F = 0, H0, H0 + 1, H0 + 1 + H2
        NG = G2F + 1

        def width(g):
            return C2 if G2 <= g < G2F else D

        def inner(g):
            return g if g <= G0F else g - 1

        def arow(g):
            s = 0 if g < G0F else (2 if g % 2 == 0 else 4)
            return [G[:, s + j, 0:width(g)] for j in range(2)]

        def hbuf(g):
            return Hs[:, g % 2, 0:width(g)]

        def elbuf(g, j):
            return el[:, 2 * (g % 2) + j, 0:width(g)]

        def shape_of(n):
            _, k, c = chunks[n].shape
            return k, c

        def cut(n):
            k, c = shape_of(n)
            return k * c * 10 // 18 // 64 * 64

        def w_of(buf, n):
            k, c = shape_of(n)
            return buf[:, n % SPLIT, 0:k * c].rearrange("p (k c) -> p k c", k=k)

        block = ctx.enter_context(nc.Block())

        BIAS_SLOT = {"L0_gnn_b2": 0, "L1_gnn_msg_b1": 1, "L1_gnn_msg_b2": 2, "L1_gnn_agg_b1": 3,
                     "L1_gnn_agg_b2": 4, "L1_gnn_out_b": 5, "L1_gnn_ln_g": 2, "L1_gnn_ln_b": 0,
                     "L2_gnn_b2": 1, "L3_gnn_b2": 4, "L3_gnn_b1": 3}

        def bc(v):
            return v.partition_broadcast(P)

        @block.sync
        def _(sp):
            def chunk(n):
                if n >= RAW:
                    sp.wait_ge(lo_dve, n - RAW + 1)
                    sp.wait_ge(lo_pool, n - RAW + 1)
                k, c = shape_of(n)
                sp.dma_start(raw[:, n % RAW, 0:k * c].rearrange("p (k c) -> p k c", k=k), chunks[n])\
                  .then_inc(raw_landed[n % RAW], 16)

            def load_bias(name):
                sp.dma_start(bias[:, BIAS_SLOT[name], :], bc(io[name])).then_inc(ev("ld_" + name), 16)

            def load_arow(g, a, b):
                src, dst = arow(g)
                sp.dma_start(src, bc(a)).then_inc(ev(f"arow{g}"), 16)
                sp.dma_start(dst, bc(b)).then_inc(ev(f"arow{g}"), 16)

            sp.dma_start(X[:, :], io["x"]).then_inc(ev("ld_x"), 16)
            for n in range(N):
                chunk(n)
                if n == 0:
                    for j, name in enumerate(("L0_gnn_a_src1", "L0_gnn_a_dst1")):
                        for q in range(4):
                            sp.dma_start(G[32 * q:32 * q + 1, 2 + 2 * j:4 + 2 * j, :], io[name][2 * q:2 * q + 2, :])\
                               .then_inc(ev("ld_rows"), 16)
                if n == L0W1[1, 1]:
                    sp.dma_start(tyr, io["node_type_6"].partition_broadcast(TYPES)).then_inc(ev("ld_tyr"), 16)
                    sp.dma_start(eW1[0:EA, :], io["L1_gnn_edge_W1"]).then_inc(ev("ld_edge"), 16)
                    sp.dma_start(eW1[EA:EA + 1, :], io["L1_gnn_edge_b1"].rearrange("(a n) -> a n", a=1)).then_inc(ev("ld_edge"), 16)
                    sp.dma_start(eW2, bc(io["L1_gnn_edge_W2"].rearrange("n a -> (n a)"))).then_inc(ev("ld_edge"), 16)
                    sp.dma_start(eb2[:, :], bc(io["L1_gnn_edge_b2"])).then_inc(ev("ld_edge"), 16)
                    sp.dma_start(bst[0:H0 * KT, :], io["L0_gnn_b1"].rearrange("(a n) -> a n", n=P)).then_inc(ev("ld_edge"), 16)
                    sp.dma_start(bst[H0 * KT:64, :], io["L2_gnn_b1"].rearrange("(a n) -> a n", n=P)).then_inc(ev("ld_edge"), 16)
                    sp.dma_start(qk[:, :, 0:H3], tiles(io["L3_gnn_q1"])).then_inc(ev("ld_qk"), 16)
                    sp.dma_start(qk[:, :, H3:2 * H3], tiles(io["L3_gnn_k1"])).then_inc(ev("ld_qk"), 16)
                if n == L0W1[2, 1]:
                    sp.wait_ge(ev("counted"), 1)
                    sp.dma_start(ea[:, :, 0:EA], io["edge_attr_32"].rearrange("(p t) c -> p t c", t=ET)).then_inc(ev("ld_ea"), 16)
                    load_bias("L0_gnn_b2")
                if n == L0W2[7, 0]:
                    sp.wait_ge(ev("abc"), H0)
                    load_arow(G0F, io["L0_gnn_a_src2"][0], io["L0_gnn_a_dst2"][0])
                if n == L1T[0, 0]:
                    sp.wait_ge(ev("dots"), H0)
                    sp.dma_start(bty, io["L1_gnn_b_type"]).then_inc(ev("ld_bty"), 16)
                    load_bias("L1_gnn_msg_b1")
                if n == L1T[2, 0]:
                    sp.wait_ge(ev("edge_hidden"), ET // 2)
                    sp.wait_ge(ev("dots"), G0F + 1)
                    sp.dma_start(row1[0], io["src"].rearrange("(a n) -> a n", a=1)).then_inc(ev("row1"), 16)
                    sp.dma_start(row1[1], io["dst"].rearrange("(a n) -> a n", a=1)).then_inc(ev("row1"), 16)
                if n == L1M[3]:
                    sp.wait_ge(ev("rows"), 4)
                    for name in ("agg_b2", "msg_b2", "agg_b1", "out_b"):
                        load_bias("L1_gnn_" + name)
                    sp.wait_ge(ev("x_biased"), 1)
                    load_bias("L1_gnn_ln_b")
                if n == L1D["out_W", 0]:
                    sp.wait_ge(ev("ts_src"), 2 * 4)
                    load_bias("L1_gnn_ln_g")
                if n == L1D["agg_W1", 1]:
                    sp.wait_ge(ev("q_sum"), 2)
                    load_bias("L2_gnn_b2")
                    sp.wait_ge(ev("oh_made"), ET)
                    for g in (G2, G2 + 1):
                        load_arow(g, io["L2_gnn_a1_src"][g - G2], io["L2_gnn_a1_dst"][g - G2])
                if n == L2W2[1, 0]:
                    sp.wait_ge(ev("ts_src"), 2 * 4)
                    load_bias("L3_gnn_b2")
                if n == L2W1[2, 1]:
                    sp.wait_ge(ev("dots"), G2 + 1)
                    g = G2 + 2
                    load_arow(g, io["L2_gnn_a1_src"][g - G2], io["L2_gnn_a1_dst"][g - G2])
                if n == L2W1[3, 1]:
                    sp.wait_ge(ev("dots"), G2 + 2)
                    g = G2 + 3
                    load_arow(g, io["L2_gnn_a1_src"][g - G2], io["L2_gnn_a1_dst"][g - G2])
                if n == L2W2[2, 0]:
                    sp.wait_ge(ev("dots"), G2 + 3)
                    load_arow(G2F, io["L2_gnn_a2_src"][0], io["L2_gnn_a2_dst"][0])
                    load_bias("L3_gnn_b1")
            sp.wait_ge(ev("dots"), NG)
            sp.dma_start(G[:, 4, :], bc(io["L3_gnn_q2"].rearrange("d a -> (d a)"))).then_inc(ev("qk2"), 16)
            sp.dma_start(G[:, 5, :], bc(io["L3_gnn_k2"].rearrange("d a -> (d a)"))).then_inc(ev("qk2"), 16)
            sp.wait_ge(ev("normed"), 2)
            sp.dma_start(out, X[:, :]).then_inc(ev("stored"), 16)
            sp.wait_ge(ev("stored"), 16)

        @block.tensor
        def _(pe):
            def wait_chunk(n):
                pe.wait_ge(hi_ready, n + 1)
                pe.wait_ge(lo_dve, n + 1)
                pe.wait_ge(lo_pool, n + 1)

            def dense(outs, left, n, kts, start, stop, mid=None):
                wait_chunk(n)
                k, c = shape_of(n)
                hi, lo = w_of(whi, n), w_of(wlo, n)
                for i, (o, (a, b)) in enumerate(outs):
                    if i == 1 and n in HALVES:
                        last.then_inc(ev("first_half"), 1)
                    for j, kt in enumerate(kts):
                        if i == 1 and j == k - 1 and mid:
                            mid()
                        for m, (x, w) in enumerate(((left(0, kt), hi), (left(0, kt), lo), (left(1, kt), hi))):
                            last = pe.matmul(o, x, w[:, j, a:b], start=start and j == 0 and m == 0,
                                             stop=stop and j == k - 1 and m == 2)
                last.then_inc(used, 1)

            def keep_busy(n, bank):
                for _ in range(n):
                    pe.matmul(bank[:, 0:P], ones[:, :], ident[:, :], start=True, stop=True)

            def left_x(i, kt):
                return xT[:, i, kt * P:(kt + 1) * P]

            def halves(pair):
                return [(pair[:, h, 0:HALF], (h * HALF, (h + 1) * HALF)) for h in range(2)]

            def product(pair, ns, k=None, mid=None):
                for a, n in enumerate(ns):
                    if k is not None:
                        xt_ready(k, a)
                    dense(halves(pair), left_x, n, range(3 * a, 3 * a + 3), a == 0, a == 1,
                          mid if a == 1 else None)

            def transpose_half(k, src, h):
                if k == 0:
                    pe.wait_ge(ev("ld_x"), 16)
                else:
                    pe.wait_ge(ev("ts_src"), 2 * (k - 1) + h + 1)
                for j in range(3):
                    c = (3 * h + j) * P
                    last = pe.transpose(TP[:, h, j * P:(j + 1) * P], src[:, c:c + P], ident[:, :])
                last.then_inc(ev("ts_out"), 1)

            def transposes(k, src):
                for h in range(2):
                    transpose_half(k, src, h)

            def xt_ready(k, h):
                pe.wait_ge(ev("ts_hi"), 2 * k + h + 1)
                pe.wait_ge(ev("ts_lo"), 2 * k + h + 1)

            def w1(g, a, n):
                if a == 0 and g > 0:
                    pe.wait_ge(ev("h_out"), inner(g))
                if g in (G0, G2):
                    xt_ready(0 if g == G0 else 7, a)
                o = halves(HP) if width(g) == D else [(HP[:, 0, :], (0, C2))]
                dense(o, left_x, n, range(3 * a, 3 * a + 3), a == 0, a == 1)

            def spread(g):
                pe.wait_ge(ev("diag"), g + 1)
                pe.matmul(SB[:, 0, 0:P], ones[:, :], diag, start=True, stop=True).then_inc(ev("spread"), 1)

            def turn(g):
                pe.wait_ge(ev("weights"), g + 1)
                if g == 0:
                    pe.wait_ge(ev("biasT"), 1)
                pe.transpose(SB[:, 1, 0:P], wt, ident[:, :]).then_inc(ev("turned"), 1)

            def aggregate_T(g):
                pe.wait_ge(ev("turned_out"), g + 1)
                if inner(g) > 0:
                    pe.wait_ge(ev("z"), inner(g))
                for k in range(width(g) // P):
                    last = pe.matmul(TP[:, k // 3, (k % 3) * P:(k % 3 + 1) * P],
                                     hbuf(g)[:, k * P:(k + 1) * P], wtT, start=True, stop=True)
                last.then_inc(ev("summed"), 1)

            def w2(g, a, n, first, final):
                if a == 0 and g == 0:
                    pe.wait_ge(ev("ew_dot"), ET // 2)
                if a == 0:
                    pe.wait_ge(ev("el_hi"), inner(g) + 1)
                    pe.wait_ge(ev("el_lo"), inner(g) + 1)
                k, _ = shape_of(n)

                def left(i, kt):
                    return elbuf(g, i)[:, kt * P:(kt + 1) * P]
                dense(halves(AC), left, n, range(k * a, k * a + k), first and a == 0, final and a == 1)

            def gat(g0, heads, W1, W2):
                def late(i):
                    return i in (0, 1)

                for i in range(heads + 2):
                    g = g0 + i
                    if i == heads:
                        turn(g - 1)
                        w2(g - 2, 0, W2[i - 2, 0], False, False)
                        aggregate_T(g - 1)
                        w2(g - 2, 1, W2[i - 2, 1], False, False)
                        continue
                    if i < heads:
                        w1(g, 0, W1[i, 0])
                    if late(i - 1):
                        spread(g - 1)
                    elif 1 <= i <= heads:
                        turn(g - 1)
                    if i < heads:
                        w1(g, 1, W1[i, 1])
                    if late(i - 1):
                        if g == G2 + 2:
                            keep_busy(10, AC[:, 1, :])
                        turn(g - 1)
                        if g == G2 + 2:
                            keep_busy(5, AC[:, 1, :])
                    if g in (1, 2):
                        keep_busy(7, AC[:, 1, :])
                    if 1 <= i <= heads:
                        aggregate_T(g - 1)
                    if g == 0:
                        pe.wait_ge(ev("ld_edge"), 16 * 6)
                        pe.transpose(SB[:, 1, 0:64], bst, ident[0:64, 0:64]).then_inc(ev("bst"), 1)
                        count_edges()
                    if g == 2:
                        edge_hidden()
                        spread(g)
                        keep_busy(8, SB[:, 1, :])
                    if i == heads + 1:
                        keep_busy(8, HP[:, 0, :])
                    if i >= 2:
                        w2(g - 2, 0, W2[i - 2, 0], i == 2, i == heads + 1)
                    if g != 2 and i < heads and not late(i):
                        spread(g)
                    if i >= 2:
                        w2(g - 2, 1, W2[i - 2, 1], i == 2, i == heads + 1)
                g = g0 + heads
                keep_busy(14, HP[:, 0, :])
                spread(g)
                keep_busy(7, HP[:, 0, :])
                turn(g)
                pe.wait_ge(ev("turned_out"), g + 1)
                pe.wait_ge(ev("final_out"), 2 if g == G0F else 4)
                for h in range(2):
                    pe.matmul(HP[:, h, 0:HALF], wtT, half(hbuf(g), h), start=True, stop=True)\
                      .then_inc(ev("summed_h"), 1)
                keep_busy(15, AC[:, 0, :])

            def count_edges():
                pe.wait_ge(ev("onehots"), ET)
                for t in range(ET):
                    last = pe.matmul(AC[:, 0, 0:REL * P], ohd[:, t, :], ohk[:, t, :], start=t == 0, stop=t == ET - 1)
                last.then_inc(ev("counted"), 1)

            def edge_hidden():
                pe.wait_ge(ev("ea_ones"), 1)
                pe.wait_ge(ev("ld_ea"), 16)
                pe.wait_ge(ev("turned_out"), 2)
                pe.wait_ge(ev("scored"), 2)
                pe.wait_ge(ev("cnt_out"), 1)
                for q in range(2):
                    if q:
                        pe.wait_ge(ev("ea_out"), 1)
                    for j in range(8):
                        last = pe.transpose(SB[0:EA + 1, j // 4, (j % 4) * P:(j % 4 + 1) * P], ea[:, 8 * q + j, :], ident[:, :])
                    last.then_inc(ev("ea_T"), 1)
                keep_busy(6, AC[:, 0, :])
                pe.wait_ge(ev("z"), 2)
                for n in range(ET // 2):
                    if n == 4:
                        pe.wait_ge(ev("ea_out"), 2)
                    if n >= 4:
                        pe.wait_ge(ev("ew_dot"), n - 3)
                    for m in range(2):
                        last = pe.matmul(hidden_bank(n)[:, m * H4:(m + 1) * H4], eaT[:, (2 * n + m) * P:(2 * n + m + 1) * P],
                                         eW1, start=True, stop=True)
                    last.then_inc(ev("edge_hidden"), 1)

            def xr_T(r):
                pe.wait_ge(ev("xr_out"), r + 1)
                for k in range(KT):
                    last = pe.transpose(TP[:, k // 3, (k % 3) * P:(k % 3 + 1) * P], G[:, r, k * P:(k + 1) * P], ident[:, :])
                last.then_inc(ev("xrT"), 1)

            def xr_scores(r):
                pe.wait_ge(ev("xrT_out"), r + 1)
                for k in range(KT):
                    last = pe.matmul(AC[:, 0, r * 8:(r + 1) * 8], G[:, 3, k * P:(k + 1) * P], qk[:, k, :],
                                     start=k == 0, stop=k == KT - 1)
                last.then_inc(ev("qk_dot"), 1)

            def spread3(v):
                pe.wait_ge(ev("diag3"), v + 1)
                if v >= 2:
                    pe.wait_ge(ev("scored3"), v - 1)
                pe.matmul(bank3(v, 0), ones[:, :], diag3(v), start=True, stop=True).then_inc(ev("spread3"), 1)

            def turn3(v):
                pe.wait_ge(ev("weights3"), v + 1)
                for r in range(REL):
                    last = pe.transpose(bank3(v, 1)[:, r * P:(r + 1) * P], weight3(v)[:, r * P:(r + 1) * P], ident[:, :])
                last.then_inc(ev("turned3"), 1)

            def sum3(v):
                pe.wait_ge(ev("turned3_out"), v + 1)
                h, c = v // 2, (v % 2) * C3
                for r in range(REL):
                    last = pe.matmul(HP[:, h, c:c + C3], weight3_T(v)[:, r * P:(r + 1) * P],
                                     G[:, r, v * C3:(v + 1) * C3], start=r == 0, stop=r == REL - 1)
                last.then_inc(ev("summed3"), 1)

            pe.wait_ge(ev("consts"), 5)
            transposes(0, X)
            keep_busy(12, SB[:, 0, :])
            gat(G0, H0, L0W1, L0W2)
            transposes(1, X)
            keep_busy(4, AC[:, 0, :])
            for t in range(TYPES):
                if t >= 2:
                    pe.wait_ge(ev("chosen"), t - 1)
                if t == 2:
                    pe.wait_ge(ev("ld_bty"), 16)
                    pe.wait_ge(ev("tyo"), 1)
                    for h in range(2):
                        last = pe.matmul(AC[:, h, 0:HALF], tyo[:, :], half(bty, h), start=True, stop=True)
                    last.then_inc(ev("type_bias"), 1)
                product((HP, SB)[t % 2], [L1T[t, a] for a in range(2)], 1 if t == 0 else None,
                        (lambda: transpose_half(2, Hs[:, 1, :], 0)) if t == TYPES - 1 else None)
            pe.wait_ge(ev("chosen"), TYPES - 1)
            keep_busy(5, HP[:, 0, :])
            transpose_half(2, Hs[:, 1, :], 1)
            keep_busy(3, HP[:, 0, :])
            product(HP, L1M[0:2], 2)
            product(SB, L1M[2:4])
            keep_busy(15, AC[:, 0, :])
            def gather(t, slot, first=False):
                pe.wait_ge(ev("oh_made"), t + 1)
                if not first:
                    pe.wait_ge(ev("relu_out"), t - 1)
                for h in range(2):
                    if first:
                        pe.wait_ge(ev("pq_hi"), 2 + h)
                        pe.wait_ge(ev("pq_lo"), 2 + h)
                    for m in range(4):
                        last = pe.matmul((HP, SB)[slot % 2][:, h, 0:HALF], oh[:, slot % 2, m // 2, :],
                                         half(pq[:, m, :], h), start=m == 0, stop=m == 3)
                last.then_inc(ev("gathered"), 1)

            def scatter(s, slot, first=False, final=False):
                pe.wait_ge(ev("r_hi"), s + 1)
                pe.wait_ge(ev("r_lo"), s + 1)
                for h in range(2):
                    for m in range(2):
                        last = pe.matmul(AC[:, h, 0:HALF], ohe[:, slot % 4, :], half(el[:, 2 * (slot % 2) + m, :], h),
                                         start=first and m == 0, stop=final and m == 1)
                last = pe.matmul(TP[:, 0, HALF:HALF + 2], ohe[:, slot % 4, :], ewhl[:, s, :], start=first, stop=final)
                last.then_inc(ev("scattered"), 1)

            for t in range(4):
                gather(t, t, first=t < 2)
                if t >= 2:
                    scatter(t - 2, t - 2, first=t == 2)
            with pe.Fori(1, ET // 4) as turn4:
                for k in range(4):
                    gather(turn4 * 4 + k, k)
                    scatter(turn4 * 4 + (k - 2), (k + 2) % 4)
            for s in (ET - 2, ET - 1):
                scatter(s, s, final=s == ET - 1)
            for j, name in enumerate(("msg_W2", "agg_W1", "agg_W2", "out_W")):
                if j == 0:
                    keep_busy(3, SB[:, 0, :])
                    transpose_half(3, tmp[:, 0, :], 0)
                transpose_half(3 + j, tmp[:, j % 2, :], 1)
                product(HP, [L1D[name, a] for a in range(2)], 3 + j,
                        (lambda: transpose_half(4 + j, tmp[:, (j + 1) % 2, :], 0)) if j < 3 else None)
            keep_busy(28, SB[:, 0, :])
            transposes(7, X)
            gat(G2, H2, L2W1, L2W2)
            transposes(8, X)
            keep_busy(4, AC[:, 0, :])
            pe.wait_ge(ev("ld_qk"), 32)
            for r in range(REL):
                if r == 2:
                    pe.wait_ge(ev("xr_out"), 1)
                product((HP, SB)[r % 2], [L3W[1, r, a] for a in range(2)], 8 if r == 0 else None)
                if r >= 1:
                    if r == 2:
                        xr_scores(0)
                    xr_T(r - 1)
            xr_scores(1)
            keep_busy(4, SB[:, 0, :])
            xr_T(2)
            keep_busy(5, HP[:, 0, :])
            xr_scores(2)
            keep_busy(6, HP[:, 0, :])
            for v in range(3):
                spread3(v)
            keep_busy(5, TP[:, 0, :])
            turn3(0)
            spread3(3)
            for v in range(1, H3):
                turn3(v)
                sum3(v - 1)
            keep_busy(3, SB[:, 0, :])
            sum3(H3 - 1)
            keep_busy(8, SB[:, 0, :])
            transposes(9, tmp[:, 0, :])
            for r in range(REL):
                if r == 2:
                    pe.wait_ge(ev("xr_out"), REL + 1)
                product((HP, SB)[r % 2], [L3W[2, r, a] for a in range(2)], 9 if r == 0 else None)
            keep_busy(16, AC[:, 0, :])
            spread3(H3)
            keep_busy(14, AC[:, 0, :])
            turn3(H3)
            keep_busy(4, AC[:, 0, :])
            pe.wait_ge(ev("turned3_out"), H3 + 1)
            for h in range(2):
                for r in range(REL):
                    last = pe.matmul(HP[:, h, 0:HALF], weight3_T(H3)[:, r * P:(r + 1) * P],
                                     half(G[:, r, :], h), start=r == 0, stop=r == REL - 1)
                last.then_inc(ev("summed_h"), 1)

        @block.scalar
        def _(act):
            at = [0]

            def split_to(n):
                while at[0] <= min(n, N - 1):
                    m = at[0]
                    act.wait_ge(raw_landed[m % RAW], 16 * (m // RAW + 1))
                    if m >= SPLIT:
                        act.wait_ge(used, m - SPLIT + 1)
                    k, c = shape_of(m)
                    act.activation(whi[:, m % SPLIT, 0:k * c], raw[:, m % RAW, 0:k * c], ACT.Copy).then_inc(hi_ready, 1)
                    at[0] += 1

            def split_tile(j):
                m = at[0]
                k, c = shape_of(m)
                if j == 0:
                    act.wait_ge(raw_landed[m % RAW], 16 * (m // RAW + 1))
                    act.wait_ge(used, m - SPLIT + 1)
                ins = act.activation(whi[:, m % SPLIT, j * c:(j + 1) * c], raw[:, m % RAW, j * c:(j + 1) * c], ACT.Copy)
                if j == k - 1:
                    ins.then_inc(hi_ready, 1)
                    at[0] += 1

            def ts_hi(k, func=ACT.Copy):
                for h in range(2):
                    act.wait_ge(ev("ts_out"), 2 * k + h + 1)
                    act.activation(half(xT[:, 0, :], h), TP[:, h, 0:HALF], func).then_inc(ev("ts_hi"), 1)

            def expo(g):
                act.wait_ge(ev("lowest"), g + 1)
                act.activation(wt, sc, ACT.Exp, bias=red[:, 0:1], scale=-1.0).then_inc(ev("exped"), 1)

            def turned_out(g):
                act.wait_ge(ev("turned"), g + 1)
                act.activation(wtT, SB[:, 1, 0:P], ACT.Copy).then_inc(ev("turned_out"), 1)

            def h_out(g, n):
                if g not in (G0F, G2F):
                    act.wait_ge(used, n + 1)
                if g == 1:
                    act.wait_ge(ev("tyo"), 1)
                if inner(g) >= 2:
                    act.wait_ge(ev("summed"), inner(g) - 1)
                if g in (G0F, G2F):
                    for h in range(2):
                        wait_half(act, n, h)
                        act.activation(half(hbuf(g), h), AC[:, h, 0:HALF], ACT.Copy).then_inc(ev("final_out"), 1)
                    return
                o, i = (cols(hbuf(g)), two(HP)) if width(g) == D else (hbuf(g), HP[:, 0, :])
                act.activation(o, i, ACT.Copy).then_inc(ev("h_out"), 1)

            def elu_exp(g):
                act.wait_ge(ev("zmin"), inner(g) + 1)
                c = width(g)
                act.activation(tmp[:, 1, 0:c], tmp[:, 1, 0:c], ACT.Exp).then_inc(ev("elu_exp"), 1)

            def el_hi(g):
                act.wait_ge(ev("elu"), inner(g) + 1)
                act.activation(elbuf(g, 0), tmp[:, 0, 0:width(g)], ACT.Copy).then_inc(ev("el_hi"), 1)

            def gat(g0, heads, W1, W2):
                n = W1[0, 0]
                for i in range(heads + 2):
                    g = g0 + i
                    if i == heads:
                        turned_out(g - 1)
                        split_to(W2[i - 2, 0] + AHEAD)
                        elu_exp(g - 1)
                        el_hi(g - 1)
                        split_to(W2[i - 2, 1] + AHEAD)
                        continue
                    if i < heads:
                        n = W1[i, 0]
                        split_to(n + AHEAD)
                    if 1 <= i <= heads and i not in (1, 2):
                        turned_out(g - 1)
                    if i < 3:
                        h_out(g, W1[i, 1])
                    if i in (1, 2):
                        turned_out(g - 1)
                    if i < heads:
                        n = W1[i, 1]
                        split_to(n + AHEAD)
                    if 3 <= i < heads:
                        h_out(g, n)
                    if g == 0:
                        act.wait_ge(ev("bst"), 1)
                        act.activation(biasT[:, :], SB[:, 1, 0:64], ACT.Copy).then_inc(ev("biasT"), 1)
                    if g == 2:
                        edge_transposed()
                    if i >= 2:
                        n = W2[i - 2, 0]
                        split_to(n + AHEAD)
                    if 1 <= i <= heads:
                        elu_exp(g - 1)
                    if i < heads:
                        expo(g)
                    if i == heads - 1:
                        el_hi(g - 1)
                    if i >= 2:
                        n = W2[i - 2, 1]
                        split_to(n + AHEAD)
                    if 1 <= i < heads - 1:
                        el_hi(g - 1)
                    if g == 2:
                        edge_weights()
                g = g0 + heads
                h_out(g, n)
                expo(g)
                turned_out(g)
                split_to(n + 1 + AHEAD)

            def xrT_out(r):
                act.wait_ge(ev("xrT"), r + 1)
                if r:
                    act.wait_ge(ev("qk_dot"), r)
                act.activation(cols(G[:, 3, :]), two(TP), ACT.Copy).then_inc(ev("xrT_out"), 1)

            def exp3(v):
                act.wait_ge(ev("lowest3"), v + 1)
                if v >= 2:
                    act.wait_ge(ev("turned3"), v - 1)
                act.activation(weight3(v), score3(v), ACT.Exp, bias=low3[:, v % 2:v % 2 + 1], scale=-1.0).then_inc(ev("exped3"), 1)

            def turned3_out(v):
                act.wait_ge(ev("turned3"), v + 1)
                if v >= 2:
                    act.wait_ge(ev("summed3"), v - 1)
                act.activation(weight3_T(v), bank3(v, 1), ACT.Copy).then_inc(ev("turned3_out"), 1)

            for j, name in enumerate(("dst", "src", "edge_type_3")):
                act.dma_start(idx[:, j, :], io[name].rearrange("(p t) -> p t", t=ET)).then_inc(ev("ld_idx"), 16)
            act.dma_start(nty[:, :], io["node_type_6"].rearrange("(p a) -> p a", a=1)).then_inc(ev("ld_idx"), 16)
            def edge_transposed():
                for q in range(2):
                    act.wait_ge(ev("ea_T"), q + 1)
                    act.activation(eaT[:, q * 8 * P:(q + 1) * 8 * P].rearrange("p (a n) -> p a n", a=2), SB[0:EA + 1, :, :], ACT.Copy).then_inc(ev("ea_out"), 1)

            def edge_weights():
                act.wait_ge(ev("ew_dot"), ET // 2)
                act.wait_ge(ev("eb2_neg"), 1)
                act.activation(ew[:, :], ew[:, :], ACT.Exp, bias=eb2[:, 0:1], scale=-1.0).then_inc(ev("ew_exp"), 1)

            ts_hi(0)
            gat(G0, H0, L0W1, L0W2)
            ts_hi(1)
            for t in range(TYPES):
                for a in range(2 if t < TYPES - 1 else 1):
                    split_to(L1T[t, a] + AHEAD)
                if t == 0:
                    act.wait_ge(ev("ew_done"), 1)
                    act.activation(ewhl[:, :, 0], ew[:, :], ACT.Copy).then_inc(ev("ew_hi"), 1)
            ts_hi(2)
            for a in range(2):
                split_to(L1M[a] + AHEAD)
            act.wait_ge(used, L1M[1] + 1)
            act.activation(cols(pq[:, 0, :]), two(HP), ACT.Copy).then_inc(ev("pq_hi"), 1)
            for h in range(2):
                act.wait_ge(ev("q_sum"), h + 1)
                act.activation(half(pq[:, 2, :], h), half(tmp[:, 2, :], h), ACT.Copy).then_inc(ev("pq_hi"), 1)
            for t in range(ET):
                act.wait_ge(ev("gathered"), t + 1)
                if t >= 2:
                    act.wait_ge(ev("r_lo"), t - 1)
                act.activation(cols(tmp[:, t % 2, :]), two((HP, SB)[t % 2]), ACT.Relu, scale=ew[:, t:t + 1])\
                   .then_inc(ev("relu_out"), 1)
                act.wait_ge(ev("relu_out"), t + 1)
                if t >= 2:
                    act.wait_ge(ev("scattered"), t - 1)
                act.activation(el[:, 2 * (t % 2), :], tmp[:, t % 2, :], ACT.Copy).then_inc(ev("r_hi"), 1)
                if 1 <= t <= 3 * AHEAD:
                    split_tile((t - 1) % 3)
            for j, name in enumerate(("msg_W2", "agg_W1", "agg_W2", "out_W")):
                ts_hi(3 + j, ACT.Relu if j == 2 else ACT.Copy)
                for a in range(2):
                    split_to(L1D[name, a] + AHEAD)
            split_to(L1D["out_W", 1] + 1 + AHEAD)
            ts_hi(7)
            gat(G2, H2, L2W1, L2W2)
            ts_hi(8)
            for r in range(REL):
                for a in range(2):
                    split_to(L3W[1, r, a] + AHEAD)
                act.wait_ge(used, L3W[1, r, 1] + 1)
                if r == 0:
                    act.wait_ge(ev("dots"), NG)
                act.activation(cols(G[:, r, :]), two((HP, SB)[r % 2]), ACT.Copy).then_inc(ev("xr_out"), 1)
                if r >= 1:
                    xrT_out(r - 1)
            xrT_out(2)
            split_to(L3W[1, 2, 1] + AHEAD + 1)
            exp3(0)
            exp3(1)
            for v in range(H3):
                turned3_out(v)
                if v + 2 < H3:
                    exp3(v + 2)
            for h in range(2):
                act.wait_ge(ev("zmin3"), h + 1)
                act.activation(half(tmp[:, 1, :], h), half(tmp[:, 1, :], h), ACT.Exp).then_inc(ev("elu_exp3"), 1)
            ts_hi(9)
            for r in range(REL):
                for a in range(2):
                    split_to(L3W[2, r, a] + AHEAD)
                if r < REL - 1:
                    act.wait_ge(used, L3W[2, r, 1] + 1)
                    act.activation(cols(G[:, r, :]), two((HP, SB)[r % 2]), ACT.Copy).then_inc(ev("xr_out"), 1)
                    continue
                for h in range(2):
                    wait_half(act, L3W[2, r, 1], h)
                    act.activation(half(G[:, r, :], h), (HP, SB)[r % 2][:, h, 0:HALF], ACT.Copy).then_inc(ev("xr_out"), 1)
            exp3(H3)
            turned3_out(H3)

        @block.vector
        def _(dve):
            at = [0]
            count = {}

            def done(ins, name, by=1):
                count[name] = count.get(name, 0) + by
                ins.then_inc(ev(name), by)
                dve.wait_ge(ev(name), count[name])

            def step(ins):
                done(ins, "vector_step")

            def split_to(n):
                while at[0] <= min(n, N - 1):
                    m = at[0]
                    dve.wait_ge(hi_ready, m + 1)
                    c = cut(m)
                    dve.tensor_tensor(wlo[:, m % SPLIT, 0:c], raw[:, m % RAW, 0:c],
                                      whi[:, m % SPLIT, 0:c].bitcast(F32), ALU.subtract).then_inc(lo_dve, 1)
                    at[0] += 1

            def ts_lo(k, relu=False):
                for h in range(2):
                    dve.wait_ge(ev("ts_hi"), 2 * k + h + 1)
                    hi = half(xT[:, 0, :], h).bitcast(F32)
                    if relu:
                        ins = dve.scalar_tensor_tensor(half(xT[:, 1, :], h), TP[:, h, 0:HALF], 0.0, hi, ALU.max, ALU.subtract)
                    else:
                        ins = dve.tensor_tensor(half(xT[:, 1, :], h), TP[:, h, 0:HALF], hi, ALU.subtract)
                    ins.then_inc(ev("ts_lo"), 1)

            def dots(g):
                if g < G0F:
                    dve.wait_ge(ev("abc"), g + 1)
                else:
                    dve.wait_ge(ev(f"arow{g}"), 32)
                c = width(g)
                if g in (G0F, G2F):
                    for h in range(2):
                        dve.wait_ge(ev("final_out"), (2 if g == G2F else 0) + h + 1)
                        for j in range(2):
                            step(dve.tensor_tensor_reduce(half(junk, h), half(hbuf(g), h), half(arow(g)[j], h), 1.0, 0.0,
                                                          ALU.mult, ALU.add, alph[:, 2 * h + j:2 * h + j + 1]))
                    done(dve.tensor_tensor(alph[:, 0:2], alph[:, 0:2], alph[:, 2:4], ALU.add), "dots")
                    dve.wait_ge(ev("spread"), g)
                    dve.tensor_scalar(diag, ident[:, :], alph[:, 0:1], None, ALU.mult).then_inc(ev("diag"), 1)
                    return
                dve.wait_ge(ev("h_out"), inner(g) + 1)
                for j in range(2):
                    ins = dve.tensor_tensor_reduce(junk[:, 0:c], hbuf(g), arow(g)[j], 1.0, 0.0, ALU.mult, ALU.add,
                                                   alph[:, j:j + 1])
                    if j:
                        done(ins, "dots")
                    else:
                        step(ins)
                if g:
                    dve.wait_ge(ev("spread"), g)
                dve.tensor_scalar(diag, ident[:, :], alph[:, 0:1], None, ALU.mult).then_inc(ev("diag"), 1)

            def scores(g):
                dve.wait_ge(ev("spread"), g + 1)
                done(dve.tensor_scalar(sc, SB[:, 0, 0:P], -1.0, alph[:, 1:2], ALU.mult, ALU.subtract), "scored")
                step(dve.scalar_tensor_tensor(sc, sc, SLOPE, sc, ALU.mult, ALU.min))
                done(dve.tensor_tensor_reduce(sc, sc, far[:, :], 1.0, 3e38, ALU.add, ALU.min, red[:, 0:1]), "lowest")

            def weights(g):
                dve.wait_ge(ev("exped"), g + 1)
                total = dve.tensor_tensor_reduce(wt, wt, cnt[:, :], 1.0, 0.0, ALU.mult, ALU.add, red[:, 1:2])
                if g in (G0F, G2F):
                    done(total, "weights")
                else:
                    step(total)
                if g >= G2:
                    step(dve.tensor_scalar(red[:, 1:2], red[:, 1:2], TINY, None, ALU.add))
                step(dve.reciprocal(red[:, 1:2], red[:, 1:2]))
                if g not in (G0F, G2F):
                    done(dve.tensor_scalar(wt, wt, red[:, 1:2], None, ALU.mult), "weights")

            def elu_in(g):
                dve.wait_ge(ev("summed"), inner(g) + 1)
                if g == 0:
                    dve.wait_ge(ev("biasT"), 1)
                c = width(g)
                for b in range(2):
                    k0, k1 = 3 * b, min(3 * b + 3, c // P)
                    first = (g * KT if g < G0F else H0 * KT + (g - G2) * (C2 // P)) + k0
                    m = k1 - k0
                    ins = dve.tensor_tensor(tmp[:, 0, k0 * P:k1 * P].rearrange("p (k n) -> p k n", k=m),
                                            TP[:, b, 0:m * P].rearrange("p (k n) -> p k n", k=m),
                                            biasT[:, first:first + m].unsqueeze(2).broadcast_to((P, m, P)), ALU.add)
                    if b:
                        done(ins, "z")
                    else:
                        step(ins)
                done(dve.tensor_scalar(tmp[:, 1, 0:c], tmp[:, 0, 0:c], 0.0, None, ALU.min), "zmin")

            def elu_end(g):
                dve.wait_ge(ev("elu_exp"), inner(g) + 1)
                c = width(g)
                done(dve.scalar_tensor_tensor(tmp[:, 0, 0:c], tmp[:, 1, 0:c], -1.0, tmp[:, 0, 0:c], ALU.add, ALU.max), "elu")

            def el_low(g):
                c = width(g)
                dve.wait_ge(ev("el_hi"), inner(g) + 1)
                done(dve.tensor_tensor(elbuf(g, 1), tmp[:, 0, 0:c], elbuf(g, 0).bitcast(F32), ALU.subtract), "el_lo")

            def stats_half(h, src):
                dve.bn_stats(st[:, h, :], half(src, h)).then_inc(ev("vector_step"), 1)
                count["vector_step"] += 1

            def stats_end(k):
                dve.wait_ge(ev("vector_step"), count["vector_step"])
                step(dve.bn_aggr(mv[:, 0:2], st[:, :, :].rearrange("p a b -> p (a b)")))
                done(dve.tensor_scalar(mv[:, 2:3], mv[:, 1:2], EPS, None, ALU.add), "variance")
                dve.wait_ge(ev("rstd"), k + 1)

            def norm_x(k, last=False):
                stats_end(k)
                for h in range(2):
                    ins = dve.tensor_scalar(half(X[:, :], h), half(X[:, :], h), mv[:, 0:1], mv[:, 3:4], ALU.subtract, ALU.mult)
                    if last:
                        done(ins, "normed")
                    else:
                        done(ins, "ts_src")

            def gat(g0, heads, W1, W2, b2, ts, f):
                n = W1[0, 0]
                for i in range(heads + 2):
                    g = g0 + i
                    if i == heads:
                        split_to(W2[i - 2, 0] + AHEAD)
                        elu_in(g - 1)
                        elu_end(g - 1)
                        el_low(g - 1)
                        split_to(W2[i - 2, 1] + AHEAD)
                        continue
                    early = i < 3
                    if early:
                        split_to(W1[i, 0] + AHEAD)
                        dots(g)
                    if i < heads:
                        n = W1[i, 1]
                        split_to(n + AHEAD)
                    if g == 0:
                        edge_counts()
                    if i < heads and not early:
                        dots(g)
                    if 1 <= i <= heads:
                        elu_in(g - 1)
                    if g == 2:
                        edge_logits()
                    if i < heads:
                        scores(g)
                    if 2 <= i != heads - 1:
                        n = W2[i - 2, 0]
                        split_to(n + AHEAD)
                    if 1 <= i <= heads:
                        elu_end(g - 1)
                    if i < heads:
                        weights(g)
                    if i == heads - 1:
                        el_low(g - 1)
                    if 2 <= i <= heads:
                        n = W2[i - 2, 1]
                        split_to(n + AHEAD)
                    if 1 <= i < heads - 1:
                        el_low(g - 1)
                    if g == 2:
                        edge_weights()
                    if i == 2:
                        add_bias(b2, ts)
                g = g0 + heads
                dots(g)
                scores(g)
                weights(g)
                split_to(W2[heads - 1, 1] + AHEAD)
                residual(f, red[:, 1:2])

            def add_bias(name, ts):
                dve.wait_ge(ev("ld_" + name), 16)
                dve.wait_ge(ev("ts_out"), 2 * ts + 2)
                done(dve.tensor_tensor(X[:, :], X[:, :], bias[:, BIAS_SLOT[name], :], ALU.add), "x_biased")

            def residual(f, inv):
                for h in range(2):
                    dve.wait_ge(ev("summed_h"), 2 * f + h + 1)
                    step(dve.scalar_tensor_tensor(half(X[:, :], h), HP[:, h, 0:HALF], inv, half(X[:, :], h), ALU.mult, ALU.add))
                    stats_half(h, X[:, :])

            def edge_counts():
                dve.wait_ge(ev("counted"), 1)
                dve.memset(ea[:, :, EA], 1.0).then_inc(ev("ea_ones"), 1)
                done(dve.tensor_copy(cnt3[:, :, :].rearrange("p r n -> p (r n)"), AC[:, 0, 0:REL * P]), "cnt_out")
                step(dve.tensor_scalar(far3[:, :, :], cnt3[:, :, :], 0.5, BIG, ALU.is_lt, ALU.mult))
                step(dve.tensor_tensor(cnt[:, :], ident[:, :], cnt3[:, 0, :], ALU.add))
                for r in range(1, REL):
                    step(dve.tensor_tensor(cnt[:, :], cnt[:, :], cnt3[:, r, :], ALU.add))
                step(dve.tensor_scalar(far[:, :], cnt[:, :], 0.5, BIG, ALU.is_lt, ALU.mult))

            def edge_logits():
                for n in range(ET // 2):
                    dve.wait_ge(ev("edge_hidden"), n + 1)
                    for m in range(2):
                        ins = dve.scalar_tensor_tensor(ejunk, hidden_bank(n)[:, m * H4:(m + 1) * H4], 0.0, eW2,
                                                       ALU.max, ALU.mult, accum_out=ew[:, 2 * n + m:2 * n + m + 1])
                        if m:
                            done(ins, "ew_dot")
                        else:
                            step(ins)

            def edge_weights():
                dve.wait_ge(ev("ew_exp"), 1)
                step(dve.tensor_scalar(ew[:, :], ew[:, :], 1.0, None, ALU.add))
                done(dve.reciprocal(ew[:, :], ew[:, :]), "ew_done")

            def by_rel(buf):
                return buf.rearrange("p (r n) -> p r n", r=REL)

            def scores3(v):
                dve.wait_ge(ev("spread3"), v + 1)
                s, q = score3(v), v if v < H3 else 8
                done(dve.scalar_tensor_tensor(by_rel(s), by_rel(bank3(v, 0)), -1.0,
                                              qkn[:, q, :].unsqueeze(2).broadcast_to((P, REL, P)), ALU.mult, ALU.subtract), "scored3")
                step(dve.scalar_tensor_tensor(s, s, SLOPE, s, ALU.mult, ALU.min))
                done(dve.tensor_tensor_reduce(s, s, far3[:, :, :].rearrange("p r n -> p (r n)"), 1.0, 3e38, ALU.add, ALU.min,
                                              low3[:, v % 2:v % 2 + 1]), "lowest3")

            def weights3(v):
                dve.wait_ge(ev("exped3"), v + 1)
                w, total = weight3(v), inv3[:, v:v + 1]
                done(dve.tensor_tensor_reduce(w, w, cnt3[:, :, :].rearrange("p r n -> p (r n)"), 1.0, 0.0, ALU.mult, ALU.add,
                                              total), "weights3")

            def inverses(v0, v1):
                total = inv3[:, v0:v1]
                step(dve.tensor_scalar(total, total, TINY, None, ALU.add))
                step(dve.reciprocal(total, total))

            dve.wait_ge(ev("consts"), 5)
            dve.wait_ge(ev("ld_idx"), 16 * 4)
            step(dve.tensor_copy(idf[:, 0, :], idx[:, 0, :]))
            step(dve.scalar_tensor_tensor(idf[:, 1, :], idx[:, 2, :], float(P), idx[:, 1, :], ALU.mult, ALU.add))

            step(dve.tensor_copy(iota16, iota[:, :]))

            def onehots(t0, t1):
                for t in range(t0, t1):
                    dve.tensor_scalar(ohd[:, t, :], iota16[:, 0:P], idf[:, 0, t:t + 1], None, ALU.is_equal)
                    dve.tensor_scalar(ohk[:, t, :], iota16, idf[:, 1, t:t + 1], None, ALU.is_equal).then_inc(ev("onehots"), 1)

            ts_lo(0)
            split_to(0)
            onehots(0, ET // 4)
            split_to(1)
            onehots(ET // 4, ET)
            step(dve.tensor_scalar(typ[:, :], iota[:, 0:TYPES], nty[:, 0:1], None, ALU.is_equal))
            dve.wait_ge(ev("ld_tyr"), 16)
            done(dve.tensor_scalar(tyo[:, :], tyr, iotap[0:TYPES, 0:1], None, ALU.is_equal), "tyo")
            dve.wait_ge(ev("ld_edge"), 16 * 6)
            done(dve.tensor_scalar(eb2[:, :], eb2[:, :], -1.0, None, ALU.mult), "eb2_neg")
            gat(G0, H0, L0W1, L0W2, "L0_gnn_b2", 0, 0)
            norm_x(0)
            ts_lo(1)
            for t in range(TYPES):
                for a in range(2 if t < TYPES - 1 else 1):
                    split_to(L1T[t, a] + AHEAD)
                if t == 1:
                    dve.wait_ge(ev("ew_hi"), 1)
                    step(dve.tensor_tensor(ewhl[:, :, 1], ew[:, :], ewhl[:, :, 0].bitcast(F32), ALU.subtract))
                if t < TYPES - 1:
                    dve.wait_ge(used, L1T[t, 1] + 1)
                    done(dve.copy_predicated(cols(Hs[:, 1, :]), typ[:, t:t + 1].unsqueeze(2).broadcast_to((P, 2, HALF)),
                                             two((HP, SB)[t % 2])), "chosen")
            dve.wait_ge(ev("type_bias"), 1)
            for h in range(2):
                wait_half(dve, L1T[t, 1], h)
                done(dve.copy_predicated(half(Hs[:, 1, :], h), typ[:, t:t + 1].broadcast_to((P, HALF)),
                                         (HP, SB)[t % 2][:, h, 0:HALF]), "chosen_last")
                done(dve.tensor_tensor(half(Hs[:, 1, :], h), half(Hs[:, 1, :], h), AC[:, h, 0:HALF], ALU.add), "ts_src")
            ts_lo(2)
            split_to(L1T[TYPES - 1, 1] + AHEAD)
            for a in range(2):
                split_to(L1M[a] + AHEAD)
            dve.wait_ge(ev("pq_hi"), 1)
            dve.tensor_tensor(cols(pq[:, 1, :]), two(HP), cols(pq[:, 0, :].bitcast(F32)), ALU.subtract).then_inc(ev("pq_lo"), 1)
            dve.wait_ge(ev("ld_L1_gnn_msg_b1"), 16)
            dve.wait_ge(ev("rows"), 4)
            for h in range(2):
                wait_half(dve, L1M[3], h)
                done(dve.tensor_tensor(half(tmp[:, 2, :], h), SB[:, h, 0:HALF], half(bias[:, BIAS_SLOT["L1_gnn_msg_b1"], :], h),
                                       ALU.add), "q_sum")
            for h in range(2):
                dve.wait_ge(ev("pq_hi"), 2 + h)
                dve.tensor_tensor(half(pq[:, 3, :], h), half(tmp[:, 2, :], h), half(pq[:, 2, :], h).bitcast(F32), ALU.subtract)\
                   .then_inc(ev("pq_lo"), 1)

            def edge_onehots(t):
                if t >= 2:
                    dve.wait_ge(ev("gathered"), t - 1)
                if t >= 4:
                    dve.wait_ge(ev("scattered"), t - 3)
                for j, row in enumerate((rowT[0], rowT[1])):
                    dve.tensor_scalar(oh[:, t % 2, j, :], row[:, t, :], iotap[:, 0:1], None, ALU.is_equal)
                dve.tensor_scalar(ohe[:, t % 4, :], iota[:, 0:P], idf[:, 0, t:t + 1], None, ALU.is_equal).then_inc(ev("oh_made"), 1)

            edge_onehots(0)
            edge_onehots(1)
            for t in range(ET):
                if t + 2 < ET:
                    edge_onehots(t + 2)
                dve.wait_ge(ev("r_hi"), t + 1)
                dve.tensor_tensor(el[:, 2 * (t % 2) + 1, :], tmp[:, t % 2, :], el[:, 2 * (t % 2), :].bitcast(F32), ALU.subtract)\
                   .then_inc(ev("r_lo"), 1)
                if t % 3 == 1 and 1 < t <= 3 * AHEAD + 1:
                    split_to(L1M[3] + 1 + t // 3)
            dve.wait_ge(ev("scattered"), ET)
            dve.wait_ge(ev("r_lo"), ET)
            step(dve.tensor_reduce(sew[:, :], TP[:, 0, HALF:HALF + 2], mybir.AxisListType.X, ALU.add))
            for h in range(2):
                done(dve.tensor_copy(half(tmp[:, 0, :], h), AC[:, h, 0:HALF]), "ts_src")
            ts_lo(3)
            for b, name, y in ((Hs[:, 1, :], "agg_b2", bias[:, BIAS_SLOT["L1_gnn_agg_b2"], :]),
                               (bias[:, BIAS_SLOT["L1_gnn_out_b"], :], "out_b", X[:, :]),
                               (bias[:, BIAS_SLOT["L1_gnn_ln_b"], :], "ln_b", X[:, :])):
                dve.wait_ge(ev("ld_L1_gnn_" + name), 16)
                step(dve.tensor_tensor(b, b, y, ALU.add))
            for j, name in enumerate(("msg_W2", "agg_W1", "agg_W2", "out_W")):
                split_to(L1D[name, 0] + AHEAD)
                b = bias[:, BIAS_SLOT["L1_gnn_" + ("msg_b2", "agg_b1", "agg_b2", "out_b")[j]], :]
                if j < 2:
                    dve.wait_ge(ev("ld_L1_gnn_" + ("msg_b2", "agg_b1")[j]), 16)
                if j == 2:
                    b = Hs[:, 1, :]
                for h in range(2):
                    wait_half(dve, L1D[name, 1], h)
                    o = half(tmp[:, (j + 1) % 2, :], h)
                    if j == 0:
                        ins = dve.scalar_tensor_tensor(o, half(b, h), sew[:, 0:1], HP[:, h, 0:HALF], ALU.mult, ALU.add)
                    else:
                        ins = dve.tensor_tensor(o, HP[:, h, 0:HALF], half(b, h), ALU.add)
                    if j < 3:
                        done(ins, "ts_src")
                    else:
                        step(ins)
                        stats_half(h, tmp[:, 0, :])
                if j < 3:
                    ts_lo(4 + j, relu=j == 1)
                    split_to(L1D[name, 1] + AHEAD)
            stats_end(1)
            y = tmp[:, 0, :]
            dve.wait_ge(ev("ld_L1_gnn_ln_g"), 16)
            step(dve.scalar_tensor_tensor(y, y, mv[:, 0:1], bias[:, BIAS_SLOT["L1_gnn_ln_g"], :], ALU.subtract, ALU.mult))
            for h in range(2):
                step(dve.scalar_tensor_tensor(half(X[:, :], h), half(y, h), mv[:, 3:4], half(bias[:, BIAS_SLOT["L1_gnn_ln_b"], :], h),
                                              ALU.mult, ALU.add))
                stats_half(h, X[:, :])
            norm_x(2)
            ts_lo(7)
            split_to(L1D["out_W", 1] + 1 + AHEAD)
            gat(G2, H2, L2W1, L2W2, "L2_gnn_b2", 7, 1)
            norm_x(3)
            ts_lo(8)
            add_bias("L3_gnn_b2", 8)
            for r in range(REL):
                for a in range(2):
                    split_to(L3W[1, r, a] + AHEAD)
            dve.wait_ge(ev("qk_dot"), REL)
            done(dve.tensor_copy(qkn[:, 0:8, :], AC[:, 0, 0:REL * 8].rearrange("p (r c) -> p c r", r=REL)), "qk_out")
            split_to(L3W[1, 2, 1] + AHEAD + 1)
            scores3(0)
            for v in range(H3):
                if v + 1 < H3:
                    scores3(v + 1)
                weights3(v)
            inverses(0, H3)
            dve.wait_ge(ev("ld_L3_gnn_b1"), 16)
            for h in range(2):
                for v in (2 * h, 2 * h + 1):
                    dve.wait_ge(ev("summed3"), 2 * h + 2)
                    c = v % 2 * C3
                    step(dve.scalar_tensor_tensor(tmp[:, 0, v * C3:(v + 1) * C3], HP[:, h, c:c + C3], inv3[:, v:v + 1],
                                                  bias[:, BIAS_SLOT["L3_gnn_b1"], v * C3:(v + 1) * C3], ALU.mult, ALU.add))
                done(dve.tensor_scalar(half(tmp[:, 1, :], h), half(tmp[:, 0, :], h), 0.0, None, ALU.min), "zmin3")
            for h in range(2):
                dve.wait_ge(ev("elu_exp3"), h + 1)
                done(dve.scalar_tensor_tensor(half(tmp[:, 0, :], h), half(tmp[:, 1, :], h), -1.0, half(tmp[:, 0, :], h),
                                              ALU.add, ALU.max), "ts_src")
            ts_lo(9)
            dve.wait_ge(ev("qk2"), 32)
            for r in range(REL):
                for a in range(2):
                    split_to(L3W[2, r, a] + AHEAD)
                if r < REL - 1:
                    dve.wait_ge(ev("xr_out"), REL + r + 1)
                    for j in range(2):
                        step(dve.tensor_tensor_reduce(Hs[:, 1, :], G[:, r, :], G[:, 4 + j, :], 1.0, 0.0, ALU.mult, ALU.add,
                                                      qkn[:, 8 + j, r:r + 1]))
                    continue
                for h in range(2):
                    dve.wait_ge(ev("xr_out"), REL + r + 1 + h)
                    for j in range(2):
                        step(dve.tensor_tensor_reduce(half(Hs[:, 1, :], h), half(G[:, r, :], h), half(G[:, 4 + j, :], h), 1.0, 0.0,
                                                      ALU.mult, ALU.add, alph[:, 2 * h + j:2 * h + j + 1]))
                done(dve.tensor_tensor(qkn[:, 8:10, r], alph[:, 0:2], alph[:, 2:4], ALU.add), "qk_out")
            scores3(H3)
            weights3(H3)
            inverses(H3, H3 + 1)
            residual(2, inv3[:, H3:H3 + 1])
            norm_x(4, last=True)

        @block.gpsimd
        def _(pool):
            at = [0]

            def split_to(n):
                while at[0] <= min(n, N - 1):
                    m = at[0]
                    pool.wait_ge(hi_ready, m + 1)
                    k, c = shape_of(m)
                    a = cut(m)
                    pool.tensor_tensor(wlo[:, m % SPLIT, a:k * c], raw[:, m % RAW, a:k * c],
                                       whi[:, m % SPLIT, a:k * c].bitcast(F32), ALU.subtract).then_inc(lo_pool, 1)
                    at[0] += 1

            def spread_vectors(g):
                if g == 0:
                    pool.wait_ge(ev("ld_rows"), 16 * 8)
                else:
                    pool.wait_ge(ev("dots"), g)
                    pool.wait_ge(lo_pool, at[0])
                q = 32 * (g // 2)
                for j in range(2):
                    ins = pool.partition_broadcast(arow(g)[j], G[q:q + 1, 2 + 2 * j + g % 2, :])
                ins.then_inc(ev("abc"), 1)
                pool.wait_ge(ev("abc"), g + 1)

            def spread_row(j, c):
                pool.wait_ge(ev("row1"), 32)
                pool.wait_ge(ev("dots"), G0F + 1)
                pool.wait_ge(ev("type_bias"), 1)
                pool.wait_ge(lo_pool, at[0])
                c0, c1 = c * E // 2, (c + 1) * E // 2
                pool.partition_broadcast(rows[:, j * E + c0:j * E + c1].bitcast(F32), row1[j][:, c0:c1].bitcast(F32))\
                    .then_inc(ev("rows"), 1)
                pool.wait_ge(ev("rows"), 2 * j + c + 1)

            def diagonals(v):
                pool.wait_ge(ev("qk_out"), 1 if v < H3 else 2)
                if v >= 2:
                    pool.wait_ge(ev("spread3"), v - 1)
                k = H3 + v if v < H3 else 9
                pool.tensor_tensor(diag3(v).rearrange("p (r n) -> p r n", r=REL),
                                   ident[:, :].unsqueeze(1).broadcast_to((P, REL, P)),
                                   qkn[:, k, :].unsqueeze(2).broadcast_to((P, REL, P)), ALU.mult).then_inc(ev("diag3"), 1)

            def power(k):
                pool.wait_ge(ev("variance"), k + 1)
                pool.tensor_tensor(mv[:, 3:4], mv[:, 2:3], neghalf[:, :], ALU.pow).then_inc(ev("rstd"), 1)

            def gat(g0, heads, W1, W2):
                n = W1[0, 0]
                for i in range(heads + 2):
                    for k in range(2):
                        if i < heads:
                            n = W1[i, k]
                            split_to(n + AHEAD)
                    for k in range(2):
                        if i >= 2:
                            n = W2[i - 2, k]
                            split_to(n + AHEAD)
                    if g0 == G0 and i + 1 < heads:
                        spread_vectors(i + 1)

            pool.memset(ident[:, :], 0.0).then_inc(ev("pool_step"), 1)
            pool.memset(ones[:, :], 1.0).then_inc(ev("consts"), 1)
            pool.iota(iota[:, :], pattern=[[1, REL * P]], base=0, channel_multiplier=0).then_inc(ev("consts"), 1)
            pool.iota(iotap[:, :], pattern=[[0, 1]], base=0, channel_multiplier=1).then_inc(ev("consts"), 1)
            pool.memset(neghalf[:, :], -0.5).then_inc(ev("consts"), 1)
            pool.wait_ge(ev("pool_step"), 1)
            pool.affine_select(out=ident[:, :], in_=ident[:, :], compare_op=ALU.not_equal, fill=1.0, base=0,
                               pattern=[[-1, P]], channel_multiplier=1).then_inc(ev("consts"), 1)
            split_to(0)
            spread_vectors(0)
            gat(G0, H0, L0W1, L0W2)
            power(0)
            for t in range(TYPES):
                for a in range(2):
                    split_to(L1T[t, a] + AHEAD)
                    if t in (2, 3):
                        spread_row(t - 2, a)
            split_to(L1M[3] + 1 + AHEAD)
            for name in ("msg_W2", "agg_W1", "agg_W2", "out_W"):
                for a in range(2):
                    split_to(L1D[name, a] + AHEAD)
            power(1)
            power(2)
            gat(G2, H2, L2W1, L2W2)
            power(3)
            split_to(L3W[1, 2, 1] + AHEAD)
            for v in range(H3):
                diagonals(v)
            split_to(N - 1)
            diagonals(H3)
            power(4)


INPUTS = ["x", "src", "dst", "edge_attr_32", "edge_type_3", "node_type_6",
          "L0_gnn_W1", "L0_gnn_a_src1", "L0_gnn_a_dst1", "L0_gnn_b1", "L0_gnn_W2", "L0_gnn_a_src2", "L0_gnn_a_dst2", "L0_gnn_b2",
          "L1_gnn_W_type", "L1_gnn_b_type", "L1_gnn_msg_W1", "L1_gnn_msg_b1", "L1_gnn_msg_W2", "L1_gnn_msg_b2",
          "L1_gnn_edge_W1", "L1_gnn_edge_b1", "L1_gnn_edge_W2", "L1_gnn_edge_b2", "L1_gnn_agg_W1", "L1_gnn_agg_b1",
          "L1_gnn_agg_W2", "L1_gnn_agg_b2", "L1_gnn_out_W", "L1_gnn_out_b", "L1_gnn_ln_g", "L1_gnn_ln_b",
          "L2_gnn_W1", "L2_gnn_a1_src", "L2_gnn_a1_dst", "L2_gnn_b1", "L2_gnn_W2", "L2_gnn_a2_src", "L2_gnn_a2_dst", "L2_gnn_b2",
          "L3_gnn_W1", "L3_gnn_q1", "L3_gnn_k1", "L3_gnn_b1", "L3_gnn_W2", "L3_gnn_q2", "L3_gnn_k2", "L3_gnn_b2"]


def kernel(**inputs):
    import numpy as np
    import concourse.bacc as bacc
    from concourse.bass_utils import run_bass_kernel_spmd

    nc = bacc.Bacc("TRN2", target_bir_lowering=False, num_devices=1)
    arrays, io = {}, {}
    for name in INPUTS:
        a = np.ascontiguousarray(inputs[name])
        arrays[name + "_dram"] = a
        io[name] = nc.dram_tensor(name + "_dram", a.shape, mybir.dt.from_np(a.dtype), kind="ExternalInput").ap()
    out = nc.dram_tensor("out_dram", (P, D), F32, kind="ExternalOutput").ap()
    build(nc, io, out)
    r = run_bass_kernel_spmd(nc, [arrays], core_ids=[0])
    return r.results[0]["out_dram"]
```
